# Optimizing a Trainium2 kernel written in Bass

```python
import numpy as np
import jax
import jax.numpy as jnp

def _softmax(x, axis=-1):
    return jax.nn.softmax(x, axis=axis)

def _gelu(x):
    return jax.nn.gelu(x, approximate=True)

def _silu(x):
    return jax.nn.silu(x)

def _sigmoid(x):
    return jax.nn.sigmoid(x)

def _layernorm(x, axis=-1, eps=1e-05):
    m = jnp.mean(x, axis=axis, keepdims=True)
    v = jnp.var(x, axis=axis, keepdims=True)
    return (x - m) / jnp.sqrt(v + eps)

def _scatter_add(tgt, idx, src, axis=0):
    return tgt.at[idx].add(src)

def _segment_sum(src, seg, n):
    return jax.ops.segment_sum(src, seg, n)
kernel_name = 'mk_adj_preln_d4_adj_r2_770a34'

def setup_inputs(seed: int=0):
    np.random.seed(seed)
    _w = jnp.asarray

    def _rec_inputs():
        import jax
        import jax.numpy as jnp
        _gk = jax.random.key(seed)
        x = 7.22e-05 + 1 * jax.random.normal(jax.random.fold_in(_gk, 1), (128, 128, 128), jnp.float32)
        _w = (1.0 + jnp.arange(128, dtype=jnp.float32)) ** (-0.5)
        _w = _w / _w.mean()
        _pij = jnp.clip(0.03125 * _w[:, None] * _w[None, :], 0.0, 1.0)
        _a = jax.random.uniform(jax.random.fold_in(_gk, 2), (128, 128, 128)) < _pij
        _a = jnp.logical_or(_a, jnp.swapaxes(_a, -1, -2))
        _a = jnp.logical_or(_a, jnp.eye(128, dtype=bool))
        _af = _a.astype(jnp.float32)
        adj = _af
        return (x, adj)
    x, adj = _rec_inputs()

    def _L0_gnn_setup():
        import jax, jax.numpy as jnp
        import numpy as np
        from jax import lax
        DIM = 128
        EPS = 1e-05

        def _bn(h, g, b, m, v):
            scale = g / jnp.sqrt(v + EPS)
            return h * scale[None, :, None] + (b - m * scale)[None, :, None]

        def _conv1d(h, w, pad):
            return lax.conv_general_dilated(h, w, window_strides=(1,), padding=[(pad, pad)], dimension_numbers=('NCH', 'OIH', 'NCH'))
        key = jax.random.key(seed)
        ks = jax.random.split(key, 16)
        bs, n, d = (16, 1024, DIM)
        s = 0.05
        return {'x': jax.random.normal(ks[0], (bs, n, d), jnp.float32), 'mask': jnp.ones((bs, n, n), jnp.float32), 'w_se': jax.random.normal(ks[1], (3, d), jnp.float32) * s, 'b_se': jnp.zeros((3,), jnp.float32), 'conv1_w': jax.random.normal(ks[2], (d, d, 1), jnp.float32) * s, 'bn1_g': jnp.ones((d,), jnp.float32), 'bn1_b': jnp.zeros((d,), jnp.float32), 'bn1_m': jnp.zeros((d,), jnp.float32), 'bn1_v': jnp.ones((d,), jnp.float32), 'conv2_w': jax.random.normal(ks[3], (d, d, 17), jnp.float32) * s, 'bn2_g': jnp.ones((d,), jnp.float32), 'bn2_b': jnp.zeros((d,), jnp.float32), 'bn2_m': jnp.zeros((d,), jnp.float32), 'bn2_v': jnp.ones((d,), jnp.float32), 'w_msg': jax.random.normal(ks[4], (d, d), jnp.float32) * s, 'b_msg': jnp.zeros((d,), jnp.float32), 'w_ih': jax.random.normal(ks[5], (3 * d, 2 * d), jnp.float32) * s, 'b_ih': jnp.zeros((3 * d,), jnp.float32), 'w_hh': jax.random.normal(ks[6], (3 * d, d), jnp.float32) * s, 'b_hh': jnp.zeros((3 * d,), jnp.float32)}
    _L0_gnn_all = _L0_gnn_setup()
    _L0_gnn_in = {k: v for k, v in _L0_gnn_all.items() if k in ('w_se', 'b_se', 'conv1_w', 'bn1_g', 'bn1_b', 'bn1_m', 'bn1_v', 'conv2_w', 'bn2_g', 'bn2_b', 'bn2_m', 'bn2_v', 'w_msg', 'b_msg', 'w_ih', 'b_ih', 'w_hh', 'b_hh')}
    del _L0_gnn_all

    def _L1_gnn_setup():
        import jax, jax.numpy as jnp
        import numpy as np
        B, N, D = (4, 2048, 128)
        DENSITY = 0.02
        key = jax.random.key(seed)
        kx, ka1, ka2, kwt, kbt, kwh, kth = jax.random.split(key, 7)
        x = jax.random.normal(kx, (B, N, D), dtype=jnp.float32)
        mask = jax.random.uniform(ka1, (B, N, N)) < DENSITY
        vals = jax.random.uniform(ka2, (B, N, N), dtype=jnp.float32)
        adj = jnp.where(mask, vals, 0.0).astype(jnp.float32)
        s = 0.02
        W_t = s * jax.random.normal(kwt, (D, D), dtype=jnp.float32)
        b_t = s * jax.random.normal(kbt, (D,), dtype=jnp.float32)
        W_h = s * jax.random.normal(kwh, (D, D), dtype=jnp.float32)
        theta = s * jax.random.normal(kth, (D, D), dtype=jnp.float32)
        return {'x': x, 'adj': adj, 'W_t': W_t, 'b_t': b_t, 'W_h': W_h, 'theta': theta}
    _L1_gnn_all = _L1_gnn_setup()
    _L1_gnn_in = {k: v for k, v in _L1_gnn_all.items() if k in ('W_t', 'b_t', 'W_h', 'theta')}
    del _L1_gnn_all

    def _L2_gnn_setup():
        import jax, jax.numpy as jnp
        import numpy as np
        B, K, H = (32, 512, 128)
        LN_EPS = 1e-05

        def layer_norm(x, gamma, beta):
            mu = jnp.mean(x, axis=-1, keepdims=True)
            var = jnp.mean(jnp.square(x - mu), axis=-1, keepdims=True)
            return (x - mu) * jax.lax.rsqrt(var + LN_EPS) * gamma + beta
        key = jax.random.key(seed)
        k1, k2, k3, k4 = jax.random.split(key, 4)
        x = jax.random.normal(k1, (B, K, H), dtype=jnp.float32)
        adj = jax.random.uniform(k2, (B, K, K), dtype=jnp.float32)
        s = 1.0 / np.sqrt(H)
        W_rel = jax.random.normal(k3, (H, H), dtype=jnp.float32) * s
        b_rel = jnp.zeros((H,), dtype=jnp.float32)
        W_root = jax.random.normal(k4, (H, H), dtype=jnp.float32) * s
        ln_gamma = jnp.ones((H,), dtype=jnp.float32)
        ln_beta = jnp.zeros((H,), dtype=jnp.float32)
        return {'x': x, 'adj': adj, 'W_rel': W_rel, 'b_rel': b_rel, 'W_root': W_root, 'ln_gamma': ln_gamma, 'ln_beta': ln_beta}
    _L2_gnn_all = _L2_gnn_setup()
    _L2_gnn_in = {k: v for k, v in _L2_gnn_all.items() if k in ('W_rel', 'b_rel', 'W_root', 'ln_gamma', 'ln_beta')}
    del _L2_gnn_all

    def _L3_gnn_setup():
        import jax, jax.numpy as jnp
        import numpy as np
        B, N, D, H = (8, 1024, 128, 512)
        RMS_EPS = 1e-06

        def _rmsnorm(h, w, eps=RMS_EPS):
            var = jnp.mean(jnp.square(h), axis=-1, keepdims=True)
            return h * jax.lax.rsqrt(var + eps) * w
        key = jax.random.key(seed)
        ks = jax.random.split(key, 5)
        x = jax.random.normal(ks[0], (B, N, D), dtype=jnp.float32)
        adjacency = jax.random.uniform(ks[1], (B, N, N), dtype=jnp.float32)
        epsilon = jnp.zeros((), dtype=jnp.float32)
        W1 = jax.random.normal(ks[2], (D, H), dtype=jnp.float32) * (1.0 / np.sqrt(D))
        b1 = jnp.zeros((H,), dtype=jnp.float32)
        rms_weight = jnp.ones((H,), dtype=jnp.float32)
        W2 = jax.random.normal(ks[3], (H, D), dtype=jnp.float32) * (1.0 / np.sqrt(H))
        b2 = jnp.zeros((D,), dtype=jnp.float32)
        return {'x': x, 'adjacency': adjacency, 'epsilon': epsilon, 'W1': W1, 'b1': b1, 'rms_weight': rms_weight, 'W2': W2, 'b2': b2}
    _L3_gnn_all = _L3_gnn_setup()
    _L3_gnn_in = {k: v for k, v in _L3_gnn_all.items() if k in ('epsilon', 'W1', 'b1', 'rms_weight', 'W2', 'b2')}
    del _L3_gnn_all
    return {'x': x, 'adj': adj, 'L0_gnn_w_se': _L0_gnn_in['w_se'], 'L0_gnn_b_se': _L0_gnn_in['b_se'], 'L0_gnn_conv1_w': _L0_gnn_in['conv1_w'], 'L0_gnn_bn1_g': _L0_gnn_in['bn1_g'], 'L0_gnn_bn1_b': _L0_gnn_in['bn1_b'], 'L0_gnn_bn1_m': _L0_gnn_in['bn1_m'], 'L0_gnn_bn1_v': _L0_gnn_in['bn1_v'], 'L0_gnn_conv2_w': _L0_gnn_in['conv2_w'], 'L0_gnn_bn2_g': _L0_gnn_in['bn2_g'], 'L0_gnn_bn2_b': _L0_gnn_in['bn2_b'], 'L0_gnn_bn2_m': _L0_gnn_in['bn2_m'], 'L0_gnn_bn2_v': _L0_gnn_in['bn2_v'], 'L0_gnn_w_msg': _L0_gnn_in['w_msg'], 'L0_gnn_b_msg': _L0_gnn_in['b_msg'], 'L0_gnn_w_ih': _L0_gnn_in['w_ih'], 'L0_gnn_b_ih': _L0_gnn_in['b_ih'], 'L0_gnn_w_hh': _L0_gnn_in['w_hh'], 'L0_gnn_b_hh': _L0_gnn_in['b_hh'], 'L1_gnn_W_t': _L1_gnn_in['W_t'], 'L1_gnn_b_t': _L1_gnn_in['b_t'], 'L1_gnn_W_h': _L1_gnn_in['W_h'], 'L1_gnn_theta': _L1_gnn_in['theta'], 'L2_gnn_W_rel': _L2_gnn_in['W_rel'], 'L2_gnn_b_rel': _L2_gnn_in['b_rel'], 'L2_gnn_W_root': _L2_gnn_in['W_root'], 'L2_gnn_ln_gamma': _L2_gnn_in['ln_gamma'], 'L2_gnn_ln_beta': _L2_gnn_in['ln_beta'], 'L3_gnn_epsilon': _L3_gnn_in['epsilon'], 'L3_gnn_W1': _L3_gnn_in['W1'], 'L3_gnn_b1': _L3_gnn_in['b1'], 'L3_gnn_rms_weight': _L3_gnn_in['rms_weight'], 'L3_gnn_W2': _L3_gnn_in['W2'], 'L3_gnn_b2': _L3_gnn_in['b2']}

def reference(x, adj, L0_gnn_w_se, L0_gnn_b_se, L0_gnn_conv1_w, L0_gnn_bn1_g, L0_gnn_bn1_b, L0_gnn_bn1_m, L0_gnn_bn1_v, L0_gnn_conv2_w, L0_gnn_bn2_g, L0_gnn_bn2_b, L0_gnn_bn2_m, L0_gnn_bn2_v, L0_gnn_w_msg, L0_gnn_b_msg, L0_gnn_w_ih, L0_gnn_b_ih, L0_gnn_w_hh, L0_gnn_b_hh, L1_gnn_W_t, L1_gnn_b_t, L1_gnn_W_h, L1_gnn_theta, L2_gnn_W_rel, L2_gnn_b_rel, L2_gnn_W_root, L2_gnn_ln_gamma, L2_gnn_ln_beta, L3_gnn_epsilon, L3_gnn_W1, L3_gnn_b1, L3_gnn_rms_weight, L3_gnn_W2, L3_gnn_b2):
    import jax
    import jax.numpy as jnp

    def _L0_gnn_ref(x, mask, w_se, b_se, conv1_w, bn1_g, bn1_b, bn1_m, bn1_v, conv2_w, bn2_g, bn2_b, bn2_m, bn2_v, w_msg, b_msg, w_ih, b_ih, w_hh, b_hh):
        import jax, jax.numpy as jnp
        import numpy as np
        from jax import lax
        DIM = 128
        EPS = 1e-05

        def _bn(h, g, b, m, v):
            scale = g / jnp.sqrt(v + EPS)
            return h * scale[None, :, None] + (b - m * scale)[None, :, None]

        def _conv1d(h, w, pad):
            return lax.conv_general_dilated(h, w, window_strides=(1,), padding=[(pad, pad)], dimension_numbers=('NCH', 'OIH', 'NCH'))
        d = x.shape[-1]
        xc = jnp.transpose(x, (0, 2, 1))
        h = _bn(_conv1d(xc, conv1_w, 0), bn1_g, bn1_b, bn1_m, bn1_v)
        h = jax.nn.relu(h)
        h = _bn(_conv1d(h, conv2_w, 8), bn2_g, bn2_b, bn2_m, bn2_v)
        x_conv = jnp.transpose(jax.nn.relu(h + xc), (0, 2, 1))
        s = x @ w_se.T + b_se
        sq = jnp.sum(s * s, axis=-1)
        dist = sq[:, :, None] + sq[:, None, :] - 2.0 * jnp.einsum('bnd,bmd->bnm', s, s)
        A = jnp.exp(-dist) * mask
        msg = jax.nn.relu(x @ w_msg.T + b_msg)
        x_nmp = jnp.einsum('bnm,bmd->bnd', A, msg)
        x_in = jnp.concatenate([x_conv, x_nmp], axis=-1)
        gi = x_in @ w_ih.T + b_ih
        gh = x @ w_hh.T + b_hh
        gi_r, gi_z, gi_n = (gi[..., :d], gi[..., d:2 * d], gi[..., 2 * d:])
        gh_r, gh_z, gh_n = (gh[..., :d], gh[..., d:2 * d], gh[..., 2 * d:])
        r = jax.nn.sigmoid(gi_r + gh_r)
        z = jax.nn.sigmoid(gi_z + gh_z)
        nn_ = jnp.tanh(gi_n + r * gh_n)
        return (1.0 - z) * nn_ + z * x

    def _L1_gnn_ref(x, adj, W_t, b_t, W_h, theta):
        import jax, jax.numpy as jnp
        import numpy as np
        B, N, D = (4, 2048, 128)
        DENSITY = 0.02
        in_degrees = jnp.sum(adj, axis=-1)
        norm = jnp.power(in_degrees + 1e-06, -0.5)[..., None]
        f_hom = jnp.einsum('bnd,de->bne', x, theta) * norm
        f_hom = jnp.einsum('bnm,bmd->bnd', adj, f_hom) * norm
        f_het = jnp.einsum('bnd,de->bne', x, W_h)
        gate = jax.nn.sigmoid(jnp.einsum('bnd,de->bne', x, W_t) + b_t)
        out = gate * f_hom + (1.0 - gate) * f_het
        return jax.nn.elu(out)

    def _L2_gnn_ref(x, adj, W_rel, b_rel, W_root, ln_gamma, ln_beta):
        import jax, jax.numpy as jnp
        import numpy as np
        B, K, H = (32, 512, 128)
        LN_EPS = 1e-05

        def layer_norm(x, gamma, beta):
            mu = jnp.mean(x, axis=-1, keepdims=True)
            var = jnp.mean(jnp.square(x - mu), axis=-1, keepdims=True)
            return (x - mu) * jax.lax.rsqrt(var + LN_EPS) * gamma + beta
        h = layer_norm(x, ln_gamma, ln_beta)
        agg = jnp.einsum('bij,bjh->bih', adj, h)
        conv = jnp.einsum('bkh,ho->bko', agg, W_rel) + b_rel + jnp.einsum('bkh,ho->bko', h, W_root)
        return x + jax.nn.relu(conv)

    def _L3_gnn_ref(x, adjacency, epsilon, W1, b1, rms_weight, W2, b2):
        import jax, jax.numpy as jnp
        import numpy as np
        B, N, D, H = (8, 1024, 128, 512)
        RMS_EPS = 1e-06

        def _rmsnorm(h, w, eps=RMS_EPS):
            var = jnp.mean(jnp.square(h), axis=-1, keepdims=True)
            return h * jax.lax.rsqrt(var + eps) * w
        neighbor_sum = jnp.einsum('bnm,bmd->bnd', adjacency, x)
        agg = epsilon * x + neighbor_sum
        h = jnp.einsum('bnd,dh->bnh', agg, W1) + b1
        h = jax.nn.silu(_rmsnorm(h, rms_weight))
        out = jnp.einsum('bnh,hd->bnd', h, W2) + b2
        return out
    h = jnp.maximum(_layernorm(x, axis=-1), 0.0)
    x = x + _L0_gnn_ref(h, adj, L0_gnn_w_se, L0_gnn_b_se, L0_gnn_conv1_w, L0_gnn_bn1_g, L0_gnn_bn1_b, L0_gnn_bn1_m, L0_gnn_bn1_v, L0_gnn_conv2_w, L0_gnn_bn2_g, L0_gnn_bn2_b, L0_gnn_bn2_m, L0_gnn_bn2_v, L0_gnn_w_msg, L0_gnn_b_msg, L0_gnn_w_ih, L0_gnn_b_ih, L0_gnn_w_hh, L0_gnn_b_hh)
    h = jnp.maximum(_layernorm(x, axis=-1), 0.0)
    x = x + _L1_gnn_ref(h, adj, L1_gnn_W_t, L1_gnn_b_t, L1_gnn_W_h, L1_gnn_theta)
    h = jnp.maximum(_layernorm(x, axis=-1), 0.0)
    x = x + _L2_gnn_ref(h, adj, L2_gnn_W_rel, L2_gnn_b_rel, L2_gnn_W_root, L2_gnn_ln_gamma, L2_gnn_ln_beta)
    h = jnp.maximum(_layernorm(x, axis=-1), 0.0)
    x = x + _L3_gnn_ref(h, adj, L3_gnn_epsilon, L3_gnn_W1, L3_gnn_b1, L3_gnn_rms_weight, L3_gnn_W2, L3_gnn_b2)
    return x

_drawn_inputs = setup_inputs


def setup_inputs(seed=0):
    import zlib

    import numpy as np

    out = dict(_drawn_inputs(seed))
    spreads = {'L0_gnn_b_se': (0.0, 2.0),
     'L0_gnn_bn1_g': (1.0, 0.6),
     'L0_gnn_bn1_b': (0.0, 0.287),
     'L0_gnn_bn1_m': (0.0, 0.293),
     'L0_gnn_bn1_v': (1.0, 0.6),
     'L0_gnn_bn2_g': (1.0, 0.6),
     'L0_gnn_bn2_b': (0.0, 0.391),
     'L0_gnn_bn2_m': (0.0, 0.348),
     'L0_gnn_bn2_v': (1.0, 0.6),
     'L0_gnn_b_msg': (0.0, 0.1),
     'L0_gnn_b_ih': (0.0, 0.1),
     'L0_gnn_b_hh': (0.0, 0.1),
     'L2_gnn_b_rel': (0.0, 0.42),
     'L2_gnn_ln_gamma': (1.0, 0.2),
     'L2_gnn_ln_beta': (0.0, 0.1),
     'L3_gnn_b1': (0.0, 0.8),
     'L3_gnn_rms_weight': (1.0, 0.2),
     'L3_gnn_b2': (0.0, 0.303)}
    factors = {'L1_gnn_W_t': 8.0, 'L1_gnn_b_t': 64.0}
    for name, (base, spread) in spreads.items():
        noise = np.random.default_rng([zlib.crc32(name.encode()), seed]).standard_normal(out[name].shape)
        drawn = base * np.exp(spread * noise) if base else spread * noise
        out[name] = jnp.asarray(drawn.astype(out[name].dtype))
    for name, factor in factors.items():
        out[name] = (out[name] * factor).astype(out[name].dtype)
    return out
```

```python
from contextlib import ExitStack

import concourse.bass as bass
from concourse import mybir

ALU = mybir.AluOpType
ACT = mybir.ActivationFunctionType
F32 = mybir.dt.float32
F32R = mybir.dt.float32r

P = 128
GRAPHS = 128
PER = 4
GROUPS = GRAPHS // PER
TAPS = 17
HID = 512
CHUNKS = HID // P
LAG = {"N": 0, "A1": 1, "A2": 2, "B1": 3, "B2": 4, "C": 5}
TURNS = GROUPS + LAG["C"]
UNROLL = 4
LOOP_FROM, LOOP_TO = 8, GROUPS
LN_EPS = 1e-5
RMS_EPS = 1e-6
DEG_EPS = 1e-6
INF = float("inf")

WIDTHS = [("conv1", P), ("se", 96), ("msg", P), ("ih", 2 * 3 * P), ("hh", 3 * P),
          ("theta", P), ("W_h", P), ("W_t", P), ("rel", P), ("root", P), ("W1", HID), ("W2", CHUNKS * P)]
AT = {}
WIDE = 0
for _name, _width in WIDTHS:
    AT[_name] = WIDE
    WIDE += _width
COLUMN = {name: n for n, name in enumerate(
    ["g1", "g2", "b1", "b2", "m1", "m2", "v1", "v2", "ih_r", "ih_z", "ih_n", "hh_r", "hh_z", "hh_n",
     "se", "gamma", "beta", "eps", "h0", "h1", "h2", "h3", "w0", "w1", "w2", "w3"])}
ROW = {"msg": 0, "b_t": 1, "rel": 2, "out": 3}
OFFSETS = sorted(range(-(TAPS // 2), TAPS // 2 + 1), key=abs)


class Group:

    def __init__(self, loop, n):
        self.loop, self.n = loop, n
        self.real = loop is not None or 0 <= n < GROUPS

    def at(self):
        return self.n if self.loop is None else self.loop.first + self.n

    def __mod__(self, places):
        return self.n % places

    def past(self, back):
        return self.loop is not None or self.n >= back

    def upto(self, back=0):
        count = self.n - back + 1
        return min(count, GROUPS) if self.loop is None else self.loop.plus[count]

    def transfers(self, places, back=0):
        count = 16 * ((self.n - back) // places + 1)
        return count if self.loop is None else self.loop.first * (16 // places) + count


class Loop:

    def __init__(self, engine, first):
        self.first = first
        self.plus = {n: engine.snap(first + n) for n in range(-LAG["C"] - 1, UNROLL + 1)}


class Turn:

    def __init__(self, loop, t):
        self.N, self.A1, self.A2, self.B1, self.B2, self.C = (Group(loop, t - LAG[s]) for s in LAG)
        self.next_adj = Group(loop, t - LAG["A2"] + 1)


def turns(engine, turn):
    for t in range(LOOP_FROM):
        turn(Turn(None, t))
    with engine.Fori(0, (LOOP_TO - LOOP_FROM) // UNROLL, 1) as body:
        loop = Loop(engine, engine.snap(body * UNROLL + LOOP_FROM))
        for t in range(UNROLL):
            turn(Turn(loop, t))
    for t in range(LOOP_TO, TURNS):
        turn(Turn(None, t))


def graph_layers(nc, d_x, d_adj, d_weights, d_conv2, d_columns, d_rows, d_out):
    with ExitStack() as ctx:
        def sb(name, shape, dtype=F32):
            return ctx.enter_context(nc.sbuf_tensor(name, shape, dtype))

        def signal(name):
            return ctx.enter_context(nc.semaphore(name))

        def ring(name, places, shape=(P, PER, P), dtype=F32):
            return [sb(f"{name}_{n}", list(shape), dtype) for n in range(places)]

        def signals(name, n):
            return [signal(f"{name}_{k}") for k in range(n)]

        weights = sb("weights", [P, WIDE])
        conv2_hi = sb("conv2_hi", [P, TAPS, P], F32R)
        conv2_lo = sb("conv2_lo", [P, TAPS, P], F32R)
        columns = sb("columns", [P, len(COLUMN)])
        rows = sb("rows", [P, len(ROW), P])
        identity = sb("identity", [P, P])
        eps_identity = sb("eps_identity", [P, P])
        ones = sb("ones", [P, P])
        minus_half = sb("minus_half", [P, PER])
        bn_var = sb("bn_var", [P, 2])
        bn_root = sb("bn_root", [P, 2])
        bn_scale = sb("bn_scale", [P, 2])
        bn_mean = sb("bn_mean", [P, 2])
        bn_bias = sb("bn_bias", [P, 2])
        gate_sum = sb("gate_sum", [P, 2])
        gate_bias = sb("gate_bias", [P, 2])
        half_rms = sb("half_rms", [P, CHUNKS])
        w2_half = sb("w2_half", [P, CHUNKS, P])

        def weight(name, width=P, skip=0):
            return weights[:, AT[name] + skip:AT[name] + skip + width]

        def column(name, parts=P, first=0, n=1):
            return columns[first:first + parts, COLUMN[name]:COLUMN[name] + n]

        def row(name):
            return rows[:, ROW[name], :].unsqueeze(1).to_broadcast([P, PER, P])

        x_in = ring("x_in", 4)
        adj = ring("adj", 4)
        h0n = ring("h0n", 2)
        h0 = ring("h0", 2)
        c1_hi = ring("c1_hi", 2, (P, PER, P + 2), F32R)
        c1_lo = ring("c1_lo", 2, (P, PER, P + 2), F32R)
        left = ring("left", 2, (96, PER, P))
        right = ring("right", 2, (96, PER, P))
        message = ring("message", 2)
        x1 = ring("x1", 2)
        x2 = ring("x2", 2)
        x3 = ring("x3", 2)
        result = ring("result", 2)
        c1 = sb("c1", [P, PER, P])
        message_sum = sb("message_sum", [P, PER, P])
        affinity = sb("affinity", [P, PER, P])
        masked = sb("masked", [P, PER, P])
        nmp = sb("nmp", [P, PER, P])
        conv_sum = sb("conv_sum", [P, PER, P])
        x_conv = sb("x_conv", [P, PER, P])
        tanh_r = sb("tanh_r", [P, PER, P])
        tanh_z = sb("tanh_z", [P, PER, P])
        gate_r = sb("gate_r", [P, PER, P])
        gate_z = sb("gate_z", [P, PER, P])
        r_hidden = sb("r_hidden", [P, PER, P])
        n_sum = sb("n_sum", [P, PER, P])
        n_tanh = sb("n_tanh", [P, PER, P])
        h_less_n = sb("h_less_n", [P, PER, P])
        gru = sb("gru", [P, PER, P])
        h1n = sb("h1n", [P, PER, P])
        h1 = sb("h1", [P, PER, P])
        degree = sb("degree", [P, PER])
        deg_scale = sb("deg_scale", [P, PER])
        f_hom = sb("f_hom", [P, PER, P])
        f_het = sb("f_het", [P, PER, P])
        gate_sum1 = sb("gate_sum1", [P, PER, P])
        gate_tanh = sb("gate_tanh", [P, PER, P])
        hom = sb("hom", [P, PER, P])
        mix = sb("mix", [P, PER, P])
        elu_pos = sb("elu_pos", [P, PER, P])
        elu_neg = sb("elu_neg", [P, PER, P])
        h2n = sb("h2n", [P, PER, P])
        h2 = sb("h2", [P, PER, P])
        h2nn = sb("h2nn", [P, PER, P])
        h2_col = sb("h2_col", [P, PER, P])
        rel = sb("rel", [P, PER, P])
        x2_h2 = sb("x2_h2", [P, PER, P])
        conv_rel = sb("conv_rel", [P, PER, P])
        h3n = sb("h3n", [P, PER, P])
        h3 = sb("h3", [P, PER, P])
        adj_eps = sb("adj_eps", [P, PER, P])
        agg = sb("agg", [P, PER, P])
        perceptron = sb("perceptron", [P, 2 * CHUNKS * PER * P])
        conv2_raw = perceptron[:, 0:TAPS * P].rearrange("p (k o) -> p k o", k=TAPS)
        halves = perceptron[:, :].rearrange("p (k b n) -> p k b n", k=2 * CHUNKS, b=PER)
        square = [halves[:, c, :, :] for c in range(CHUNKS)]
        hidden = [halves[:, CHUNKS + c, :, :] for c in range(CHUNKS)]
        mean_square = sb("mean_square", [P, PER])
        rms_scale = sb("rms_scale", [P, PER])
        rms_diag = sb("rms_diag", [P, PER, P])
        rms_wide = sb("rms_wide", [P, PER, P])
        silu = ring("silu", CHUNKS)
        x3_b2 = sb("x3_b2", [P, PER, P])

        bank = [ctx.enter_context(nc.psum_tensor(f"bank_{n}", [P, PER, P], F32)) for n in range(8)]

        weights_loaded = signal("weights_loaded")
        identity_blank = signal("identity_blank")
        constants_ready = signal("constants_ready")
        bn_var_ready = signal("bn_var_ready")
        dve_setup = signal("dve_setup")
        dve_held, pool_held = signal("dve_held"), signal("pool_held")
        prepared = signal("prepared")
        x_loaded = signals("x_loaded", 4)
        adj_loaded = signals("adj_loaded", 4)
        stored = signals("stored", 2)

        class Norm:

            def __init__(self, name):
                self.stats = sb(f"{name}_stats", [P, PER, 6])
                self.moments = sb(f"{name}_moments", [P, PER, 2])
                self.var = sb(f"{name}_var", [P, PER])
                self.scale = sb(f"{name}_scale", [P, PER])
                self.stats_ready = signal(f"{name}_stats_ready")
                self.moments_ready = signal(f"{name}_moments_ready")
                self.var_ready = signal(f"{name}_var_ready")
                self.scale_ready = signal(f"{name}_scale_ready")
                self.normed = signal(f"{name}_normed")

        norm0, norm1, norm2, norm2b, norm3 = (Norm(f"norm{n}") for n in ("0", "1", "2", "2b", "3"))

        h0_turned, h0_ready = signal("h0_turned"), signal("h0_ready")
        conv1_done, c1_ready = signal("conv1_done"), signal("c1_ready")
        c1_hi_ready, c1_lo_ready = signal("c1_hi_ready"), signal("c1_lo_ready")
        se_done, left_ready, right_ready = signal("se_done"), signal("left_ready"), signal("right_ready")
        message_done, message_summed, message_ready = signal("message_done"), signal("message_summed"), signal("message_ready")
        dist_done, affinity_ready, masked_ready = signal("dist_done"), signal("affinity_ready"), signal("masked_ready")
        nmp_done, nmp_ready = signal("nmp_done"), signal("nmp_ready")
        conv2_done, conv_summed, x_conv_ready = signal("conv2_done"), signal("conv_summed"), signal("x_conv_ready")
        hidden_n_done, r_done, z_done, input_n_done = signal("hidden_n_done"), signal("r_done"), signal("z_done"), signal("input_n_done")
        tanh_r_ready, gate_r_ready, tanh_z_ready, gate_z_ready = signal("tanh_r_ready"), signal("gate_r_ready"), signal("tanh_z_ready"), signal("gate_z_ready")
        r_hidden_ready, n_summed, n_ready = signal("r_hidden_ready"), signal("n_summed"), signal("n_ready")
        h_less_n_ready, z_part_ready, gru_ready = signal("h_less_n_ready"), signal("z_part_ready"), signal("gru_ready")
        gru_turned, x1_ready = signal("gru_turned"), signal("x1_ready")
        degree_done, degree_ready, deg_scale_ready = signal("degree_done"), signal("degree_ready"), signal("deg_scale_ready")
        h1_turned, h1_ready = signal("h1_turned"), signal("h1_ready")
        theta_done, het_done, gate_done = signal("theta_done"), signal("het_done"), signal("gate_done")
        f_hom_ready, f_het_ready, gate1_summed, gate1_ready = signal("f_hom_ready"), signal("f_het_ready"), signal("gate1_summed"), signal("gate1_ready")
        hom_done, hom_ready, difference_ready, gated_ready, mix_ready = signal("hom_done"), signal("hom_ready"), signal("difference_ready"), signal("gated_ready"), signal("mix_ready")
        elu_pos_ready, elu_exp_ready, elu_neg_ready, x2_ready = signal("elu_pos_ready"), signal("elu_exp_ready"), signal("elu_neg_ready"), signal("x2_ready")
        h2_ready, h2_turned, h2_col_ready = signal("h2_ready"), signal("h2_turned"), signal("h2_col_ready")
        rel_done, rel_ready, conv_rel_done = signal("rel_done"), signal("rel_ready"), signal("conv_rel_done")
        x2_h2_ready, conv_rel_ready, x3_ready = signal("x2_h2_ready"), signal("conv_rel_ready"), signal("x3_ready")
        h3_ready, adj_eps_ready, agg_done, agg_ready = signal("h3_ready"), signal("adj_eps_ready"), signal("agg_done"), signal("agg_ready")
        hidden_done, square_ready, hidden_ready = signals("hidden_done", CHUNKS), signals("square_ready", CHUNKS), signals("hidden_ready", CHUNKS)
        square_summed, rms_done, mean_square_ready, rms_scale_ready = signals("square_summed", 2), signal("rms_done"), signal("mean_square_ready"), signal("rms_scale_ready")
        rms_diag_ready, rms_wide_done, rms_wide_ready = signal("rms_diag_ready"), signal("rms_wide_done"), signal("rms_wide_ready")
        scaled_ready, silu_tanh_ready, silu_ready = signals("scaled_ready", CHUNKS), signals("silu_tanh_ready", CHUNKS), signals("silu_ready", CHUNKS)
        x3_b2_ready, out_done, result_ready = signal("x3_b2_ready"), signal("out_done"), signal("result_ready")

        block = ctx.enter_context(nc.Block())

        @block.sync
        def _(sp):
            sp.dma_start(columns[:, :], d_columns).then_inc(weights_loaded, 16)
            sp.dma_start(weights[:, :], d_weights).then_inc(weights_loaded, 16)
            sp.dma_start(conv2_raw, d_conv2).then_inc(weights_loaded, 16)
            sp.dma_start(rows[:, :, :], d_rows.partition_broadcast(P)).then_inc(weights_loaded, 16)

            def turn(t):
                if t.N.real:
                    if t.N.past(4): sp.wait_ge(x1_ready, t.N.upto(4))
                    sp.dma_start(x_in[t.N % 4][:, :, :],
                                 d_x[:, t.N.at(), :, :]).then_inc(x_loaded[t.N % 4], 16)
                if t.next_adj.real:
                    if t.next_adj.past(4): sp.wait_ge(conv_rel_done, t.next_adj.upto(4))
                    if t.next_adj.past(4): sp.wait_ge(adj_eps_ready, t.next_adj.upto(4))
                    sp.dma_start(adj[t.next_adj % 4][:, :, :],
                                 d_adj[:, t.next_adj.at(), :, :]).then_inc(adj_loaded[t.next_adj % 4], 16)
                if t.C.real:
                    if t.C.past(0): sp.wait_ge(result_ready, t.C.upto())
                    sp.dma_start(d_out[:, t.C.at(), :, :],
                                 result[t.C % 2][:, :, :]).then_inc(stored[t.C % 2], 16)

            turns(sp, turn)
            for done in stored:
                sp.wait_ge(done, 16 * (GROUPS // 2))

        @block.tensor
        def _(pe):
            pe.wait_ge(prepared, 1)

            def per_graph(out, lhs, rhs, start=True, stop=True):
                for b in range(PER):
                    last = pe.matmul(out[:, b, :], lhs(b), rhs(b), start=start, stop=stop,
                                     skip_group_check=True)
                return last

            def turned(out, tile):
                for b in range(PER):
                    last = pe.transpose(out[:, b, :], tile[:, b, :], identity[:, :])
                return last

            def conv2(g, taps):
                hi, lo = c1_hi[g % 2], c1_lo[g % 2]
                for k in taps:
                    off = OFFSETS[k]
                    a = max(0, -off) // 2 * 2
                    n = P - a if off <= 0 else (P - off + 1) // 2 * 2
                    tap = off + TAPS // 2
                    src = slice(1 + a + off, 1 + a + off + n)
                    for w, c in ((conv2_hi, hi), (conv2_hi, lo), (conv2_lo, hi)):
                        last = pe.matmul(bank[2][:, :, a:a + n], w[:, tap, :], c[:, :, src],
                                         start=(k == 0 and w is conv2_hi and c is hi),
                                         stop=(k == TAPS - 1 and w is conv2_lo), skip_group_check=True)
                return last

            def turn(t):
                g = t.A2
                if g.real:
                    pe.wait_ge(c1_hi_ready, g.upto())
                    pe.wait_ge(c1_lo_ready, g.upto())
                    if g.past(1): pe.wait_ge(conv_summed, g.upto(1))
                    conv2(g, range(0, 4))
                g = t.A1
                if g.real:
                    pe.wait_ge(norm0.normed, g.upto())
                    if t.C.past(1): pe.wait_ge(rms_wide_ready, t.C.upto(1))
                    turned(bank[0], h0n[g % 2]).then_inc(h0_turned, 1)
                g = t.A2
                if g.real:
                    pe.wait_ge(left_ready, g.upto())
                    pe.wait_ge(right_ready, g.upto())
                    if g.past(1): pe.wait_ge(r_hidden_ready, g.upto(1))
                    per_graph(bank[1], lambda b: left[g % 2][:, b, :], lambda b: right[g % 2][:, b, :]).then_inc(dist_done, 1)
                g = t.B1
                if g.real:
                    pe.wait_ge(adj_loaded[g % 4], g.transfers(4))
                    if t.A2.past(1): pe.wait_ge(tanh_r_ready, t.A2.upto(1))
                    for b in range(PER):
                        last = pe.matmul(bank[3][:, 0, b:b + 1], adj[g % 4][:, b, :], ones[:, 0:1],
                                         start=True, stop=True, skip_group_check=True)
                    last.then_inc(degree_done, 1)
                    pe.wait_ge(norm1.normed, g.upto())
                    if t.A2.past(1): pe.wait_ge(n_summed, t.A2.upto(1))
                    turned(bank[4], h1n).then_inc(h1_turned, 1)
                g = t.A1
                if g.real:
                    pe.wait_ge(h0_ready, g.upto())
                    if t.A2.past(1): pe.wait_ge(tanh_z_ready, t.A2.upto(1))
                    pe.matmul(bank[5][:, :, :], weight("conv1"), h0[g % 2][:, :, :],
                              start=True, stop=True).then_inc(conv1_done, 1)
                g = t.C
                if g.real:
                    pe.wait_ge(h3_ready, g.upto())
                    pe.wait_ge(adj_eps_ready, g.upto())
                    if g.past(1): pe.wait_ge(result_ready, g.upto(1))
                    per_graph(bank[6], lambda b: h3[:, b, :], lambda b: adj_eps[:, b, :]).then_inc(agg_done, 1)
                g = t.A1
                if g.real:
                    if t.A2.past(1): pe.wait_ge(x1_ready, t.A2.upto(1))
                    pe.matmul(bank[7][0:96, :, :], weight("se", 96), h0[g % 2][:, :, :],
                              start=True, stop=True).then_inc(se_done, 1)
                    pe.wait_ge(h0_ready, g.upto())
                    per_graph(bank[0], lambda b: h0[g % 2][:, b, :], lambda b: weight("msg")).then_inc(message_done, 1)
                g = t.A2
                if g.real:
                    conv2(g, range(4, 6))
                g = t.C
                if g.real:
                    pe.wait_ge(agg_ready, g.upto())
                    for c, place, read, reader in ((0, 1, affinity_ready, t.A2), (1, 3, degree_ready, t.B1),
                                                   (2, 4, h1_ready, t.B1), (3, 5, c1_ready, t.A1)):
                        if reader.past(0): pe.wait_ge(read, reader.upto())
                        pe.matmul(bank[place][:, :, :], weight("W1", P, c * P), agg[:, :, :],
                                  start=True, stop=True).then_inc(hidden_done[c], 1)
                g = t.B1
                if g.real:
                    pe.wait_ge(h1_ready, g.upto())
                    if t.C.past(0): pe.wait_ge(agg_ready, t.C.upto())
                    per_graph(bank[6], lambda b: h1[:, b, :], lambda b: weight("theta")).then_inc(theta_done, 1)
                    if t.A1.past(0): pe.wait_ge(left_ready, t.A1.upto())
                    if t.A1.past(0): pe.wait_ge(right_ready, t.A1.upto())
                    per_graph(bank[7], lambda b: h1[:, b, :], lambda b: weight("W_h")).then_inc(het_done, 1)
                    if t.A1.past(0): pe.wait_ge(message_summed, t.A1.upto())
                    per_graph(bank[0], lambda b: h1[:, b, :], lambda b: weight("W_t")).then_inc(gate_done, 1)
                g = t.A2
                if g.real:
                    pe.wait_ge(masked_ready, g.upto())
                    pe.wait_ge(message_ready, g.upto())
                    if t.C.past(0): pe.wait_ge(hidden_ready[0], t.C.upto())
                    per_graph(bank[1], lambda b: message[g % 2][:, b, :], lambda b: masked[:, b, :]).then_inc(nmp_done, 1)
                g = t.B2
                if g.real:
                    pe.wait_ge(norm2b.normed, g.upto())
                    if t.C.past(0): pe.wait_ge(hidden_ready[1], t.C.upto())
                    turned(bank[3], h2nn).then_inc(h2_turned, 1)
                    if t.A2.real:
                        conv2(t.A2, range(6, 8))
                    pe.wait_ge(h2_col_ready, g.upto())
                    if t.C.past(0): pe.wait_ge(hidden_ready[2], t.C.upto())
                    per_graph(bank[4], lambda b: h2_col[:, b, :], lambda b: weight("rel")).then_inc(rel_done, 1)
                elif t.A2.real:
                    conv2(t.A2, range(6, 8))
                g = t.B1
                if g.real:
                    pe.wait_ge(f_hom_ready, g.upto())
                    if t.C.past(0): pe.wait_ge(hidden_ready[3], t.C.upto())
                    per_graph(bank[5], lambda b: adj[g % 4][:, b, :], lambda b: f_hom[:, b, :]).then_inc(hom_done, 1)
                g = t.B2
                if g.real:
                    pe.wait_ge(rel_ready, g.upto())
                    if t.B1.past(0): pe.wait_ge(f_hom_ready, t.B1.upto())
                    for b in range(PER):
                        pe.matmul(bank[6][:, b, :], h2_col[:, b, :], weight("root"), start=True, stop=False,
                                  skip_group_check=True)
                        last = pe.matmul(bank[6][:, b, :], adj[g % 4][:, b, :], rel[:, b, :], start=False, stop=True,
                                         skip_group_check=True)
                    last.then_inc(conv_rel_done, 1)
                g = t.C
                if g.real:
                    pe.wait_ge(square_summed[0], g.upto())
                    pe.wait_ge(square_summed[1], g.upto())
                    if t.B1.past(0): pe.wait_ge(f_het_ready, t.B1.upto())
                    for b in range(PER):
                        for k in range(2):
                            last = pe.matmul(bank[7][:, 0, b:b + 1], square[2 * k][:, b, :], ones[:, 0:1],
                                             start=(k == 0), stop=(k == 1), skip_group_check=True)
                    last.then_inc(rms_done, 1)
                g = t.A2
                if g.real:
                    conv2(g, range(8, TAPS)).then_inc(conv2_done, 1)
                g = t.C
                if g.real:
                    pe.wait_ge(rms_diag_ready, g.upto())
                    if t.B1.past(0): pe.wait_ge(gate1_summed, t.B1.upto())
                    pe.matmul(bank[0][:, :, :], ones[:, :], rms_diag[:, :, :],
                              start=True, stop=True).then_inc(rms_wide_done, 1)
                g = t.A2
                if g.real:
                    def gate(place, part, sources, start=True, stop=True):
                        for k, (name, skip, tile) in enumerate(sources):
                            last = pe.matmul(bank[place][:, :, :], weight(name, P, skip + part * P), tile[:, :, :],
                                             start=(start and k == 0), stop=(stop and k == len(sources) - 1))
                        return last

                    from_h, from_conv, from_nmp = ("hh", 0, h0[g % 2]), ("ih", 0, x_conv), ("ih", 3 * P, nmp)
                    pe.wait_ge(nmp_ready, g.upto())
                    gate(1, 2, [from_h]).then_inc(hidden_n_done, 1)
                    if t.B2.past(0): pe.wait_ge(h2_col_ready, t.B2.upto())
                    gate(3, 0, [from_h, from_nmp], stop=False)
                    pe.wait_ge(x_conv_ready, g.upto())
                    gate(3, 0, [from_conv], start=False).then_inc(r_done, 1)
                    if t.B2.past(0): pe.wait_ge(rel_ready, t.B2.upto())
                    gate(4, 2, [from_nmp, from_conv]).then_inc(input_n_done, 1)
                    if t.B1.past(0): pe.wait_ge(hom_ready, t.B1.upto())
                    gate(5, 1, [from_h, from_nmp, from_conv]).then_inc(z_done, 1)
                g = t.C
                if g.real:
                    for c in range(CHUNKS):
                        pe.wait_ge(silu_ready[c], g.upto())
                    if t.B2.past(0): pe.wait_ge(conv_rel_ready, t.B2.upto())
                    for b in range(PER):
                        for c in range(CHUNKS):
                            last = pe.matmul(bank[6][:, b, :], silu[c][:, b, :], w2_half[:, c, :],
                                             start=(c == 0), stop=(c == CHUNKS - 1), skip_group_check=True)
                    last.then_inc(out_done, 1)
                g = t.A2
                if g.real:
                    pe.wait_ge(gru_ready, g.upto())
                    if t.C.past(0): pe.wait_ge(mean_square_ready, t.C.upto())
                    turned(bank[7], gru).then_inc(gru_turned, 1)

            turns(pe, turn)

        @block.scalar
        def _(act):
            act.wait_ge(prepared, 1)

            def turn(t):
                g = t.C
                if g.real:
                    act.wait_ge(norm3.normed, g.upto())
                    if g.past(1): act.wait_ge(agg_done, g.upto(1))
                    act.activation(h3[:, :, :], h3n[:, :, :], ACT.Relu).then_inc(h3_ready, 1)
                g = t.B2
                if g.real:
                    act.wait_ge(norm2.normed, g.upto())
                    if g.past(1): act.wait_ge(norm2b.normed, g.upto(1))
                    if g.past(1): act.wait_ge(x2_h2_ready, g.upto(1))
                    act.activation(h2[:, :, :], h2n[:, :, :], ACT.Relu).then_inc(h2_ready, 1)
                g = t.A1
                if g.real:
                    act.wait_ge(h0_turned, g.upto())
                    if g.past(2): act.wait_ge(z_done, g.upto(2))
                    if g.past(2): act.wait_ge(h_less_n_ready, g.upto(2))
                    act.activation(h0[g % 2][:, :, :], bank[0][:, :, :], ACT.Relu).then_inc(h0_ready, 1)
                g = t.A2
                if g.real:
                    act.wait_ge(dist_done, g.upto())
                    if g.past(1): act.wait_ge(masked_ready, g.upto(1))
                    act.activation(affinity[:, :, :], bank[1][:, :, :], ACT.Exp).then_inc(affinity_ready, 1)
                g = t.B1
                if g.real:
                    act.wait_ge(h1_turned, g.upto())
                    if g.past(1): act.wait_ge(gate_done, g.upto(1))
                    act.activation(h1[:, :, :], bank[4][:, :, :], ACT.Relu).then_inc(h1_ready, 1)
                g = t.A1
                if g.real:
                    act.wait_ge(conv1_done, g.upto())
                    if g.past(1): act.wait_ge(c1_hi_ready, g.upto(1))
                    if g.past(1): act.wait_ge(c1_lo_ready, g.upto(1))
                    act.activation(c1[:, :, :], bank[5][:, :, :], ACT.Relu, bias=bn_bias[:, 0:1],
                                   scale=bn_scale[:, 0:1]).then_inc(c1_ready, 1)
                g = t.C
                if g.real:
                    act.wait_ge(agg_done, g.upto())
                    if g.past(1): act.wait_ge(hidden_done[CHUNKS - 1], g.upto(1))
                    act.activation(agg[:, :, :], bank[6][:, :, :], ACT.Copy).then_inc(agg_ready, 1)
                g = t.A1
                if g.real:
                    act.wait_ge(se_done, g.upto())
                    act.wait_ge(left_ready, g.upto())
                    if g.past(2): act.wait_ge(dist_done, g.upto(2))
                    act.activation(right[g % 2][0:32, :, :], bank[7][0:32, :, :], ACT.Identity, bias=column("se", 32))
                    act.activation(left[g % 2][32:64, :, :], bank[7][32:64, :, :], ACT.Square, bias=column("se", 32, 32))
                    act.activation(right[g % 2][64:96, :, :], bank[7][64:96, :, :], ACT.Square,
                                   bias=column("se", 32, 64)).then_inc(right_ready, 1)
                    act.wait_ge(message_summed, g.upto())
                    if g.past(2): act.wait_ge(nmp_done, g.upto(2))
                    act.activation(message[g % 2][:, :, :], message_sum[:, :, :], ACT.Relu).then_inc(message_ready, 1)
                g = t.C
                if g.real:
                    for c, place in enumerate((1, 3, 4, 5)):
                        act.wait_ge(hidden_done[c], g.upto())
                        if g.past(1): act.wait_ge(square_summed[c // 2], g.upto(1))
                        if g.past(1): act.wait_ge(rms_done, g.upto(1))
                        act.activation(square[c][:, :, :], bank[place][:, :, :], ACT.Square,
                                       bias=column(f"h{c}")).then_inc(square_ready[c], 1)
                        if g.past(1): act.wait_ge(silu_ready[c], g.upto(1))
                        act.activation(hidden[c][:, :, :], bank[place][:, :, :], ACT.Identity,
                                       bias=column(f"h{c}")).then_inc(hidden_ready[c], 1)
                g = t.B1
                if g.real:
                    act.wait_ge(het_done, g.upto())
                    if g.past(1): act.wait_ge(mix_ready, g.upto(1))
                    act.activation(f_het[:, :, :], bank[7][:, :, :], ACT.Copy).then_inc(f_het_ready, 1)
                g = t.A2
                if g.real:
                    act.wait_ge(nmp_done, g.upto())
                    if g.past(1): act.wait_ge(z_done, g.upto(1))
                    act.activation(nmp[:, :, :], bank[1][:, :, :], ACT.Copy).then_inc(nmp_ready, 1)
                g = t.B2
                if g.real:
                    act.wait_ge(h2_turned, g.upto())
                    if g.past(1): act.wait_ge(conv_rel_done, g.upto(1))
                    act.activation(h2_col[:, :, :], bank[3][:, :, :], ACT.Identity, bias=column("beta"),
                                   scale=column("gamma")).then_inc(h2_col_ready, 1)
                g = t.B1
                if g.real:
                    act.wait_ge(gate1_summed, g.upto())
                    if g.past(1): act.wait_ge(gated_ready, g.upto(1))
                    act.activation(gate_tanh[:, :, :], gate_sum1[:, :, :], ACT.Tanh, scale=0.5).then_inc(gate1_ready, 1)
                g = t.B2
                if g.real:
                    act.wait_ge(rel_done, g.upto())
                    act.activation(rel[:, :, :], bank[4][:, :, :], ACT.Copy).then_inc(rel_ready, 1)
                g = t.B1
                if g.real:
                    act.wait_ge(mix_ready, g.upto())
                    if g.past(1): act.wait_ge(x2_ready, g.upto(1))
                    act.activation(elu_neg[:, :, :], mix[:, :, :], ACT.Exp).then_inc(elu_exp_ready, 1)
                g = t.A2
                if g.real:
                    act.wait_ge(conv_summed, g.upto())
                    act.activation(x_conv[:, :, :], conv_sum[:, :, :], ACT.Relu,
                                   bias=bn_bias[:, 1:2]).then_inc(x_conv_ready, 1)
                g = t.C
                if g.real:
                    act.wait_ge(rms_wide_done, g.upto())
                    if g.past(1): act.wait_ge(scaled_ready[CHUNKS - 1], g.upto(1))
                    act.activation(rms_wide[:, :, :], bank[0][:, :, :], ACT.Copy).then_inc(rms_wide_ready, 1)
                    for c in range(CHUNKS):
                        act.wait_ge(scaled_ready[c], g.upto())
                        if g.past(1): act.wait_ge(out_done, g.upto(1))
                        act.activation(silu[c][:, :, :], hidden[c][:, :, :], ACT.Tanh,
                                       scale=half_rms[:, c:c + 1]).then_inc(silu_tanh_ready[c], 1)
                g = t.A2
                if g.real:
                    act.wait_ge(r_done, g.upto())
                    if g.past(1): act.wait_ge(gate_r_ready, g.upto(1))
                    act.activation(tanh_r[:, :, :], bank[3][:, :, :], ACT.Tanh, bias=gate_bias[:, 0:1],
                                   scale=0.5).then_inc(tanh_r_ready, 1)
                    act.wait_ge(z_done, g.upto())
                    if g.past(1): act.wait_ge(gate_z_ready, g.upto(1))
                    act.activation(tanh_z[:, :, :], bank[5][:, :, :], ACT.Tanh, bias=gate_bias[:, 1:2],
                                   scale=0.5).then_inc(tanh_z_ready, 1)
                    act.wait_ge(n_summed, g.upto())
                    if g.past(1): act.wait_ge(gru_ready, g.upto(1))
                    act.activation(n_tanh[:, :, :], n_sum[:, :, :], ACT.Tanh, bias=column("ih_n")).then_inc(n_ready, 1)

            turns(act, turn)

        @block.vector
        def _(dve):
            dve.wait_ge(weights_loaded, 64)
            dve.tensor_scalar(bn_var[:, :], column("v1", n=2), LN_EPS, None, ALU.add).then_inc(bn_var_ready, 1)
            dve.tensor_tensor(gate_sum[:, :], column("ih_r", n=2), column("hh_r", n=2), ALU.add).then_inc(dve_setup, 1)
            dve.tensor_scalar(half_rms[:, :], column("w0", n=CHUNKS), 0.5, None, ALU.mult).then_inc(dve_setup, 1)
            dve.tensor_copy(conv2_hi[:, :, :], conv2_raw).then_inc(dve_setup, 1)
            dve.wait_ge(dve_setup, 3)
            dve.tensor_scalar(gate_bias[:, :], gate_sum[:, :], 0.5, None, ALU.mult)
            for c in range(CHUNKS):
                dve.tensor_scalar(w2_half[:, c, :], weight("W2", P, c * P), half_rms[:, c:c + 1], None, ALU.mult)
            dve.tensor_tensor(conv2_lo[:, :, :], conv2_raw,
                              conv2_hi[:, :, :].bitcast(F32), ALU.subtract)
            for tile in (*c1_hi, *c1_lo):
                dve.memset(tile[:, :, 0:1].bitcast(F32), 0.0)
                dve.memset(tile[:, :, P + 1:P + 2].bitcast(F32), 0.0)
            for n in range(2):
                dve.memset(left[n][64:96, :, :], -1.0)
                dve.memset(right[n][32:64, :, :], -1.0)
            dve.wait_ge(constants_ready, 1)
            dve.tensor_scalar(eps_identity[:, :], identity[:, :], column("eps"), None, ALU.mult)
            dve.wait_ge(constants_ready, 2)
            dve.tensor_tensor(bn_scale[:, :], bn_root[:, :], column("g1", n=2), ALU.mult).then_inc(dve_setup, 1)
            dve.wait_ge(dve_setup, 4)
            dve.tensor_tensor(bn_mean[:, :], bn_scale[:, :], column("m1", n=2), ALU.mult).then_inc(dve_setup, 1)
            dve.wait_ge(dve_setup, 5)
            dve.tensor_tensor(bn_bias[:, :], column("b1", n=2), bn_mean[:, :], ALU.subtract).then_inc(prepared, 1)
            dve.wait_ge(prepared, 1)

            def statistics(norm, tile, g):
                for b in range(PER):
                    last = dve.bn_stats(norm.stats[:, b, :], tile[:, b, :])
                last.then_inc(norm.stats_ready, 1)
                dve.wait_ge(norm.stats_ready, g.upto())
                if g.past(1): dve.wait_ge(norm.var_ready, g.upto(1))
                dve.sem_inc(dve_held, 1)
                for b in range(PER):
                    last = dve.bn_aggr(norm.moments[:, b, :], norm.stats[:, b, :])
                last.then_inc(norm.moments_ready, 1)

            def normalise(norm, out, tile, g):
                dve.wait_ge(norm.scale_ready, g.upto())
                for b in range(PER):
                    last = dve.tensor_scalar(out[:, b, :], tile[:, b, :], norm.moments[:, b, 0:1],
                                             norm.scale[:, b:b + 1], ALU.subtract, ALU.mult)
                last.then_inc(norm.normed, 1)

            def turn(t):
                g = t.C
                if g.real:
                    if g.past(1): dve.wait_ge(h3_ready, g.upto(1))
                    normalise(norm3, h3n, x3[g % 2], g)
                g = t.B2
                if g.real:
                    if g.past(1): dve.wait_ge(h2_ready, g.upto(1))
                    normalise(norm2, h2n, x2[g % 2], g)
                g = t.B1
                if g.real:
                    if g.past(1): dve.wait_ge(h1_turned, g.upto(1))
                    normalise(norm1, h1n, x1[g % 2], g)
                g = t.B2
                if g.real:
                    dve.wait_ge(h2_ready, g.upto())
                    statistics(norm2b, h2, g)
                g = t.B1
                if g.real:
                    dve.wait_ge(degree_done, g.upto())
                    if g.past(1): dve.wait_ge(deg_scale_ready, g.upto(1))
                    dve.tensor_scalar(degree[:, :], bank[3][:, 0, 0:PER], DEG_EPS, None, ALU.add).then_inc(degree_ready, 1)
                g = t.A1
                if g.real:
                    dve.wait_ge(c1_ready, g.upto())
                    if g.past(2): dve.wait_ge(conv2_done, g.upto(2))
                    dve.tensor_copy(c1_hi[g % 2][:, :, 1:P + 1], c1[:, :, :]).then_inc(c1_hi_ready, 1)
                    dve.wait_ge(c1_hi_ready, g.upto())
                    dve.tensor_tensor(c1_lo[g % 2][:, :, 1:P + 1], c1[:, :, :],
                                      c1_hi[g % 2][:, :, 1:P + 1].bitcast(F32), ALU.subtract).then_inc(c1_lo_ready, 1)
                    dve.wait_ge(se_done, g.upto())
                    if g.past(2): dve.wait_ge(dist_done, g.upto(2))
                    dve.tensor_scalar(left[g % 2][0:32, :, :], bank[7][0:32, :, :], column("se", 32), 2.0,
                                      ALU.add, ALU.mult).then_inc(left_ready, 1)
                    dve.wait_ge(message_done, g.upto())
                    if g.past(1): dve.wait_ge(message_ready, g.upto(1))
                    dve.tensor_tensor(message_sum[:, :, :], bank[0][:, :, :], row("msg"), ALU.add).then_inc(message_summed, 1)
                g = t.B2
                if g.real:
                    if g.past(1): dve.wait_ge(h2_turned, g.upto(1))
                    normalise(norm2b, h2nn, h2, g)
                g = t.B1
                if g.real:
                    dve.wait_ge(theta_done, g.upto())
                    dve.wait_ge(deg_scale_ready, g.upto())
                    if g.past(1): dve.wait_ge(hom_done, g.upto(1))
                    scale = deg_scale[:, :].unsqueeze(2).to_broadcast([P, PER, P])
                    dve.tensor_tensor(f_hom[:, :, :], bank[6][:, :, :], scale, ALU.mult).then_inc(f_hom_ready, 1)
                    dve.wait_ge(gate_done, g.upto())
                    if g.past(1): dve.wait_ge(gate1_ready, g.upto(1))
                    dve.tensor_tensor(gate_sum1[:, :, :], bank[0][:, :, :], row("b_t"), ALU.add).then_inc(gate1_summed, 1)
                    dve.wait_ge(hom_done, g.upto())
                    if g.past(1): dve.wait_ge(gated_ready, g.upto(1))
                    dve.tensor_tensor(hom[:, :, :], bank[5][:, :, :], scale, ALU.mult).then_inc(hom_ready, 1)
                    dve.wait_ge(hom_ready, g.upto())
                    dve.wait_ge(f_het_ready, g.upto())
                    dve.tensor_tensor(hom[:, :, :], hom[:, :, :], f_het[:, :, :], ALU.subtract).then_inc(difference_ready, 1)
                g = t.C
                if g.real:
                    dve.wait_ge(rms_done, g.upto())
                    if g.past(1): dve.wait_ge(rms_scale_ready, g.upto(1))
                    dve.tensor_scalar(mean_square[:, :], bank[7][:, 0, 0:PER], 1.0 / HID, RMS_EPS,
                                      ALU.mult, ALU.add).then_inc(mean_square_ready, 1)
                g = t.B1
                if g.real:
                    dve.wait_ge(gate1_ready, g.upto())
                    dve.wait_ge(difference_ready, g.upto())
                    if g.past(1): dve.wait_ge(elu_exp_ready, g.upto(1))
                    dve.scalar_tensor_tensor(out=mix[:, :, :], in0=gate_tanh[:, :, :], scalar=1.0,
                                             in1=hom[:, :, :], op0=ALU.add, op1=ALU.mult).then_inc(gated_ready, 1)
                    dve.wait_ge(gated_ready, g.upto())
                    dve.scalar_tensor_tensor(out=mix[:, :, :], in0=mix[:, :, :], scalar=0.5,
                                             in1=f_het[:, :, :], op0=ALU.mult, op1=ALU.add).then_inc(mix_ready, 1)
                    dve.wait_ge(mix_ready, g.upto())
                    dve.scalar_tensor_tensor(out=elu_pos[:, :, :], in0=mix[:, :, :], scalar=0.0,
                                             in1=x1[g % 2][:, :, :], op0=ALU.max, op1=ALU.add).then_inc(elu_pos_ready, 1)
                g = t.B2
                if g.real:
                    dve.wait_ge(conv_rel_done, g.upto())
                    dve.tensor_tensor(conv_rel[:, :, :], bank[6][:, :, :], row("rel"), ALU.add).then_inc(conv_rel_ready, 1)
                    dve.wait_ge(conv_rel_ready, g.upto())
                    dve.wait_ge(x2_h2_ready, g.upto())
                    if g.past(2): dve.wait_ge(x3_b2_ready, g.upto(2))
                    dve.scalar_tensor_tensor(out=x3[g % 2][:, :, :], in0=conv_rel[:, :, :], scalar=0.0,
                                             in1=x2_h2[:, :, :], op0=ALU.max, op1=ALU.add).then_inc(x3_ready, 1)
                    dve.wait_ge(x3_ready, g.upto())
                    statistics(norm3, x3[g % 2], g)
                g = t.B1
                if g.real:
                    dve.wait_ge(elu_neg_ready, g.upto())
                    dve.wait_ge(elu_pos_ready, g.upto())
                    if g.past(2): dve.wait_ge(x2_h2_ready, g.upto(2))
                    dve.tensor_tensor(x2[g % 2][:, :, :], elu_pos[:, :, :], elu_neg[:, :, :], ALU.add).then_inc(x2_ready, 1)
                    dve.wait_ge(x2_ready, g.upto())
                    statistics(norm2, x2[g % 2], g)
                g = t.N
                if g.real:
                    dve.wait_ge(x_loaded[g % 4], g.transfers(4))
                    statistics(norm0, x_in[g % 4], g)
                g = t.C
                if g.real:
                    dve.wait_ge(rms_scale_ready, g.upto())
                    if g.past(1): dve.wait_ge(rms_wide_done, g.upto(1))
                    for b in range(PER):
                        last = dve.tensor_scalar(rms_diag[:, b, :], identity[:, :], rms_scale[:, b:b + 1], None, ALU.mult)
                    last.then_inc(rms_diag_ready, 1)
                g = t.A2
                if g.real:
                    dve.wait_ge(conv2_done, g.upto())
                    if g.past(1): dve.wait_ge(x_conv_ready, g.upto(1))
                    dve.scalar_tensor_tensor(out=conv_sum[:, :, :], in0=bank[2][:, :, :], scalar=bn_scale[:, 1:2],
                                             in1=h0[g % 2][:, :, :], op0=ALU.mult, op1=ALU.add).then_inc(conv_summed, 1)
                g = t.C
                if g.real:
                    dve.wait_ge(rms_wide_ready, g.upto())
                    for c in range(CHUNKS):
                        dve.tensor_tensor(hidden[c][:, :, :], hidden[c][:, :, :], rms_wide[:, :, :], ALU.mult).then_inc(scaled_ready[c], 1)
                    for c in range(CHUNKS):
                        dve.wait_ge(silu_tanh_ready[c], g.upto())
                        dve.scalar_tensor_tensor(out=silu[c][:, :, :], in0=silu[c][:, :, :], scalar=1.0,
                                                 in1=hidden[c][:, :, :], op0=ALU.add, op1=ALU.mult).then_inc(silu_ready[c], 1)
                g = t.N
                if g.real:
                    if g.past(2): dve.wait_ge(h0_turned, g.upto(2))
                    normalise(norm0, h0n[g % 2], x_in[g % 4], g)
                g = t.A2
                if g.real:
                    dve.wait_ge(gate_r_ready, g.upto())
                    dve.scalar_tensor_tensor(out=r_hidden[:, :, :], in0=bank[1][:, :, :], scalar=column("hh_n"),
                                             in1=gate_r[:, :, :], op0=ALU.add, op1=ALU.mult).then_inc(r_hidden_ready, 1)
                    dve.wait_ge(r_hidden_ready, g.upto())
                    dve.wait_ge(input_n_done, g.upto())
                    if g.past(1): dve.wait_ge(n_ready, g.upto(1))
                    dve.tensor_tensor(n_sum[:, :, :], r_hidden[:, :, :], bank[4][:, :, :], ALU.add).then_inc(n_summed, 1)
                    dve.wait_ge(h_less_n_ready, g.upto())
                    dve.wait_ge(gate_z_ready, g.upto())
                    if g.past(1): dve.wait_ge(gru_turned, g.upto(1))
                    dve.tensor_tensor(gru[:, :, :], gate_z[:, :, :], h_less_n[:, :, :], ALU.mult).then_inc(z_part_ready, 1)
                    dve.wait_ge(z_part_ready, g.upto())
                    dve.tensor_tensor(gru[:, :, :], gru[:, :, :], n_tanh[:, :, :], ALU.add).then_inc(gru_ready, 1)
                g = t.C
                if g.real:
                    dve.wait_ge(out_done, g.upto())
                    dve.wait_ge(x3_b2_ready, g.upto())
                    if g.past(2): dve.wait_ge(stored[g % 2], g.transfers(2, 2))
                    dve.tensor_tensor(result[g % 2][:, :, :], bank[6][:, :, :], x3_b2[:, :, :], ALU.add).then_inc(result_ready, 1)
                g = t.A2
                if g.real:
                    dve.wait_ge(gru_turned, g.upto())
                    if g.past(2): dve.wait_ge(elu_pos_ready, g.upto(2))
                    dve.tensor_tensor(x1[g % 2][:, :, :], bank[7][:, :, :], x_in[g % 4][:, :, :], ALU.add).then_inc(x1_ready, 1)
                    dve.wait_ge(x1_ready, g.upto())
                    statistics(norm1, x1[g % 2], g)

            turns(dve, turn)

        @block.gpsimd
        def _(pool):
            pool.memset(identity[:, :], 0.0).then_inc(identity_blank, 1)
            pool.memset(ones[:, :], 1.0)
            pool.memset(minus_half[:, :], -0.5).then_inc(identity_blank, 1)
            pool.wait_ge(identity_blank, 1)
            pool.affine_select(out=identity[:, :], in_=identity[:, :], compare_op=ALU.not_equal, fill=1.0, base=0,
                               pattern=[[-1, P]], channel_multiplier=1).then_inc(constants_ready, 1)
            pool.wait_ge(identity_blank, 2)
            pool.wait_ge(bn_var_ready, 1)
            pool.tensor_tensor(bn_root[:, :], bn_var[:, :], minus_half[:, 0:2], ALU.pow).then_inc(constants_ready, 1)
            pool.wait_ge(prepared, 1)

            def inverse_deviation(norm, g):
                pool.wait_ge(norm.moments_ready, g.upto())
                if g.past(1): pool.wait_ge(norm.scale_ready, g.upto(1))
                pool.sem_inc(pool_held, 1)
                pool.tensor_scalar(norm.var[:, :], norm.moments[:, :, 1], LN_EPS, None, ALU.add).then_inc(norm.var_ready, 1)
                pool.wait_ge(norm.var_ready, g.upto())
                if g.past(1): pool.wait_ge(norm.normed, g.upto(1))
                pool.tensor_tensor(norm.scale[:, :], norm.var[:, :], minus_half[:, :], ALU.pow).then_inc(norm.scale_ready, 1)

            def turn(t):
                g = t.C
                if g.real:
                    pool.wait_ge(adj_loaded[g % 4], g.transfers(4))
                    if g.past(1): pool.wait_ge(agg_done, g.upto(1))
                    pool.tensor_tensor(adj_eps[:, :, :], adj[g % 4][:, :, :],
                                       eps_identity[:, :].unsqueeze(1).to_broadcast([P, PER, P]), ALU.add).then_inc(adj_eps_ready, 1)
                g = t.B2
                if g.real:
                    inverse_deviation(norm2b, g)
                g = t.B1
                if g.real:
                    pool.wait_ge(degree_ready, g.upto())
                    if g.past(1): pool.wait_ge(hom_ready, g.upto(1))
                    pool.tensor_tensor(deg_scale[:, :], degree[:, :], minus_half[:, :], ALU.pow).then_inc(deg_scale_ready, 1)
                g = t.A2
                if g.real:
                    pool.wait_ge(adj_loaded[g % 4], g.transfers(4))
                    pool.wait_ge(affinity_ready, g.upto())
                    if g.past(1): pool.wait_ge(nmp_done, g.upto(1))
                    pool.tensor_tensor(masked[:, :, :], affinity[:, :, :], adj[g % 4][:, :, :], ALU.mult).then_inc(masked_ready, 1)
                g = t.C
                if g.real:
                    for k in range(2):
                        pool.wait_ge(square_ready[2 * k], g.upto())
                        pool.wait_ge(square_ready[2 * k + 1], g.upto())
                        pool.tensor_tensor(square[2 * k][:, :, :], square[2 * k][:, :, :], square[2 * k + 1][:, :, :],
                                           ALU.add).then_inc(square_summed[k], 1)
                g = t.B2
                if g.real:
                    pool.wait_ge(h2_ready, g.upto())
                    if g.past(1): pool.wait_ge(x3_ready, g.upto(1))
                    pool.tensor_tensor(x2_h2[:, :, :], x2[g % 2][:, :, :], h2[:, :, :], ALU.add).then_inc(x2_h2_ready, 1)
                g = t.C
                if g.real:
                    pool.wait_ge(mean_square_ready, g.upto())
                    if g.past(1): pool.wait_ge(rms_diag_ready, g.upto(1))
                    pool.tensor_tensor(rms_scale[:, :], mean_square[:, :], minus_half[:, :], ALU.pow).then_inc(rms_scale_ready, 1)
                g = t.B1
                if g.real:
                    pool.wait_ge(elu_exp_ready, g.upto())
                    pool.sem_inc(pool_held, 1)
                    pool.tensor_scalar(elu_neg[:, :, :], elu_neg[:, :, :], 1.0, -1.0, ALU.min, ALU.add).then_inc(elu_neg_ready, 1)
                g = t.B2
                if g.real:
                    inverse_deviation(norm3, g)
                g = t.B1
                if g.real:
                    inverse_deviation(norm2, g)
                g = t.N
                if g.real:
                    inverse_deviation(norm0, g)
                g = t.C
                if g.real:
                    if g.past(1): pool.wait_ge(result_ready, g.upto(1))
                    pool.tensor_tensor(x3_b2[:, :, :], x3[g % 2][:, :, :], row("out"), ALU.add).then_inc(x3_b2_ready, 1)
                g = t.A2
                if g.real:
                    pool.wait_ge(tanh_r_ready, g.upto())
                    if g.past(1): pool.wait_ge(r_hidden_ready, g.upto(1))
                    pool.sem_inc(pool_held, 1)
                    pool.tensor_scalar(gate_r[:, :, :], tanh_r[:, :, :], 0.5, 0.5, ALU.mult, ALU.add).then_inc(gate_r_ready, 1)
                    pool.wait_ge(tanh_z_ready, g.upto())
                    if g.past(1): pool.wait_ge(z_part_ready, g.upto(1))
                    pool.sem_inc(pool_held, 1)
                    pool.tensor_scalar(gate_z[:, :, :], tanh_z[:, :, :], 0.5, 0.5, ALU.mult, ALU.add).then_inc(gate_z_ready, 1)
                    pool.wait_ge(n_ready, g.upto())
                    pool.tensor_tensor(h_less_n[:, :, :], h0[g % 2][:, :, :], n_tanh[:, :, :], ALU.subtract).then_inc(h_less_n_ready, 1)
                    inverse_deviation(norm1, g)

            turns(pool, turn)


def kernel(**inputs):
    import numpy as np
    import concourse.bacc as bacc
    from concourse.bass_utils import run_bass_kernel_spmd

    a = {name: np.asarray(value) for name, value in inputs.items()}
    L0 = {name[7:]: value for name, value in a.items() if name.startswith("L0_gnn_")}

    x = a["x"].reshape(GROUPS, PER, P, P).transpose(2, 0, 1, 3)
    adj = a["adj"].reshape(GROUPS, PER, P, P).transpose(3, 0, 1, 2)
    se = np.zeros((P, 96), np.float32)
    b_se = np.zeros(P, np.float32)
    for n in range(3):
        se[:, 32 * n:32 * n + 3] = L0["w_se"].T
        b_se[32 * n:32 * n + 3] = L0["b_se"]
    w_ih = L0["w_ih"].T.reshape(2, P, 3 * P).transpose(1, 0, 2).reshape(P, -1)
    W2 = a["L3_gnn_W2"].reshape(CHUNKS, P, P).transpose(1, 0, 2).reshape(P, -1)
    weights = np.concatenate([
        L0["conv1_w"][:, :, 0].T, se, L0["w_msg"].T, w_ih, L0["w_hh"].T,
        a["L1_gnn_theta"], a["L1_gnn_W_h"], a["L1_gnn_W_t"], a["L2_gnn_W_rel"], a["L2_gnn_W_root"], a["L3_gnn_W1"], W2], 1)
    columns = np.stack([
        L0["bn1_g"], L0["bn2_g"], L0["bn1_b"], L0["bn2_b"], L0["bn1_m"], L0["bn2_m"], L0["bn1_v"], L0["bn2_v"],
        *L0["b_ih"].reshape(3, P), *L0["b_hh"].reshape(3, P), b_se, a["L2_gnn_ln_gamma"], a["L2_gnn_ln_beta"],
        np.broadcast_to(a["L3_gnn_epsilon"], (P,)), *a["L3_gnn_b1"].reshape(CHUNKS, P),
        *a["L3_gnn_rms_weight"].reshape(CHUNKS, P)], 1)
    rows = np.stack([L0["b_msg"], a["L1_gnn_b_t"], a["L2_gnn_b_rel"], a["L3_gnn_b2"]])

    nc = bacc.Bacc("TRN2", target_bir_lowering=False, num_devices=1)
    arrays, args = {}, []
    for name, value in (("x", x), ("adj", adj), ("weights", weights), ("conv2", L0["conv2_w"].transpose(1, 2, 0)), ("columns", columns), ("rows", rows)):
        value = np.ascontiguousarray(value)
        arrays[f"in_{name}_dram"] = value
        args.append(nc.dram_tensor(f"in_{name}_dram", value.shape, mybir.dt.from_np(value.dtype), kind="ExternalInput").ap())
    args.append(nc.dram_tensor("out_dram", (P, GROUPS, PER, P), F32, kind="ExternalOutput").ap())
    graph_layers(nc, *args)
    r = run_bass_kernel_spmd(nc, [arrays], core_ids=[0])
    out = r.results[0]["out_dram"]
    return out.transpose(1, 2, 0, 3).reshape(GRAPHS, P, P)
```

```python
from contextlib import ExitStack

import concourse.bass as bass
from concourse import mybir

ALU = mybir.AluOpType
ACT = mybir.ActivationFunctionType
F32 = mybir.dt.float32
F32R = mybir.dt.float32r

P = 128
GRAPHS = 128
PER = 4
GROUPS = GRAPHS // PER
TAPS = 17
HID = 512
CHUNKS = HID // P
LAG = {"N": 0, "A1": 1, "A2": 2, "B1": 3, "B2": 4, "C": 5}
TURNS = GROUPS + LAG["C"]
UNROLL = 4
LOOP_FROM, LOOP_TO = 8, GROUPS
LN_EPS = 1e-5
RMS_EPS = 1e-6
DEG_EPS = 1e-6
INF = float("inf")

def places(widths):
    at, total = {}, 0
    for name, width in widths:
        at[name] = total
        total += width
    return at, total


WHOLE, WHOLE_WIDE = places([("msg", P), ("theta", P), ("W_h", P), ("W_t", P), ("rel", P), ("root", P),
                            ("W2", CHUNKS * P)])
SPLIT, SPLIT_WIDE = places([("conv2", TAPS * P), ("conv1", P), ("se", 96), ("ih", 2 * 3 * P), ("hh", 3 * P),
                            ("W1", HID)])
COLUMN = {name: n for n, name in enumerate(
    ["g1", "g2", "b1", "b2", "m1", "m2", "v1", "v2", "ih_r", "ih_z", "ih_n", "hh_r", "hh_z", "hh_n",
     "se", "gamma", "beta", "eps", "h0", "h1", "h2", "h3", "w0", "w1", "w2", "w3"])}
ROW = {"msg": 0, "b_t": 1, "rel": 2, "out": 3}
OFFSETS = sorted(range(-(TAPS // 2), TAPS // 2 + 1), key=abs)


class Group:

    def __init__(self, loop, n):
        self.loop, self.n = loop, n
        self.real = loop is not None or 0 <= n < GROUPS

    def at(self):
        return self.n if self.loop is None else self.loop.first + self.n

    def __mod__(self, places):
        return self.n % places

    def past(self, back):
        return self.loop is not None or self.n >= back

    def upto(self, back=0):
        count = self.n - back + 1
        return min(count, GROUPS) if self.loop is None else self.loop.plus[count]

    def transfers(self, places, back=0):
        count = 16 * ((self.n - back) // places + 1)
        return count if self.loop is None else self.loop.first * (16 // places) + count


class Loop:

    def __init__(self, engine, first):
        self.first = first
        self.plus = {n: engine.snap(first + n) for n in range(-LAG["C"] - 1, UNROLL + 1)}


class Turn:

    def __init__(self, loop, t):
        self.N, self.A1, self.A2, self.B1, self.B2, self.C = (Group(loop, t - LAG[s]) for s in LAG)
        self.next_adj = Group(loop, t - LAG["A2"] + 1)


def turns(engine, turn):
    for t in range(LOOP_FROM):
        turn(Turn(None, t))
    with engine.Fori(0, (LOOP_TO - LOOP_FROM) // UNROLL, 1) as body:
        loop = Loop(engine, engine.snap(body * UNROLL + LOOP_FROM))
        for t in range(UNROLL):
            turn(Turn(loop, t))
    for t in range(LOOP_TO, TURNS):
        turn(Turn(None, t))


def graph_layers(nc, d_x, d_adj, d_weights, d_split, d_columns, d_rows, d_out):
    with ExitStack() as ctx:
        def sb(name, shape, dtype=F32):
            return ctx.enter_context(nc.sbuf_tensor(name, shape, dtype))

        def signal(name):
            return ctx.enter_context(nc.semaphore(name))

        def ring(name, places, shape=(P, PER, P), dtype=F32):
            return [sb(f"{name}_{n}", list(shape), dtype) for n in range(places)]

        def signals(name, n):
            return [signal(f"{name}_{k}") for k in range(n)]

        weights = sb("weights", [P, WHOLE_WIDE])
        weights_hi = sb("weights_hi", [P, SPLIT_WIDE], F32R)
        weights_lo = sb("weights_lo", [P, SPLIT_WIDE], F32R)
        columns = sb("columns", [P, len(COLUMN)])
        rows = sb("rows", [P, len(ROW), P])
        identity = sb("identity", [P, P])
        eps_identity = sb("eps_identity", [P, P])
        ones = sb("ones", [P, P])
        minus_half = sb("minus_half", [P, PER])
        bn_var = sb("bn_var", [P, 2])
        bn_root = sb("bn_root", [P, 2])
        bn_scale = sb("bn_scale", [P, 2])
        bn_mean = sb("bn_mean", [P, 2])
        bn_bias = sb("bn_bias", [P, 2])
        gate_sum = sb("gate_sum", [P, 2])
        gate_bias = sb("gate_bias", [P, 2])
        half_rms = sb("half_rms", [P, CHUNKS])
        w2_half = sb("w2_half", [P, CHUNKS, P])

        def weight(name, width=P, skip=0):
            return weights[:, WHOLE[name] + skip:WHOLE[name] + skip + width]

        def column(name, parts=P, first=0, n=1):
            return columns[first:first + parts, COLUMN[name]:COLUMN[name] + n]

        def row(name):
            return rows[:, ROW[name], :].unsqueeze(1).to_broadcast([P, PER, P])

        x_in = ring("x_in", 4)
        adj = ring("adj", 4)
        h0n = ring("h0n", 2)
        h0 = ring("h0", 2)
        h0_hi = ring("h0_hi", 2, dtype=F32R)
        h0_lo = ring("h0_lo", 2, dtype=F32R)
        c1_hi = ring("c1_hi", 2, (P, PER, P + 2), F32R)
        c1_lo = ring("c1_lo", 2, (P, PER, P + 2), F32R)
        left = ring("left", 2, (96, PER, P))
        right = ring("right", 2, (96, PER, P))
        message = ring("message", 2)
        x1 = ring("x1", 2)
        x2 = ring("x2", 2)
        x3 = ring("x3", 2)
        result = ring("result", 2)
        c1 = sb("c1", [P, PER, P])
        masked = sb("masked", [P, PER, P])
        nmp_hi = sb("nmp_hi", [P, PER, P], F32R)
        nmp_lo = sb("nmp_lo", [P, PER, P], F32R)
        conv_sum = sb("conv_sum", [P, PER, P])
        x_conv_hi = sb("x_conv_hi", [P, PER, P], F32R)
        x_conv_lo = sb("x_conv_lo", [P, PER, P], F32R)
        candidate = sb("candidate", [P, PER, P])
        gate_z = sb("gate_z", [P, PER, P])
        h_less_n = sb("h_less_n", [P, PER, P])
        gru = sb("gru", [P, PER, P])
        h1n = sb("h1n", [P, PER, P])
        h1 = sb("h1", [P, PER, P])
        degree = sb("degree", [P, PER])
        deg_scale = sb("deg_scale", [P, PER])
        f_hom = sb("f_hom", [P, PER, P])
        f_het = sb("f_het", [P, PER, P])
        gate_tanh = sb("gate_tanh", [P, PER, P])
        hom = sb("hom", [P, PER, P])
        mix = sb("mix", [P, PER, P])
        elu_pos = sb("elu_pos", [P, PER, P])
        elu_neg = sb("elu_neg", [P, PER, P])
        h2 = sb("h2", [P, PER, P])
        h2nn = sb("h2nn", [P, PER, P])
        h2_col = sb("h2_col", [P, PER, P])
        rel = sb("rel", [P, PER, P])
        x2_h2 = sb("x2_h2", [P, PER, P])
        conv_rel = sb("conv_rel", [P, PER, P])
        h3 = sb("h3", [P, PER, P])
        adj_eps = sb("adj_eps", [P, PER, P])
        agg_hi = sb("agg_hi", [P, PER, P], F32R)
        agg_lo = sb("agg_lo", [P, PER, P], F32R)
        perceptron = sb("perceptron", [P, 2 * CHUNKS * PER * P])
        weights_raw = perceptron[:, 0:SPLIT_WIDE]
        halves = perceptron[:, :].rearrange("p (k b n) -> p k b n", k=2 * CHUNKS, b=PER)
        square = [halves[:, c, :, :] for c in range(CHUNKS)]
        hidden = [halves[:, CHUNKS + c, :, :] for c in range(CHUNKS)]
        mean_square = sb("mean_square", [P, PER])
        rms_scale = sb("rms_scale", [P, PER])
        rms_diag = sb("rms_diag", [P, PER, P])
        rms_wide = sb("rms_wide", [P, PER, P])
        silu = ring("silu", CHUNKS)
        x3_b2 = sb("x3_b2", [P, PER, P])

        bank = [ctx.enter_context(nc.psum_tensor(f"bank_{n}", [P, PER, P], F32)) for n in range(8)]

        weights_loaded = signal("weights_loaded")
        identity_blank = signal("identity_blank")
        constants_ready = signal("constants_ready")
        bn_var_ready = signal("bn_var_ready")
        dve_setup = signal("dve_setup")
        dve_held, pool_held = signal("dve_held"), signal("pool_held")
        prepared = signal("prepared")
        x_loaded = signals("x_loaded", 4)
        adj_loaded = signals("adj_loaded", 4)
        stored = signals("stored", 2)

        class Norm:

            def __init__(self, name):
                self.stats = sb(f"{name}_stats", [P, PER, 6])
                self.moments = sb(f"{name}_moments", [P, PER, 2])
                self.var = sb(f"{name}_var", [P, PER])
                self.scale = sb(f"{name}_scale", [P, PER])
                self.stats_ready = signal(f"{name}_stats_ready")
                self.moments_ready = signal(f"{name}_moments_ready")
                self.var_ready = signal(f"{name}_var_ready")
                self.scale_ready = signal(f"{name}_scale_ready")
                self.normed = signal(f"{name}_normed")

        norm0, norm1, norm2, norm2b, norm3 = (Norm(f"norm{n}") for n in ("0", "1", "2", "2b", "3"))

        h0_turned, h0_ready, h0_hi_ready, h0_lo_ready = signal("h0_turned"), signal("h0_ready"), signal("h0_hi_ready"), signal("h0_lo_ready")
        conv1_done, c1_ready = signal("conv1_done"), signal("c1_ready")
        c1_hi_ready, c1_lo_ready = signal("c1_hi_ready"), signal("c1_lo_ready")
        se_done, left_ready, right_ready = signal("se_done"), signal("left_ready"), signal("right_ready")
        message_done, message_summed, message_ready = signal("message_done"), signal("message_summed"), signal("message_ready")
        dist_done, affinity_ready, masked_ready = signal("dist_done"), signal("affinity_ready"), signal("masked_ready")
        nmp_done, nmp_hi_ready, nmp_lo_ready = signal("nmp_done"), signal("nmp_hi_ready"), signal("nmp_lo_ready")
        x_conv_hi_ready, x_conv_lo_ready = signal("x_conv_hi_ready"), signal("x_conv_lo_ready")
        conv2_done, conv_summed, x_conv_ready = signal("conv2_done"), signal("conv_summed"), signal("x_conv_ready")
        hidden_n_done, r_done, z_done, input_n_done = signal("hidden_n_done"), signal("r_done"), signal("z_done"), signal("input_n_done")
        tanh_r_ready, gate_r_ready, tanh_z_ready, gate_z_ready = signal("tanh_r_ready"), signal("gate_r_ready"), signal("tanh_z_ready"), signal("gate_z_ready")
        r_hidden_ready, n_summed, n_ready = signal("r_hidden_ready"), signal("n_summed"), signal("n_ready")
        h_less_n_ready, z_part_ready, gru_ready = signal("h_less_n_ready"), signal("z_part_ready"), signal("gru_ready")
        gru_turned, x1_ready = signal("gru_turned"), signal("x1_ready")
        degree_done, degree_ready, deg_scale_ready = signal("degree_done"), signal("degree_ready"), signal("deg_scale_ready")
        h1_turned, h1_ready = signal("h1_turned"), signal("h1_ready")
        theta_done, het_done, gate_done = signal("theta_done"), signal("het_done"), signal("gate_done")
        f_hom_ready, f_het_ready, gate1_summed, gate1_ready = signal("f_hom_ready"), signal("f_het_ready"), signal("gate1_summed"), signal("gate1_ready")
        hom_done, hom_ready, difference_ready, gated_ready, mix_ready = signal("hom_done"), signal("hom_ready"), signal("difference_ready"), signal("gated_ready"), signal("mix_ready")
        elu_pos_ready, elu_exp_ready, elu_neg_ready, x2_ready = signal("elu_pos_ready"), signal("elu_exp_ready"), signal("elu_neg_ready"), signal("x2_ready")
        h2_ready, h2_turned, h2_col_ready = signal("h2_ready"), signal("h2_turned"), signal("h2_col_ready")
        rel_done, rel_ready, conv_rel_done = signal("rel_done"), signal("rel_ready"), signal("conv_rel_done")
        x2_h2_ready, conv_rel_ready, x3_ready = signal("x2_h2_ready"), signal("conv_rel_ready"), signal("x3_ready")
        h3_ready, adj_eps_ready, agg_done = signal("h3_ready"), signal("adj_eps_ready"), signal("agg_done")
        agg_hi_ready, agg_lo_ready = signal("agg_hi_ready"), signal("agg_lo_ready")
        hidden_done, square_ready, hidden_ready = signals("hidden_done", CHUNKS), signals("square_ready", CHUNKS), signals("hidden_ready", CHUNKS)
        square_summed, rms_done, mean_square_ready, rms_scale_ready = signals("square_summed", 3), signal("rms_done"), signal("mean_square_ready"), signal("rms_scale_ready")
        rms_diag_ready, rms_wide_done, rms_wide_ready = signal("rms_diag_ready"), signal("rms_wide_done"), signal("rms_wide_ready")
        scaled_ready, silu_tanh_ready, silu_ready = signals("scaled_ready", CHUNKS), signals("silu_tanh_ready", CHUNKS), signals("silu_ready", CHUNKS)
        x3_b2_ready, out_done, result_ready = signal("x3_b2_ready"), signal("out_done"), signal("result_ready")

        block = ctx.enter_context(nc.Block())

        @block.sync
        def _(sp):
            sp.dma_start(columns[:, :], d_columns).then_inc(weights_loaded, 16)
            sp.dma_start(weights[:, :], d_weights).then_inc(weights_loaded, 16)
            sp.dma_start(weights_raw, d_split).then_inc(weights_loaded, 16)
            sp.dma_start(rows[:, :, :], d_rows.partition_broadcast(P)).then_inc(weights_loaded, 16)

            def turn(t):
                if t.N.real:
                    if t.N.past(4): sp.wait_ge(x1_ready, t.N.upto(4))
                    sp.dma_start(x_in[t.N % 4][:, :, :],
                                 d_x[:, t.N.at(), :, :]).then_inc(x_loaded[t.N % 4], 16)
                if t.next_adj.real:
                    if t.next_adj.past(4): sp.wait_ge(conv_rel_done, t.next_adj.upto(4))
                    if t.next_adj.past(4): sp.wait_ge(adj_eps_ready, t.next_adj.upto(4))
                    sp.dma_start(adj[t.next_adj % 4][:, :, :],
                                 d_adj[:, t.next_adj.at(), :, :]).then_inc(adj_loaded[t.next_adj % 4], 16)
                if t.C.real:
                    if t.C.past(0): sp.wait_ge(result_ready, t.C.upto())
                    sp.dma_start(d_out[:, t.C.at(), :, :],
                                 result[t.C % 2][:, :, :]).then_inc(stored[t.C % 2], 16)

            turns(sp, turn)
            for done in stored:
                sp.wait_ge(done, 16 * (GROUPS // 2))

        @block.tensor
        def _(pe):
            pe.wait_ge(prepared, 1)

            def per_graph(out, lhs, rhs, start=True, stop=True):
                for b in range(PER):
                    last = pe.matmul(out[:, b, :], lhs(b), rhs(b), start=start and b == 0, stop=stop,
                                     skip_group_check=True)
                return last

            def turned(out, tile):
                for b in range(PER):
                    last = pe.transpose(out[:, b, :], tile[:, b, :], identity[:, :])
                return last

            def split_product(out, name, skip, hi, lo, start=True, stop=True, width=P):
                a = SPLIT[name] + skip
                pe.matmul(out, weights_hi[:, a:a + width], hi, start=start, stop=False, skip_group_check=True)
                pe.matmul(out, weights_hi[:, a:a + width], lo, start=False, stop=False, skip_group_check=True)
                return pe.matmul(out, weights_lo[:, a:a + width], hi, start=False, stop=stop, skip_group_check=True)

            def conv2(g, taps):
                for k in taps:
                    off = OFFSETS[k]
                    a = max(0, -off) // 2 * 2
                    n = P - a if off <= 0 else (P - off + 1) // 2 * 2
                    nodes = slice(1 + a + off, 1 + a + off + n)
                    last = split_product(bank[2][:, :, a:a + n], "conv2", (off + TAPS // 2) * P, c1_hi[g % 2][:, :, nodes],
                                         c1_lo[g % 2][:, :, nodes], start=(k == 0), stop=(k == TAPS - 1))
                return last

            def turn(t):
                g = t.A2
                if g.real:
                    pe.wait_ge(c1_hi_ready, g.upto())
                    pe.wait_ge(c1_lo_ready, g.upto())
                    if g.past(1): pe.wait_ge(conv_summed, g.upto(1))
                    conv2(g, range(0, 2))
                g = t.A1
                if g.real:
                    pe.wait_ge(norm0.normed, g.upto())
                    if t.A2.past(1): pe.wait_ge(r_hidden_ready, t.A2.upto(1))
                    if g.past(1): pe.wait_ge(h0_hi_ready, g.upto(1))
                    turned(bank[5], h0n[g % 2]).then_inc(h0_turned, 1)
                g = t.A2
                if g.real:
                    conv2(g, range(2, 3))
                    pe.wait_ge(left_ready, g.upto())
                    pe.wait_ge(right_ready, g.upto())
                    if t.C.past(1): pe.wait_ge(mean_square_ready, t.C.upto(1))
                    if t.B1.past(1): pe.wait_ge(f_het_ready, t.B1.upto(1))
                    if g.past(1): pe.wait_ge(affinity_ready, g.upto(1))
                    per_graph(bank[1], lambda b: left[g % 2][:, b, :], lambda b: right[g % 2][:, b, :]).then_inc(dist_done, 1)
                    conv2(g, range(3, 4))
                g = t.B1
                if g.real:
                    pe.wait_ge(adj_loaded[g % 4], g.transfers(4))
                    if t.A2.past(1): pe.wait_ge(tanh_z_ready, t.A2.upto(1))
                    for b in range(PER):
                        last = pe.matmul(bank[6][:, 0, b:b + 1], adj[g % 4][:, b, :], ones[:, 0:1],
                                         start=True, stop=True, skip_group_check=True)
                    last.then_inc(degree_done, 1)
                g = t.A2
                if g.real:
                    conv2(g, range(4, 5))
                g = t.B1
                if g.real:
                    pe.wait_ge(gru_ready, g.upto())
                    if t.A2.past(1): pe.wait_ge(n_summed, t.A2.upto(1))
                    turned(bank[7], gru).then_inc(gru_turned, 1)
                g = t.A2
                if g.real:
                    conv2(g, range(5, 7))
                g = t.A1
                if g.real:
                    pe.wait_ge(h0_ready, g.upto())
                    if t.A2.past(1): pe.wait_ge(tanh_r_ready, t.A2.upto(1))
                    if g.past(1): pe.wait_ge(message_summed, g.upto(1))
                    per_graph(bank[0], lambda b: h0[g % 2][:, b, :], lambda b: weight("msg")).then_inc(message_done, 1)
                g = t.C
                if g.real:
                    pe.wait_ge(h3_ready, g.upto())
                    pe.wait_ge(adj_eps_ready, g.upto())
                    if t.B1.past(0): pe.wait_ge(x1_ready, t.B1.upto())
                    if t.B2.past(1): pe.wait_ge(rel_ready, t.B2.upto(1))
                    per_graph(bank[7], lambda b: h3[:, b, :], lambda b: adj_eps[:, b, :]).then_inc(agg_done, 1)
                g = t.A2
                if g.real:
                    conv2(g, range(7, 8))
                g = t.A1
                if g.real:
                    pe.wait_ge(h0_hi_ready, g.upto())
                    pe.wait_ge(h0_lo_ready, g.upto())
                    if t.B1.past(0): pe.wait_ge(degree_ready, t.B1.upto())
                    if g.past(1): pe.wait_ge(c1_ready, g.upto(1))
                    split_product(bank[6][:, :, :], "conv1", 0, h0_hi[g % 2][:, :, :], h0_lo[g % 2][:, :, :]).then_inc(conv1_done, 1)
                g = t.A2
                if g.real:
                    conv2(g, range(8, 9))
                g = t.A1
                if g.real:
                    pe.wait_ge(h0_hi_ready, g.upto())
                    pe.wait_ge(h0_lo_ready, g.upto())
                    if g.past(1): pe.wait_ge(left_ready, g.upto(1))
                    if g.past(1): pe.wait_ge(right_ready, g.upto(1))
                    split_product(bank[3][0:96, :, :], "se", 0, h0_hi[g % 2][:, :, :], h0_lo[g % 2][:, :, :],
                                  width=96).then_inc(se_done, 1)
                g = t.A2
                if g.real:
                    conv2(g, range(9, 10))
                g = t.C
                if g.real:
                    pe.wait_ge(agg_hi_ready, g.upto())
                    pe.wait_ge(agg_lo_ready, g.upto())
                    if t.A1.past(0): pe.wait_ge(message_summed, t.A1.upto())
                    if t.A2.past(1): pe.wait_ge(tanh_r_ready, t.A2.upto(1))
                    if t.B1.past(1): pe.wait_ge(hom_ready, t.B1.upto(1))
                    if g.past(1): pe.wait_ge(hidden_ready[0], g.upto(1))
                    split_product(bank[0][:, :, :], "W1", 0 * P, agg_hi[:, :, :], agg_lo[:, :, :]).then_inc(hidden_done[0], 1)
                    pe.wait_ge(agg_hi_ready, g.upto())
                    pe.wait_ge(agg_lo_ready, g.upto())
                    if g.past(1): pe.wait_ge(result_ready, g.upto(1))
                    if t.B2.past(1): pe.wait_ge(conv_rel_ready, t.B2.upto(1))
                    split_product(bank[4][:, :, :], "W1", 1 * P, agg_hi[:, :, :], agg_lo[:, :, :]).then_inc(hidden_done[1], 1)
                g = t.A2
                if g.real:
                    conv2(g, range(10, 11))
                g = t.C
                if g.real:
                    pe.wait_ge(agg_hi_ready, g.upto())
                    pe.wait_ge(agg_lo_ready, g.upto())
                    if t.A1.past(0): pe.wait_ge(h0_hi_ready, t.A1.upto())
                    if t.A2.past(1): pe.wait_ge(r_hidden_ready, t.A2.upto(1))
                    if g.past(1): pe.wait_ge(rms_wide_ready, g.upto(1))
                    split_product(bank[5][:, :, :], "W1", 2 * P, agg_hi[:, :, :], agg_lo[:, :, :]).then_inc(hidden_done[2], 1)
                g = t.B1
                if g.real:
                    pe.wait_ge(norm1.normed, g.upto())
                    if t.C.past(0): pe.wait_ge(hidden_ready[0], t.C.upto())
                    if t.A1.past(0): pe.wait_ge(message_summed, t.A1.upto())
                    turned(bank[0], h1n).then_inc(h1_turned, 1)
                g = t.C
                if g.real:
                    pe.wait_ge(agg_hi_ready, g.upto())
                    pe.wait_ge(agg_lo_ready, g.upto())
                    if t.A1.past(0): pe.wait_ge(c1_ready, t.A1.upto())
                    if t.B1.past(0): pe.wait_ge(degree_ready, t.B1.upto())
                    if t.B2.past(1): pe.wait_ge(h2_col_ready, t.B2.upto(1))
                    split_product(bank[6][:, :, :], "W1", 3 * P, agg_hi[:, :, :], agg_lo[:, :, :]).then_inc(hidden_done[3], 1)
                g = t.A2
                if g.real:
                    pe.wait_ge(masked_ready, g.upto())
                    pe.wait_ge(message_ready, g.upto())
                    if t.C.past(0): pe.wait_ge(agg_lo_ready, t.C.upto())
                    if t.B1.past(0): pe.wait_ge(x1_ready, t.B1.upto())
                    per_graph(bank[7], lambda b: message[g % 2][:, b, :], lambda b: masked[:, b, :]).then_inc(nmp_done, 1)
                g = t.B1
                if g.real:
                    pe.wait_ge(h1_ready, g.upto())
                    pe.wait_ge(h1_ready, g.upto())
                    per_graph(bank[0], lambda b: h1[:, b, :], lambda b: weight("theta")).then_inc(theta_done, 1)
                g = t.A2
                if g.real:
                    conv2(g, range(11, 12))
                g = t.B1
                if g.real:
                    pe.wait_ge(h1_ready, g.upto())
                    if t.A2.past(0): pe.wait_ge(affinity_ready, t.A2.upto())
                    if t.C.past(1): pe.wait_ge(mean_square_ready, t.C.upto(1))
                    per_graph(bank[1], lambda b: h1[:, b, :], lambda b: weight("W_h")).then_inc(het_done, 1)
                g = t.A2
                if g.real:
                    conv2(g, range(12, 13))
                g = t.B1
                if g.real:
                    pe.wait_ge(h1_ready, g.upto())
                    if t.C.past(0): pe.wait_ge(hidden_ready[1], t.C.upto())
                    if g.past(1): pe.wait_ge(gate1_summed, g.upto(1))
                    per_graph(bank[4], lambda b: h1[:, b, :], lambda b: weight("W_t")).then_inc(gate_done, 1)
                    pe.wait_ge(f_hom_ready, g.upto())
                    pe.wait_ge(f_hom_ready, g.upto())
                    per_graph(bank[0], lambda b: adj[g % 4][:, b, :], lambda b: f_hom[:, b, :]).then_inc(hom_done, 1)
                g = t.A2
                if g.real:
                    conv2(g, range(13, 14))
                g = t.C
                if g.real:
                    pe.wait_ge(square_summed[2], g.upto())
                    if t.B1.past(0): pe.wait_ge(f_het_ready, t.B1.upto())
                    if g.past(1): pe.wait_ge(mean_square_ready, g.upto(1))
                    for b in range(PER):
                        last = pe.matmul(bank[1][:, 0, b:b + 1], square[0][:, b, :], ones[:, 0:1],
                                         start=True, stop=True, skip_group_check=True)
                    last.then_inc(rms_done, 1)
                g = t.A2
                if g.real:
                    conv2(g, range(14, 15))
                g = t.B2
                if g.real:
                    pe.wait_ge(norm2b.normed, g.upto())
                    if t.C.past(0): pe.wait_ge(hidden_ready[3], t.C.upto())
                    if t.A1.past(0): pe.wait_ge(c1_ready, t.A1.upto())
                    turned(bank[6], h2nn).then_inc(h2_turned, 1)
                g = t.A2
                if g.real:
                    conv2(g, range(15, TAPS)).then_inc(conv2_done, 1)
                    if t.B1.past(0): pe.wait_ge(hom_ready, t.B1.upto())
                    if t.A1.past(0): pe.wait_ge(message_summed, t.A1.upto())
                    split_product(bank[0][:, :, :], "hh", 0 * P, h0_hi[g % 2][:, :, :], h0_lo[g % 2][:, :, :], stop=False)
                g = t.C
                if g.real:
                    pe.wait_ge(rms_diag_ready, g.upto())
                    pe.wait_ge(hidden_ready[2], g.upto())
                    pe.matmul(bank[5][:, :, :], ones[:, :], rms_diag[:, :, :],
                              start=True, stop=True).then_inc(rms_wide_done, 1)
                g = t.A2
                if g.real:
                    pe.wait_ge(nmp_hi_ready, g.upto())
                    pe.wait_ge(nmp_lo_ready, g.upto())
                    split_product(bank[0][:, :, :], "ih", 3 * P + 0 * P, nmp_hi[:, :, :], nmp_lo[:, :, :], start=False, stop=False)
                g = t.B2
                if g.real:
                    pe.wait_ge(h2_col_ready, g.upto())
                    if t.A2.past(0): pe.wait_ge(nmp_lo_ready, t.A2.upto())
                    if t.C.past(0): pe.wait_ge(agg_lo_ready, t.C.upto())
                    per_graph(bank[7], lambda b: h2_col[:, b, :], lambda b: weight("rel")).then_inc(rel_done, 1)
                    pe.wait_ge(h2_col_ready, g.upto())
                    if t.B1.past(0): pe.wait_ge(gate1_summed, t.B1.upto())
                    if t.C.past(0): pe.wait_ge(hidden_ready[1], t.C.upto())
                    per_graph(bank[4], lambda b: h2_col[:, b, :], lambda b: weight("root"), stop=False)
                g = t.A2
                if g.real:
                    if t.B2.past(0): pe.wait_ge(h2_col_ready, t.B2.upto())
                    if t.A1.past(0): pe.wait_ge(c1_ready, t.A1.upto())
                    split_product(bank[6][:, :, :], "hh", 1 * P, h0_hi[g % 2][:, :, :], h0_lo[g % 2][:, :, :], stop=False)
                g = t.B2
                if g.real:
                    pe.wait_ge(rel_ready, g.upto())
                    per_graph(bank[4], lambda b: adj[g % 4][:, b, :], lambda b: rel[:, b, :], start=False).then_inc(conv_rel_done, 1)
                g = t.A2
                if g.real:
                    pe.wait_ge(nmp_hi_ready, g.upto())
                    pe.wait_ge(nmp_lo_ready, g.upto())
                    split_product(bank[6][:, :, :], "ih", 3 * P + 1 * P, nmp_hi[:, :, :], nmp_lo[:, :, :], start=False, stop=False)
                    if t.C.past(0): pe.wait_ge(rms_wide_ready, t.C.upto())
                    if t.A1.past(0): pe.wait_ge(h0_hi_ready, t.A1.upto())
                    split_product(bank[5][:, :, :], "hh", 2 * P, h0_hi[g % 2][:, :, :], h0_lo[g % 2][:, :, :]).then_inc(hidden_n_done, 1)
                    pe.wait_ge(x_conv_hi_ready, g.upto())
                    pe.wait_ge(x_conv_lo_ready, g.upto())
                    split_product(bank[0][:, :, :], "ih", 0 * P, x_conv_hi[:, :, :], x_conv_lo[:, :, :], start=False).then_inc(r_done, 1)
                    pe.wait_ge(nmp_hi_ready, g.upto())
                    pe.wait_ge(nmp_lo_ready, g.upto())
                    if t.B2.past(0): pe.wait_ge(rel_ready, t.B2.upto())
                    pe.wait_ge(nmp_lo_ready, g.upto())
                    split_product(bank[7][:, :, :], "ih", 3 * P + 2 * P, nmp_hi[:, :, :], nmp_lo[:, :, :], stop=False)
                g = t.C
                if g.real:
                    pe.wait_ge(silu_ready[0], g.upto())
                    if t.B2.past(0): pe.wait_ge(conv_rel_ready, t.B2.upto())
                    pe.wait_ge(hidden_ready[1], g.upto())
                    per_graph(bank[4], lambda b: silu[0][:, b, :], lambda b: w2_half[:, 0, :], stop=False)
                g = t.A2
                if g.real:
                    pe.wait_ge(x_conv_hi_ready, g.upto())
                    pe.wait_ge(x_conv_lo_ready, g.upto())
                    split_product(bank[7][:, :, :], "ih", 2 * P, x_conv_hi[:, :, :], x_conv_lo[:, :, :], start=False).then_inc(input_n_done, 1)
                g = t.C
                if g.real:
                    pe.wait_ge(silu_ready[1], g.upto())
                    per_graph(bank[4], lambda b: silu[1][:, b, :], lambda b: w2_half[:, 1, :], start=False, stop=False)
                g = t.A2
                if g.real:
                    pe.wait_ge(x_conv_hi_ready, g.upto())
                    pe.wait_ge(x_conv_lo_ready, g.upto())
                    split_product(bank[6][:, :, :], "ih", 1 * P, x_conv_hi[:, :, :], x_conv_lo[:, :, :], start=False).then_inc(z_done, 1)
                g = t.C
                if g.real:
                    pe.wait_ge(silu_ready[2], g.upto())
                    per_graph(bank[4], lambda b: silu[2][:, b, :], lambda b: w2_half[:, 2, :], start=False, stop=False)
                    pe.wait_ge(silu_ready[3], g.upto())
                    per_graph(bank[4], lambda b: silu[3][:, b, :], lambda b: w2_half[:, 3, :], start=False).then_inc(out_done, 1)

            turns(pe, turn)

        @block.scalar
        def _(act):
            act.wait_ge(prepared, 1)

            def turn(t):
                g = t.A1
                if g.real:
                    act.wait_ge(h0_turned, g.upto())
                    if g.past(2): act.wait_ge(z_done, g.upto(2))
                    if g.past(2): act.wait_ge(h_less_n_ready, g.upto(2))
                    act.activation(h0[g % 2][:, :, :], bank[5][:, :, :], ACT.Relu).then_inc(h0_ready, 1)
                    act.activation(h0_hi[g % 2][:, :, :], bank[5][:, :, :], ACT.Relu).then_inc(h0_hi_ready, 1)
                g = t.C
                if g.real:
                    act.wait_ge(norm3.normed, g.upto())
                    act.activation(h3[:, :, :], h3[:, :, :], ACT.Relu).then_inc(h3_ready, 1)
                    act.wait_ge(agg_done, g.upto())
                    if g.past(1): act.wait_ge(hidden_done[CHUNKS - 1], g.upto(1))
                    act.activation(agg_hi[:, :, :], bank[7][:, :, :], ACT.Copy).then_inc(agg_hi_ready, 1)
                g = t.A2
                if g.real:
                    act.wait_ge(dist_done, g.upto())
                    if g.past(1): act.wait_ge(nmp_done, g.upto(1))
                    act.activation(masked[:, :, :], bank[1][:, :, :], ACT.Exp).then_inc(affinity_ready, 1)
                g = t.B2
                if g.real:
                    act.wait_ge(norm2.normed, g.upto())
                    act.activation(h2[:, :, :], h2[:, :, :], ACT.Relu).then_inc(h2_ready, 1)
                g = t.A1
                if g.real:
                    act.wait_ge(conv1_done, g.upto())
                    if g.past(1): act.wait_ge(c1_hi_ready, g.upto(1))
                    if g.past(1): act.wait_ge(c1_lo_ready, g.upto(1))
                    act.activation(c1[:, :, :], bank[6][:, :, :], ACT.Relu, bias=bn_bias[:, 0:1],
                                   scale=bn_scale[:, 0:1]).then_inc(c1_ready, 1)
                g = t.C
                if g.real:
                    act.wait_ge(hidden_done[0], g.upto())
                    if g.past(1): act.wait_ge(rms_done, g.upto(1))
                    act.activation(square[0][:, :, :], bank[0][:, :, :], ACT.Square,
                                   bias=column("h0")).then_inc(square_ready[0], 1)
                    act.wait_ge(hidden_done[0], g.upto())
                    if g.past(1): act.wait_ge(silu_ready[0], g.upto(1))
                    act.activation(hidden[0][:, :, :], bank[0][:, :, :], ACT.Identity,
                                   bias=column("h0")).then_inc(hidden_ready[0], 1)
                    act.wait_ge(hidden_done[1], g.upto())
                    if g.past(1): act.wait_ge(rms_done, g.upto(1))
                    act.activation(square[1][:, :, :], bank[4][:, :, :], ACT.Square,
                                   bias=column("h1")).then_inc(square_ready[1], 1)
                g = t.B1
                if g.real:
                    act.wait_ge(h1_turned, g.upto())
                    if g.past(1): act.wait_ge(gate_done, g.upto(1))
                    act.activation(h1[:, :, :], bank[0][:, :, :], ACT.Relu).then_inc(h1_ready, 1)
                g = t.C
                if g.real:
                    act.wait_ge(hidden_done[2], g.upto())
                    if g.past(1): act.wait_ge(rms_done, g.upto(1))
                    act.activation(square[2][:, :, :], bank[5][:, :, :], ACT.Square,
                                   bias=column("h2")).then_inc(square_ready[2], 1)
                    act.wait_ge(hidden_done[3], g.upto())
                    if g.past(1): act.wait_ge(rms_done, g.upto(1))
                    act.activation(square[3][:, :, :], bank[6][:, :, :], ACT.Square,
                                   bias=column("h3")).then_inc(square_ready[3], 1)
                    act.wait_ge(hidden_done[1], g.upto())
                    if g.past(1): act.wait_ge(silu_ready[1], g.upto(1))
                    act.activation(hidden[1][:, :, :], bank[4][:, :, :], ACT.Identity,
                                   bias=column("h1")).then_inc(hidden_ready[1], 1)
                g = t.A1
                if g.real:
                    act.wait_ge(message_summed, g.upto())
                    act.activation(message[g % 2][:, :, :], message[g % 2][:, :, :], ACT.Relu).then_inc(message_ready, 1)
                g = t.C
                if g.real:
                    act.wait_ge(hidden_done[3], g.upto())
                    if g.past(1): act.wait_ge(silu_ready[3], g.upto(1))
                    act.activation(hidden[3][:, :, :], bank[6][:, :, :], ACT.Identity,
                                   bias=column("h3")).then_inc(hidden_ready[3], 1)
                g = t.A2
                if g.real:
                    act.wait_ge(nmp_done, g.upto())
                    if g.past(1): act.wait_ge(z_done, g.upto(1))
                    act.activation(nmp_hi[:, :, :], bank[7][:, :, :], ACT.Copy).then_inc(nmp_hi_ready, 1)
                g = t.B1
                if g.real:
                    act.wait_ge(het_done, g.upto())
                    if g.past(1): act.wait_ge(mix_ready, g.upto(1))
                    act.activation(f_het[:, :, :], bank[1][:, :, :], ACT.Copy).then_inc(f_het_ready, 1)
                    act.wait_ge(gate1_summed, g.upto())
                    act.activation(gate_tanh[:, :, :], gate_tanh[:, :, :], ACT.Tanh, scale=0.5).then_inc(gate1_ready, 1)
                g = t.B2
                if g.real:
                    act.wait_ge(h2_turned, g.upto())
                    if g.past(1): act.wait_ge(conv_rel_done, g.upto(1))
                    act.activation(h2_col[:, :, :], bank[6][:, :, :], ACT.Identity, bias=column("beta"),
                                   scale=column("gamma")).then_inc(h2_col_ready, 1)
                g = t.C
                if g.real:
                    act.wait_ge(hidden_done[2], g.upto())
                    if g.past(1): act.wait_ge(silu_ready[2], g.upto(1))
                    act.activation(hidden[2][:, :, :], bank[5][:, :, :], ACT.Identity,
                                   bias=column("h2")).then_inc(hidden_ready[2], 1)
                    act.wait_ge(rms_wide_done, g.upto())
                    if g.past(1): act.wait_ge(scaled_ready[CHUNKS - 1], g.upto(1))
                    act.activation(rms_wide[:, :, :], bank[5][:, :, :], ACT.Copy).then_inc(rms_wide_ready, 1)
                g = t.A2
                if g.real:
                    act.wait_ge(conv_summed, g.upto())
                    act.activation(conv_sum[:, :, :], conv_sum[:, :, :], ACT.Relu,
                                   bias=bn_bias[:, 1:2]).then_inc(x_conv_ready, 1)
                    act.wait_ge(x_conv_ready, g.upto())
                    if g.past(1): act.wait_ge(z_done, g.upto(1))
                    act.activation(x_conv_hi[:, :, :], conv_sum[:, :, :], ACT.Copy).then_inc(x_conv_hi_ready, 1)
                g = t.B2
                if g.real:
                    act.wait_ge(rel_done, g.upto())
                    act.activation(rel[:, :, :], bank[7][:, :, :], ACT.Copy).then_inc(rel_ready, 1)
                g = t.C
                if g.real:
                    for c in range(3):
                        act.wait_ge(scaled_ready[c], g.upto())
                        if g.past(1): act.wait_ge(out_done, g.upto(1))
                        act.activation(silu[c][:, :, :], hidden[c][:, :, :], ACT.Tanh,
                                       scale=half_rms[:, c:c + 1]).then_inc(silu_tanh_ready[c], 1)
                g = t.B1
                if g.real:
                    act.wait_ge(elu_neg_ready, g.upto())
                    act.activation(elu_neg[:, :, :], elu_neg[:, :, :], ACT.Exp).then_inc(elu_exp_ready, 1)
                g = t.C
                if g.real:
                    act.wait_ge(scaled_ready[3], g.upto())
                    if g.past(1): act.wait_ge(out_done, g.upto(1))
                    act.activation(silu[3][:, :, :], hidden[3][:, :, :], ACT.Tanh,
                                   scale=half_rms[:, 3:3 + 1]).then_inc(silu_tanh_ready[3], 1)
                g = t.A2
                if g.real:
                    act.wait_ge(r_done, g.upto())
                    if g.past(1): act.wait_ge(gru_ready, g.upto(1))
                    act.activation(candidate[:, :, :], bank[0][:, :, :], ACT.Tanh, bias=gate_bias[:, 0:1],
                                   scale=0.5).then_inc(tanh_r_ready, 1)
                g = t.A1
                if g.real:
                    act.wait_ge(se_done, g.upto())
                    act.wait_ge(left_ready, g.upto())
                    if g.past(2): act.wait_ge(dist_done, g.upto(2))
                    act.activation(right[g % 2][0:32, :, :], bank[3][0:32, :, :], ACT.Identity, bias=column("se", 32))
                    act.activation(left[g % 2][32:64, :, :], bank[3][32:64, :, :], ACT.Square, bias=column("se", 32, 32))
                    act.activation(right[g % 2][64:96, :, :], bank[3][64:96, :, :], ACT.Square,
                                   bias=column("se", 32, 64)).then_inc(right_ready, 1)
                g = t.A2
                if g.real:
                    act.wait_ge(z_done, g.upto())
                    if g.past(1): act.wait_ge(z_part_ready, g.upto(1))
                    act.activation(gate_z[:, :, :], bank[6][:, :, :], ACT.Tanh, bias=gate_bias[:, 1:2],
                                   scale=0.5).then_inc(tanh_z_ready, 1)
                    act.wait_ge(n_summed, g.upto())
                    act.activation(candidate[:, :, :], candidate[:, :, :], ACT.Tanh, bias=column("ih_n")).then_inc(n_ready, 1)

            turns(act, turn)

        @block.vector
        def _(dve):
            dve.wait_ge(weights_loaded, 64)
            dve.tensor_scalar(bn_var[:, :], column("v1", n=2), LN_EPS, None, ALU.add).then_inc(bn_var_ready, 1)
            dve.tensor_tensor(gate_sum[:, :], column("ih_r", n=2), column("hh_r", n=2), ALU.add).then_inc(dve_setup, 1)
            dve.tensor_scalar(half_rms[:, :], column("w0", n=CHUNKS), 0.5, None, ALU.mult).then_inc(dve_setup, 1)
            dve.tensor_copy(weights_hi[:, :], weights_raw).then_inc(dve_setup, 1)
            dve.wait_ge(dve_setup, 3)
            dve.tensor_scalar(gate_bias[:, :], gate_sum[:, :], 0.5, None, ALU.mult)
            for c in range(CHUNKS):
                dve.tensor_scalar(w2_half[:, c, :], weight("W2", P, c * P), half_rms[:, c:c + 1], None, ALU.mult)
            dve.tensor_tensor(weights_lo[:, :], weights_raw, weights_hi[:, :].bitcast(F32), ALU.subtract)
            for tile in (*c1_hi, *c1_lo):
                dve.memset(tile[:, :, 0:1].bitcast(F32), 0.0)
                dve.memset(tile[:, :, P + 1:P + 2].bitcast(F32), 0.0)
            for n in range(2):
                dve.memset(left[n][64:96, :, :], -1.0)
                dve.memset(right[n][32:64, :, :], -1.0)
            dve.wait_ge(constants_ready, 1)
            dve.tensor_scalar(eps_identity[:, :], identity[:, :], column("eps"), None, ALU.mult)
            dve.wait_ge(constants_ready, 2)
            dve.tensor_tensor(bn_scale[:, :], bn_root[:, :], column("g1", n=2), ALU.mult).then_inc(dve_setup, 1)
            dve.wait_ge(dve_setup, 4)
            dve.tensor_tensor(bn_mean[:, :], bn_scale[:, :], column("m1", n=2), ALU.mult).then_inc(dve_setup, 1)
            dve.wait_ge(dve_setup, 5)
            dve.tensor_tensor(bn_bias[:, :], column("b1", n=2), bn_mean[:, :], ALU.subtract).then_inc(prepared, 1)
            dve.wait_ge(prepared, 1)

            def statistics(norm, tile, g):
                for b in range(PER):
                    last = dve.bn_stats(norm.stats[:, b, :], tile[:, b, :])
                last.then_inc(norm.stats_ready, 1)
                dve.wait_ge(norm.stats_ready, g.upto())
                if g.past(1): dve.wait_ge(norm.var_ready, g.upto(1))
                dve.sem_inc(dve_held, 1)
                for b in range(PER):
                    last = dve.bn_aggr(norm.moments[:, b, :], norm.stats[:, b, :])
                last.then_inc(norm.moments_ready, 1)

            def normalise(norm, out, tile, g):
                dve.wait_ge(norm.scale_ready, g.upto())
                for b in range(PER):
                    last = dve.tensor_scalar(out[:, b, :], tile[:, b, :], norm.moments[:, b, 0:1],
                                             norm.scale[:, b:b + 1], ALU.subtract, ALU.mult)
                last.then_inc(norm.normed, 1)

            def turn(t):
                g = t.C
                if g.real:
                    if g.past(1): dve.wait_ge(agg_done, g.upto(1))
                    normalise(norm3, h3, x3[g % 2], g)
                g = t.B1
                if g.real:
                    dve.wait_ge(gru_turned, g.upto())
                    if g.past(2): dve.wait_ge(elu_pos_ready, g.upto(2))
                    dve.tensor_tensor(x1[g % 2][:, :, :], bank[7][:, :, :], x_in[g % 4][:, :, :], ALU.add).then_inc(x1_ready, 1)
                    dve.wait_ge(degree_done, g.upto())
                    if g.past(1): dve.wait_ge(deg_scale_ready, g.upto(1))
                    dve.tensor_scalar(degree[:, :], bank[6][:, 0, 0:PER], DEG_EPS, None, ALU.add).then_inc(degree_ready, 1)
                g = t.A1
                if g.real:
                    dve.wait_ge(h0_ready, g.upto())
                    dve.wait_ge(h0_hi_ready, g.upto())
                    if g.past(2): dve.wait_ge(z_done, g.upto(2))
                    dve.tensor_tensor(h0_lo[g % 2][:, :, :], h0[g % 2][:, :, :], h0_hi[g % 2][:, :, :].bitcast(F32),
                                      ALU.subtract).then_inc(h0_lo_ready, 1)
                g = t.B1
                if g.real:
                    dve.wait_ge(x1_ready, g.upto())
                    statistics(norm1, x1[g % 2], g)
                g = t.A1
                if g.real:
                    dve.wait_ge(message_done, g.upto())
                    if g.past(2): dve.wait_ge(nmp_done, g.upto(2))
                    dve.tensor_tensor(message[g % 2][:, :, :], bank[0][:, :, :], row("msg"), ALU.add).then_inc(message_summed, 1)
                g = t.B2
                if g.real:
                    if g.past(1): dve.wait_ge(x2_h2_ready, g.upto(1))
                    normalise(norm2, h2, x2[g % 2], g)
                g = t.C
                if g.real:
                    dve.wait_ge(agg_hi_ready, g.upto())
                    if g.past(1): dve.wait_ge(hidden_done[CHUNKS - 1], g.upto(1))
                    dve.tensor_tensor(agg_lo[:, :, :], bank[7][:, :, :], agg_hi[:, :, :].bitcast(F32),
                                      ALU.subtract).then_inc(agg_lo_ready, 1)
                g = t.B1
                if g.real:
                    if g.past(1): dve.wait_ge(h1_turned, g.upto(1))
                    normalise(norm1, h1n, x1[g % 2], g)
                g = t.N
                if g.real:
                    dve.wait_ge(x_loaded[g % 4], g.transfers(4))
                    statistics(norm0, x_in[g % 4], g)
                g = t.B2
                if g.real:
                    dve.wait_ge(h2_ready, g.upto())
                    statistics(norm2b, h2, g)
                g = t.A1
                if g.real:
                    dve.wait_ge(c1_ready, g.upto())
                    if g.past(2): dve.wait_ge(conv2_done, g.upto(2))
                    dve.tensor_copy(c1_hi[g % 2][:, :, 1:P + 1], c1[:, :, :]).then_inc(c1_hi_ready, 1)
                    dve.wait_ge(c1_hi_ready, g.upto())
                    dve.tensor_tensor(c1_lo[g % 2][:, :, 1:P + 1], c1[:, :, :],
                                      c1_hi[g % 2][:, :, 1:P + 1].bitcast(F32), ALU.subtract).then_inc(c1_lo_ready, 1)
                    dve.wait_ge(se_done, g.upto())
                    if g.past(2): dve.wait_ge(dist_done, g.upto(2))
                    dve.tensor_scalar(left[g % 2][0:32, :, :], bank[3][0:32, :, :], column("se", 32), 2.0,
                                      ALU.add, ALU.mult).then_inc(left_ready, 1)
                g = t.B1
                if g.real:
                    dve.wait_ge(theta_done, g.upto())
                    dve.wait_ge(deg_scale_ready, g.upto())
                    if g.past(1): dve.wait_ge(hom_done, g.upto(1))
                    scale = deg_scale[:, :].unsqueeze(2).to_broadcast([P, PER, P])
                    dve.tensor_tensor(f_hom[:, :, :], bank[0][:, :, :], scale, ALU.mult).then_inc(f_hom_ready, 1)
                g = t.N
                if g.real:
                    if g.past(2): dve.wait_ge(h0_turned, g.upto(2))
                    normalise(norm0, h0n[g % 2], x_in[g % 4], g)
                g = t.B2
                if g.real:
                    if g.past(1): dve.wait_ge(h2_turned, g.upto(1))
                    normalise(norm2b, h2nn, h2, g)
                g = t.B1
                if g.real:
                    dve.wait_ge(gate_done, g.upto())
                    if g.past(1): dve.wait_ge(gated_ready, g.upto(1))
                    dve.tensor_tensor(gate_tanh[:, :, :], bank[4][:, :, :], row("b_t"), ALU.add).then_inc(gate1_summed, 1)
                g = t.A2
                if g.real:
                    dve.wait_ge(nmp_hi_ready, g.upto())
                    if g.past(1): dve.wait_ge(z_done, g.upto(1))
                    dve.tensor_tensor(nmp_lo[:, :, :], bank[7][:, :, :], nmp_hi[:, :, :].bitcast(F32),
                                      ALU.subtract).then_inc(nmp_lo_ready, 1)
                g = t.B1
                if g.real:
                    dve.wait_ge(hom_done, g.upto())
                    if g.past(1): dve.wait_ge(gated_ready, g.upto(1))
                    dve.tensor_tensor(hom[:, :, :], bank[0][:, :, :], scale, ALU.mult).then_inc(hom_ready, 1)
                g = t.C
                if g.real:
                    dve.wait_ge(rms_done, g.upto())
                    if g.past(1): dve.wait_ge(rms_scale_ready, g.upto(1))
                    dve.tensor_scalar(mean_square[:, :], bank[1][:, 0, 0:PER], 1.0 / HID, RMS_EPS,
                                      ALU.mult, ALU.add).then_inc(mean_square_ready, 1)
                g = t.B1
                if g.real:
                    dve.wait_ge(hom_ready, g.upto())
                    dve.wait_ge(f_het_ready, g.upto())
                    dve.tensor_tensor(hom[:, :, :], hom[:, :, :], f_het[:, :, :], ALU.subtract).then_inc(difference_ready, 1)
                    dve.wait_ge(gate1_ready, g.upto())
                    dve.wait_ge(difference_ready, g.upto())
                    dve.scalar_tensor_tensor(out=mix[:, :, :], in0=gate_tanh[:, :, :], scalar=1.0,
                                             in1=hom[:, :, :], op0=ALU.add, op1=ALU.mult).then_inc(gated_ready, 1)
                g = t.C
                if g.real:
                    dve.wait_ge(rms_scale_ready, g.upto())
                    if g.past(1): dve.wait_ge(rms_wide_done, g.upto(1))
                    for b in range(PER):
                        last = dve.tensor_scalar(rms_diag[:, b, :], identity[:, :], rms_scale[:, b:b + 1], None, ALU.mult)
                    last.then_inc(rms_diag_ready, 1)
                g = t.A2
                if g.real:
                    dve.wait_ge(conv2_done, g.upto())
                    if g.past(1): dve.wait_ge(x_conv_lo_ready, g.upto(1))
                    dve.scalar_tensor_tensor(out=conv_sum[:, :, :], in0=bank[2][:, :, :], scalar=bn_scale[:, 1:2],
                                             in1=h0[g % 2][:, :, :], op0=ALU.mult, op1=ALU.add).then_inc(conv_summed, 1)
                g = t.B1
                if g.real:
                    dve.wait_ge(gated_ready, g.upto())
                    dve.scalar_tensor_tensor(out=mix[:, :, :], in0=mix[:, :, :], scalar=0.5,
                                             in1=f_het[:, :, :], op0=ALU.mult, op1=ALU.add).then_inc(mix_ready, 1)
                    dve.wait_ge(mix_ready, g.upto())
                    dve.scalar_tensor_tensor(out=elu_pos[:, :, :], in0=mix[:, :, :], scalar=0.0,
                                             in1=x1[g % 2][:, :, :], op0=ALU.max, op1=ALU.add).then_inc(elu_pos_ready, 1)
                    dve.wait_ge(mix_ready, g.upto())
                    if g.past(1): dve.wait_ge(x2_ready, g.upto(1))
                    dve.tensor_scalar(elu_neg[:, :, :], mix[:, :, :], 0.0, None, ALU.min).then_inc(elu_neg_ready, 1)
                g = t.C
                if g.real:
                    for c in range(3):
                        dve.wait_ge(rms_wide_ready, g.upto())
                        dve.wait_ge(hidden_ready[c], g.upto())
                        dve.tensor_tensor(hidden[c][:, :, :], hidden[c][:, :, :], rms_wide[:, :, :], ALU.mult).then_inc(scaled_ready[c], 1)
                g = t.A2
                if g.real:
                    dve.wait_ge(x_conv_hi_ready, g.upto())
                    if g.past(1): dve.wait_ge(z_done, g.upto(1))
                    dve.tensor_tensor(x_conv_lo[:, :, :], conv_sum[:, :, :], x_conv_hi[:, :, :].bitcast(F32),
                                      ALU.subtract).then_inc(x_conv_lo_ready, 1)
                g = t.C
                if g.real:
                    dve.wait_ge(silu_tanh_ready[0], g.upto())
                    dve.scalar_tensor_tensor(out=silu[0][:, :, :], in0=silu[0][:, :, :], scalar=1.0,
                                             in1=hidden[0][:, :, :], op0=ALU.add, op1=ALU.mult).then_inc(silu_ready[0], 1)
                    dve.wait_ge(rms_wide_ready, g.upto())
                    dve.wait_ge(hidden_ready[3], g.upto())
                    dve.tensor_tensor(hidden[3][:, :, :], hidden[3][:, :, :], rms_wide[:, :, :], ALU.mult).then_inc(scaled_ready[3], 1)
                g = t.B2
                if g.real:
                    dve.wait_ge(conv_rel_done, g.upto())
                    dve.tensor_tensor(conv_rel[:, :, :], bank[4][:, :, :], row("rel"), ALU.add).then_inc(conv_rel_ready, 1)
                g = t.C
                if g.real:
                    dve.wait_ge(silu_tanh_ready[1], g.upto())
                    dve.scalar_tensor_tensor(out=silu[1][:, :, :], in0=silu[1][:, :, :], scalar=1.0,
                                             in1=hidden[1][:, :, :], op0=ALU.add, op1=ALU.mult).then_inc(silu_ready[1], 1)
                g = t.B1
                if g.real:
                    dve.wait_ge(elu_exp_ready, g.upto())
                    dve.wait_ge(elu_pos_ready, g.upto())
                    if g.past(2): dve.wait_ge(x2_h2_ready, g.upto(2))
                    dve.scalar_tensor_tensor(out=x2[g % 2][:, :, :], in0=elu_neg[:, :, :], scalar=-1.0,
                                             in1=elu_pos[:, :, :], op0=ALU.add, op1=ALU.add).then_inc(x2_ready, 1)
                g = t.B2
                if g.real:
                    dve.wait_ge(conv_rel_ready, g.upto())
                    dve.wait_ge(x2_h2_ready, g.upto())
                    if g.past(2): dve.wait_ge(x3_b2_ready, g.upto(2))
                    dve.scalar_tensor_tensor(out=x3[g % 2][:, :, :], in0=conv_rel[:, :, :], scalar=0.0,
                                             in1=x2_h2[:, :, :], op0=ALU.max, op1=ALU.add).then_inc(x3_ready, 1)
                g = t.C
                if g.real:
                    for c in (2, 3):
                        dve.wait_ge(silu_tanh_ready[c], g.upto())
                        dve.scalar_tensor_tensor(out=silu[c][:, :, :], in0=silu[c][:, :, :], scalar=1.0,
                                                 in1=hidden[c][:, :, :], op0=ALU.add, op1=ALU.mult).then_inc(silu_ready[c], 1)
                g = t.A2
                if g.real:
                    dve.wait_ge(gate_r_ready, g.upto())
                    dve.scalar_tensor_tensor(out=candidate[:, :, :], in0=bank[5][:, :, :], scalar=column("hh_n"),
                                             in1=candidate[:, :, :], op0=ALU.add, op1=ALU.mult).then_inc(r_hidden_ready, 1)
                    dve.wait_ge(r_hidden_ready, g.upto())
                    dve.wait_ge(input_n_done, g.upto())
                    dve.tensor_tensor(candidate[:, :, :], candidate[:, :, :], bank[7][:, :, :], ALU.add).then_inc(n_summed, 1)
                g = t.B2
                if g.real:
                    dve.wait_ge(x3_ready, g.upto())
                    statistics(norm3, x3[g % 2], g)
                g = t.B1
                if g.real:
                    dve.wait_ge(x2_ready, g.upto())
                    statistics(norm2, x2[g % 2], g)
                g = t.C
                if g.real:
                    dve.wait_ge(out_done, g.upto())
                    dve.wait_ge(x3_b2_ready, g.upto())
                    if g.past(2): dve.wait_ge(stored[g % 2], g.transfers(2, 2))
                    dve.tensor_tensor(result[g % 2][:, :, :], bank[4][:, :, :], x3_b2[:, :, :], ALU.add).then_inc(result_ready, 1)
                g = t.A2
                if g.real:
                    dve.wait_ge(h_less_n_ready, g.upto())
                    dve.wait_ge(gate_z_ready, g.upto())
                    if g.past(1): dve.wait_ge(gru_turned, g.upto(1))
                    dve.tensor_tensor(gru[:, :, :], gate_z[:, :, :], h_less_n[:, :, :], ALU.mult).then_inc(z_part_ready, 1)
                    dve.wait_ge(z_part_ready, g.upto())
                    dve.tensor_tensor(gru[:, :, :], gru[:, :, :], candidate[:, :, :], ALU.add).then_inc(gru_ready, 1)

            turns(dve, turn)

        @block.gpsimd
        def _(pool):
            pool.memset(identity[:, :], 0.0).then_inc(identity_blank, 1)
            pool.memset(ones[:, :], 1.0)
            pool.memset(minus_half[:, :], -0.5).then_inc(identity_blank, 1)
            pool.wait_ge(identity_blank, 1)
            pool.affine_select(out=identity[:, :], in_=identity[:, :], compare_op=ALU.not_equal, fill=1.0, base=0,
                               pattern=[[-1, P]], channel_multiplier=1).then_inc(constants_ready, 1)
            pool.wait_ge(identity_blank, 2)
            pool.wait_ge(bn_var_ready, 1)
            pool.tensor_tensor(bn_root[:, :], bn_var[:, :], minus_half[:, 0:2], ALU.pow).then_inc(constants_ready, 1)
            pool.wait_ge(prepared, 1)

            def inverse_deviation(norm, g):
                pool.wait_ge(norm.moments_ready, g.upto())
                if g.past(1): pool.wait_ge(norm.scale_ready, g.upto(1))
                pool.sem_inc(pool_held, 1)
                pool.tensor_scalar(norm.var[:, :], norm.moments[:, :, 1], LN_EPS, None, ALU.add).then_inc(norm.var_ready, 1)
                pool.wait_ge(norm.var_ready, g.upto())
                if g.past(1): pool.wait_ge(norm.normed, g.upto(1))
                pool.tensor_tensor(norm.scale[:, :], norm.var[:, :], minus_half[:, :], ALU.pow).then_inc(norm.scale_ready, 1)

            def turn(t):
                g = t.B1
                if g.real:
                    pool.wait_ge(degree_ready, g.upto())
                    if g.past(1): pool.wait_ge(hom_ready, g.upto(1))
                    pool.tensor_tensor(deg_scale[:, :], degree[:, :], minus_half[:, :], ALU.pow).then_inc(deg_scale_ready, 1)
                    inverse_deviation(norm1, g)
                g = t.A2
                if g.real:
                    pool.wait_ge(adj_loaded[g % 4], g.transfers(4))
                    pool.wait_ge(affinity_ready, g.upto())
                    pool.tensor_tensor(masked[:, :, :], masked[:, :, :], adj[g % 4][:, :, :], ALU.mult).then_inc(masked_ready, 1)
                g = t.B2
                if g.real:
                    pool.wait_ge(adj_loaded[g % 4], g.transfers(4))
                    if g.past(1): pool.wait_ge(agg_done, g.upto(1))
                    pool.tensor_tensor(adj_eps[:, :, :], adj[g % 4][:, :, :],
                                       eps_identity[:, :].unsqueeze(1).to_broadcast([P, PER, P]), ALU.add).then_inc(adj_eps_ready, 1)
                g = t.N
                if g.real:
                    inverse_deviation(norm0, g)
                g = t.B2
                if g.real:
                    inverse_deviation(norm2b, g)
                g = t.C
                if g.real:
                    pool.wait_ge(square_ready[0], g.upto())
                    pool.wait_ge(square_ready[1], g.upto())
                    pool.tensor_tensor(square[0][:, :, :], square[0][:, :, :], square[1][:, :, :],
                                       ALU.add).then_inc(square_summed[0], 1)
                    pool.wait_ge(square_ready[2], g.upto())
                    pool.wait_ge(square_ready[3], g.upto())
                    pool.tensor_tensor(square[2][:, :, :], square[2][:, :, :], square[3][:, :, :],
                                       ALU.add).then_inc(square_summed[1], 1)
                    pool.wait_ge(square_summed[0], g.upto())
                    pool.wait_ge(square_summed[1], g.upto())
                    pool.tensor_tensor(square[0][:, :, :], square[0][:, :, :], square[2][:, :, :],
                                       ALU.add).then_inc(square_summed[2], 1)
                    if g.past(1): pool.wait_ge(result_ready, g.upto(1))
                    pool.tensor_tensor(x3_b2[:, :, :], x3[g % 2][:, :, :], row("out"), ALU.add).then_inc(x3_b2_ready, 1)
                    pool.wait_ge(mean_square_ready, g.upto())
                    if g.past(1): pool.wait_ge(rms_diag_ready, g.upto(1))
                    pool.tensor_tensor(rms_scale[:, :], mean_square[:, :], minus_half[:, :], ALU.pow).then_inc(rms_scale_ready, 1)
                g = t.B2
                if g.real:
                    pool.wait_ge(h2_ready, g.upto())
                    if g.past(1): pool.wait_ge(x3_ready, g.upto(1))
                    pool.tensor_tensor(x2_h2[:, :, :], x2[g % 2][:, :, :], h2[:, :, :], ALU.add).then_inc(x2_h2_ready, 1)
                g = t.A2
                if g.real:
                    pool.wait_ge(tanh_r_ready, g.upto())
                    pool.sem_inc(pool_held, 1)
                    pool.tensor_scalar(candidate[:, :, :], candidate[:, :, :], 0.5, 0.5, ALU.mult, ALU.add).then_inc(gate_r_ready, 1)
                    pool.wait_ge(tanh_z_ready, g.upto())
                    pool.sem_inc(pool_held, 1)
                    pool.tensor_scalar(gate_z[:, :, :], gate_z[:, :, :], 0.5, 0.5, ALU.mult, ALU.add).then_inc(gate_z_ready, 1)
                    pool.wait_ge(n_ready, g.upto())
                    pool.tensor_tensor(h_less_n[:, :, :], h0[g % 2][:, :, :], candidate[:, :, :], ALU.subtract).then_inc(h_less_n_ready, 1)
                g = t.B2
                if g.real:
                    inverse_deviation(norm3, g)
                g = t.B1
                if g.real:
                    inverse_deviation(norm2, g)

            turns(pool, turn)


def kernel(**inputs):
    import numpy as np
    import concourse.bacc as bacc
    from concourse.bass_utils import run_bass_kernel_spmd

    a = {name: np.asarray(value) for name, value in inputs.items()}
    L0 = {name[7:]: value for name, value in a.items() if name.startswith("L0_gnn_")}

    x = a["x"].reshape(GROUPS, PER, P, P).transpose(2, 0, 1, 3)
    adj = a["adj"].reshape(GROUPS, PER, P, P).transpose(3, 0, 1, 2)
    se = np.zeros((P, 96), np.float32)
    b_se = np.zeros(P, np.float32)
    for n in range(3):
        se[:, 32 * n:32 * n + 3] = L0["w_se"].T
        b_se[32 * n:32 * n + 3] = L0["b_se"]
    w_ih = L0["w_ih"].T.reshape(2, P, 3 * P).transpose(1, 0, 2).reshape(P, -1)
    W2 = a["L3_gnn_W2"].reshape(CHUNKS, P, P).transpose(1, 0, 2).reshape(P, -1)
    weights = np.concatenate([L0["w_msg"].T, a["L1_gnn_theta"], a["L1_gnn_W_h"], a["L1_gnn_W_t"], a["L2_gnn_W_rel"],
                              a["L2_gnn_W_root"], W2], 1)
    split = np.concatenate([L0["conv2_w"].transpose(1, 2, 0).reshape(P, -1), L0["conv1_w"][:, :, 0].T, se, w_ih,
                            L0["w_hh"].T, a["L3_gnn_W1"]], 1)
    columns = np.stack([
        L0["bn1_g"], L0["bn2_g"], L0["bn1_b"], L0["bn2_b"], L0["bn1_m"], L0["bn2_m"], L0["bn1_v"], L0["bn2_v"],
        *L0["b_ih"].reshape(3, P), *L0["b_hh"].reshape(3, P), b_se, a["L2_gnn_ln_gamma"], a["L2_gnn_ln_beta"],
        np.broadcast_to(a["L3_gnn_epsilon"], (P,)), *a["L3_gnn_b1"].reshape(CHUNKS, P),
        *a["L3_gnn_rms_weight"].reshape(CHUNKS, P)], 1)
    rows = np.stack([L0["b_msg"], a["L1_gnn_b_t"], a["L2_gnn_b_rel"], a["L3_gnn_b2"]])

    nc = bacc.Bacc("TRN2", target_bir_lowering=False, num_devices=1)
    arrays, args = {}, []
    for name, value in (("x", x), ("adj", adj), ("weights", weights), ("split", split), ("columns", columns), ("rows", rows)):
        value = np.ascontiguousarray(value)
        arrays[f"in_{name}_dram"] = value
        args.append(nc.dram_tensor(f"in_{name}_dram", value.shape, mybir.dt.from_np(value.dtype), kind="ExternalInput").ap())
    args.append(nc.dram_tensor("out_dram", (P, GROUPS, PER, P), F32, kind="ExternalOutput").ap())
    graph_layers(nc, *args)
    r = run_bass_kernel_spmd(nc, [arrays], core_ids=[0])
    out = r.results[0]["out_dram"]
    return out.transpose(1, 2, 0, 3).reshape(GRAPHS, P, P)
```

```python
from contextlib import ExitStack

import concourse.bass as bass
from concourse import mybir

ALU = mybir.AluOpType
ACT = mybir.ActivationFunctionType
F32 = mybir.dt.float32
F32R = mybir.dt.float32r

P = 128
GRAPHS = 128
PER = 4
PREPARED = 7
CONV2_READY = 9
GROUPS = GRAPHS // PER
TAPS = 17
HALF = P // 2
REACH = TAPS // 4
BEFORE = REACH + 2
PAIRS = TAPS // 2
HID = 512
CHUNKS = HID // P
LAG = {"N": 0, "A1": 1, "A2": 2, "B1": 3, "B2": 4, "C": 5}
TURNS = GROUPS + LAG["C"]
UNROLL = 4
LOOP_FROM, LOOP_TO = 8, GROUPS - UNROLL
LN_EPS = 1e-5
RMS_EPS = 1e-6
DEG_EPS = 1e-6

def places(widths):
    at, total = {}, 0
    for name, width in widths:
        at[name] = total
        total += width
    return at, total


WHOLE, WHOLE_WIDE = places([("msg", P), ("theta", P), ("W_h", P), ("W_t", P), ("rel", P), ("root", P),
                            ("W2", CHUNKS * P)])
SPLIT, SPLIT_WIDE = places([("conv1", P), ("se", 96), ("ih", 2 * 3 * P), ("hh", 3 * P), ("W1", HID),
                            ("conv2", TAPS * P)])
CONV2 = slice(SPLIT["conv2"], SPLIT_WIDE)
OTHERS = slice(0, SPLIT["conv2"])
COLUMN = {name: n for n, name in enumerate(
    ["g1", "g2", "b1", "b2", "m1", "m2", "v1", "v2", "ih_r", "ih_z", "ih_n", "hh_r", "hh_z", "hh_n",
     "se", "gamma", "beta", "eps", "h0", "h1", "h2", "h3", "w0", "w1", "w2", "w3"])}
ROW = {"msg": 0, "b_t": 1, "rel": 2, "out": 3}


class Group:

    def __init__(self, loop, n):
        self.loop, self.n = loop, n
        self.real = loop is not None or 0 <= n < GROUPS
        self.first = loop is None and n == 0

    def at(self):
        return self.n if self.loop is None else self.loop.first + self.n

    def __mod__(self, places):
        return self.n % places

    def past(self, back):
        return self.loop is not None or self.n >= back

    def upto(self, back=0):
        count = self.n - back + 1
        return min(count, GROUPS) if self.loop is None else self.loop.plus[count]

    def steps(self, step, back=0):
        count = 2 * (self.n - back) + step
        return count if self.loop is None else self.loop.first * 2 + count

    def transfers(self, places, back=0):
        count = 16 * ((self.n - back) // places + 1)
        return count if self.loop is None else self.loop.first * (16 // places) + count


class Loop:

    def __init__(self, engine, first):
        self.first = first
        self.plus = {n: engine.snap(first + n) for n in range(-LAG["C"] - 1, UNROLL + 1)}


class Turn:

    def __init__(self, loop, t):
        self.N, self.A1, self.A2, self.B1, self.B2, self.C = (Group(loop, t - LAG[s]) for s in LAG)
        self.next_x = Group(loop, t - LAG["N"] + 1)
        self.next_adj = Group(loop, t - LAG["A2"] + 1)
        self.next_rows = Group(loop, t - LAG["B1"] + 1)


def turns(engine, turn):
    for t in range(LOOP_FROM):
        turn(Turn(None, t))
    with engine.Fori(0, (LOOP_TO - LOOP_FROM) // UNROLL, 1) as body:
        loop = Loop(engine, engine.snap(body * UNROLL + LOOP_FROM))
        for t in range(UNROLL):
            turn(Turn(loop, t))
    for t in range(LOOP_TO, TURNS):
        turn(Turn(None, t))


def graph_layers(nc, d_x, d_adj, d_adj_rows, d_weights, d_split, d_columns, d_rows, d_out):
    with ExitStack() as ctx:
        def sb(name, shape, dtype=F32):
            return ctx.enter_context(nc.sbuf_tensor(name, shape, dtype))

        def signal(name):
            return ctx.enter_context(nc.semaphore(name))

        def ring(name, places, shape=(P, PER, P), dtype=F32):
            return [sb(f"{name}_{n}", list(shape), dtype) for n in range(places)]

        def signals(name, n):
            return [signal(f"{name}_{k}") for k in range(n)]

        weights = sb("weights", [P, WHOLE_WIDE])
        weights_hi = sb("weights_hi", [P, SPLIT_WIDE], F32R)
        weights_lo = sb("weights_lo", [P, SPLIT_WIDE], F32R)
        hom_het_hi = sb("hom_het_hi", [P, 2 * P], F32R)
        hom_het_lo = sb("hom_het_lo", [P, 2 * P], F32R)
        rel_root_hi = sb("rel_root_hi", [P, 2 * P], F32R)
        rel_root_lo = sb("rel_root_lo", [P, 2 * P], F32R)
        pairs_hi = sb("pairs_hi", [P, PAIRS, P], F32R)
        pairs_lo = sb("pairs_lo", [P, PAIRS, P], F32R)
        columns = sb("columns", [P, len(COLUMN)])
        rows = sb("rows", [P, len(ROW), P])
        identity = sb("identity", [P, P])
        eps_identity = sb("eps_identity", [P, P])
        ones = sb("ones", [P, P])
        minus_half = sb("minus_half", [P, PER])
        bn_var = sb("bn_var", [P, 2])
        bn_root = sb("bn_root", [P, 2])
        bn_scale = sb("bn_scale", [P, 2])
        bn_mean = sb("bn_mean", [P, 2])
        bn_bias = sb("bn_bias", [P, 2])
        norm2_bias = sb("norm2_bias", [P, PER])
        norm3_bias = sb("norm3_bias", [P, PER])
        minus_scale2 = sb("minus_scale2", [P, 1])
        gate_sum = sb("gate_sum", [P, 2])
        gate_bias = sb("gate_bias", [P, 2])
        half_rms = sb("half_rms", [P, CHUNKS])

        def weight(name, width=P, skip=0):
            return weights[:, WHOLE[name] + skip:WHOLE[name] + skip + width]

        def column(name, parts=P, first=0, n=1):
            return columns[first:first + parts, COLUMN[name]:COLUMN[name] + n]

        def row(name):
            return rows[:, ROW[name], :].unsqueeze(1).to_broadcast([P, PER, P])

        x_in = ring("x_in", 4)
        adj = ring("adj", 4)
        h0n = sb("h0n", [P, PER, P])
        h0 = ring("h0", 2)
        h0_hi = ring("h0_hi", 2, dtype=F32R)
        h0_lo = ring("h0_lo", 2, dtype=F32R)
        c1_hi = sb("c1_hi", [P, 2 * PER, BEFORE + HALF + REACH], F32R)
        c1_lo = sb("c1_lo", [P, 2 * PER, BEFORE + HALF + REACH], F32R)
        pair_hi = sb("pair_hi", [P, PER, REACH + HALF + REACH], F32R)
        pair_lo = sb("pair_lo", [P, PER, REACH + HALF + REACH], F32R)
        left = sb("left", [96, PER, P])
        right = sb("right", [96, PER, P])
        message = ring("message", 2)
        x1 = sb("x1", [P, PER, P])
        x2 = sb("x2", [P, PER, P])
        x3 = sb("x3", [P, PER, P])
        result = sb("result", [P, PER, P])
        c1 = sb("c1", [P, 2 * PER, HALF])
        pair = sb("pair", [P, PER, HALF])
        odd_conv = sb("odd_conv", [P, PER, HALF + 2])
        masked = sb("masked", [P, PER, P])
        nmp_hi = sb("nmp_hi", [P, PER, P], F32R)
        nmp_lo = sb("nmp_lo", [P, PER, P], F32R)
        conv_sum = sb("conv_sum", [P, PER, P])
        conv_sum_parts = conv_sum[:, :, :].rearrange("p b (j s) -> p s b j", s=2)
        x_conv_hi = sb("x_conv_hi", [P, PER, P], F32R)
        x_conv_lo = sb("x_conv_lo", [P, PER, P], F32R)
        candidate = sb("candidate", [P, PER, P])
        gate_z = sb("gate_z", [P, PER, P])
        h_less_n = sb("h_less_n", [P, PER, P])
        gru = sb("gru", [P, PER, P])
        h1n = sb("h1n", [P, PER, P])
        h1 = sb("h1", [P, PER, P])
        h1_hi = sb("h1_hi", [P, PER, P], F32R)
        h1_lo = sb("h1_lo", [P, PER, P], F32R)
        adj_rows = sb("adj_rows", [P, PER, P])
        row_sum = sb("row_sum", [P, PER])
        degree = sb("degree", [P, PER])
        deg_scale = sb("deg_scale", [P, PER])
        f_hom = sb("f_hom", [P, PER, P])
        f_het = sb("f_het", [P, PER, P])
        gate_tanh = sb("gate_tanh", [P, PER, P])
        hom = sb("hom", [P, PER, P])
        mix = sb("mix", [P, PER, P])
        elu_pos = sb("elu_pos", [P, PER, P])
        elu_neg = sb("elu_neg", [P, PER, P])
        h2 = sb("h2", [P, PER, P])
        h2nn = sb("h2nn", [P, PER, P])
        h2_col_hi = sb("h2_col_hi", [P, PER, P], F32R)
        h2_col_lo = sb("h2_col_lo", [P, PER, P], F32R)
        rel = sb("rel", [P, PER, P])
        h2_col = rel
        x2_h2 = sb("x2_h2", [P, PER, P])
        h3 = sb("h3", [P, PER, P])
        adj_eps = sb("adj_eps", [P, PER, P])
        agg_hi = sb("agg_hi", [P, PER, P], F32R)
        agg_lo = sb("agg_lo", [P, PER, P], F32R)
        perceptron = sb("perceptron", [P, 2 * CHUNKS * PER * P])
        weights_raw = perceptron[:, 0:SPLIT_WIDE]
        halves = perceptron[:, :].rearrange("p (k b n) -> p k b n", k=2 * CHUNKS, b=PER)
        square = [halves[:, c, :, :] for c in range(CHUNKS)]
        hidden = [halves[:, CHUNKS + c, :, :] for c in range(CHUNKS)]
        mean_square = sb("mean_square", [P, PER])
        rms_scale = sb("rms_scale", [P, PER])
        rms_scale_hi = sb("rms_scale_hi", [P, PER], F32R)
        rms_scale_lo = sb("rms_scale_lo", [P, PER])
        rms_diag_hi = sb("rms_diag_hi", [P, PER, P], F32R)
        rms_diag_lo = sb("rms_diag_lo", [P, PER, P], F32R)
        rms_wide = sb("rms_wide", [P, PER, P])
        silu = ring("silu", CHUNKS)
        x3_b2 = sb("x3_b2", [P, PER, P])
        pairs = [silu[0], silu[1]]

        bank = [ctx.enter_context(nc.psum_tensor(f"bank_{n}", [P, PER, P], F32)) for n in range(8)]

        conv_bank = bank[2][:, :, :].rearrange("p (s c) n -> p s (c n)", s=2).rearrange("p s (b j) -> p s b j", b=PER)

        weights_loaded, conv2_loaded = signal("weights_loaded"), signal("conv2_loaded")
        act_setup = signal("act_setup")
        pool_setup = signal("pool_setup")
        dve_setup = signal("dve_setup")
        dve_held, pool_held = signal("dve_held"), signal("pool_held")
        x_loaded = signals("x_loaded", 4)
        adj_loaded = signals("adj_loaded", 4)
        rows_loaded = signal("rows_loaded")
        stored = signal("stored")

        class Norm:

            def __init__(self, name):
                self.stats = sb(f"{name}_stats", [P, PER, 6])
                self.moments = sb(f"{name}_moments", [P, PER, 2])
                self.scale = sb(f"{name}_scale", [P, PER])
                self.stats_ready = signal(f"{name}_stats_ready")
                self.moments_ready = signal(f"{name}_moments_ready")
                self.scale_steps = signal(f"{name}_scale_steps")
                self.normed = signal(f"{name}_normed")

        norm0, norm1, norm2, norm2b, norm3 = (Norm(f"norm{n}") for n in ("0", "1", "2", "2b", "3"))

        h0_turned, h0_ready, h0_lo_ready = signal("h0_turned"), signal("h0_ready"), signal("h0_lo_ready")
        conv1_done, c1_ready = signal("conv1_done"), signal("c1_ready")
        c1_hi_ready, c1_lo_ready = signal("c1_hi_ready"), signal("c1_lo_ready")
        pair_ready, pair_hi_ready, pair_lo_ready = signal("pair_ready"), signal("pair_hi_ready"), signal("pair_lo_ready")
        se_done, left_ready, right_ready = signal("se_done"), signal("left_ready"), signal("right_ready")
        message_done, message_summed, message_ready = signal("message_done"), signal("message_summed"), signal("message_ready")
        dist_done, affinity_ready, masked_ready = signal("dist_done"), signal("affinity_ready"), signal("masked_ready")
        nmp_done, nmp_hi_ready, nmp_lo_ready = signal("nmp_done"), signal("nmp_hi_ready"), signal("nmp_lo_ready")
        x_conv_lo_ready = signal("x_conv_lo_ready")
        odd_conv_done, even_conv_done, conv2_done = signal("odd_conv_done"), signal("even_conv_done"), signal("conv2_done")
        odd_conv_ready, odd_conv_added = signal("odd_conv_ready"), signal("odd_conv_added")
        conv_sum_steps = signal("conv_sum_steps")
        x_conv_ready = signal("x_conv_ready")
        r_done, z_done, input_n_done = signal("r_done"), signal("z_done"), signal("input_n_done")
        tanh_r_ready, gate_r_ready, tanh_z_ready, gate_z_ready = signal("tanh_r_ready"), signal("gate_r_ready"), signal("tanh_z_ready"), signal("gate_z_ready")
        r_hidden_ready, n_summed, n_ready = signal("r_hidden_ready"), signal("n_summed"), signal("n_ready")
        h_less_n_ready, z_part_ready, gru_ready = signal("h_less_n_ready"), signal("z_part_ready"), signal("gru_ready")
        gru_turned, x1_ready = signal("gru_turned"), signal("x1_ready")
        rows_summed, degree_ready, deg_scale_ready = signal("rows_summed"), signal("degree_ready"), signal("deg_scale_ready")
        h1_turned, h1_ready = signal("h1_turned"), signal("h1_ready")
        h1_lo_ready, hom_het_done, gate_done = signal("h1_lo_ready"), signal("hom_het_done"), signal("gate_done")
        f_hom_ready, f_het_ready, gate1_summed, gate1_ready = signal("f_hom_ready"), signal("f_het_ready"), signal("gate1_summed"), signal("gate1_ready")
        hom_done, hom_ready, difference_ready, gated_ready, mix_ready = signal("hom_done"), signal("hom_ready"), signal("difference_ready"), signal("gated_ready"), signal("mix_ready")
        elu_pos_ready, elu_exp_ready, elu_neg_ready, x2_ready = signal("elu_pos_ready"), signal("elu_exp_ready"), signal("elu_neg_ready"), signal("x2_ready")
        h2_ready, h2_turned = signal("h2_ready"), signal("h2_turned")
        h2_col_ready, h2_col_lo_ready = signal("h2_col_ready"), signal("h2_col_lo_ready")
        rel_done, rel_ready, conv_rel_done = signal("rel_done"), signal("rel_ready"), signal("conv_rel_done")
        x2_h2_ready, conv_rel_ready, x3_ready = signal("x2_h2_ready"), signal("conv_rel_ready"), signal("x3_ready")
        h3_ready, adj_eps_ready, agg_done = signal("h3_ready"), signal("adj_eps_ready"), signal("agg_done")
        agg_hi_ready, agg_lo_ready = signal("agg_hi_ready"), signal("agg_lo_ready")
        hidden_done, square_ready, hidden_ready = signals("hidden_done", CHUNKS), signals("square_ready", CHUNKS), signals("hidden_ready", CHUNKS)
        square_summed, rms_done, mean_square_ready, rms_scale_ready = signals("square_summed", 3), signal("rms_done"), signal("mean_square_ready"), signal("rms_scale_ready")
        rms_scale_hi_ready, rms_scale_lo_ready = signal("rms_scale_hi_ready"), signal("rms_scale_lo_ready")
        rms_diag_ready, rms_diag_lo_ready = signal("rms_diag_ready"), signal("rms_diag_lo_ready")
        rms_wide_done, rms_wide_ready = signal("rms_wide_done"), signal("rms_wide_ready")
        scaled_ready, silu_tanh_ready, silu_ready = signals("scaled_ready", CHUNKS), signals("silu_tanh_ready", CHUNKS), signals("silu_ready", CHUNKS)
        x3_b2_ready, out_done, result_ready = signal("x3_b2_ready"), signal("out_done"), signal("result_ready")

        block = ctx.enter_context(nc.Block())

        @block.sync
        def _(sp):
            sp.dma_start(columns[:, :], d_columns).then_inc(weights_loaded, 16)
            sp.dma_start(weights_raw[:, OTHERS], d_split[:, OTHERS]).then_inc(weights_loaded, 16)
            sp.dma_start(weights[:, :], d_weights).then_inc(weights_loaded, 16)
            sp.dma_start(rows[:, :, :], d_rows.partition_broadcast(P)).then_inc(weights_loaded, 16)
            sp.dma_start(x_in[0][:, :, :], d_x[:, 0, :, :]).then_inc(x_loaded[0], 16)

            def turn(t):
                if t.next_x.real:
                    if t.next_x.past(4): sp.wait_ge(x1_ready, t.next_x.upto(4))
                    sp.dma_start(x_in[t.next_x % 4][:, :, :],
                                 d_x[:, t.next_x.at(), :, :]).then_inc(x_loaded[t.next_x % 4], 16)
                if t.N.first:
                    sp.dma_start(weights_raw[:, CONV2], d_split[:, CONV2]).then_inc(conv2_loaded, 16)
                if t.next_adj.real:
                    if t.next_adj.past(4): sp.wait_ge(conv_rel_done, t.next_adj.upto(4))
                    if t.next_adj.past(4): sp.wait_ge(adj_eps_ready, t.next_adj.upto(4))
                    sp.dma_start(adj[t.next_adj % 4][:, :, :],
                                 d_adj[:, t.next_adj.at(), :, :]).then_inc(adj_loaded[t.next_adj % 4], 16)
                if t.next_rows.real:
                    if t.next_rows.past(1): sp.wait_ge(rows_summed, t.next_rows.upto(1))
                    sp.dma_start(adj_rows[:, :, :], d_adj_rows[:, t.next_rows.at(), :, :]).then_inc(rows_loaded, 16)
                if t.C.real:
                    if t.C.past(0): sp.wait_ge(result_ready, t.C.upto())
                    sp.dma_start(d_out[:, t.C.at(), :, :],
                                 result[:, :, :]).then_inc(stored, 16)

            turns(sp, turn)
            sp.wait_ge(stored, 16 * GROUPS)

        @block.tensor
        def _(pe):
            pe.wait_ge(dve_setup, PREPARED)

            def per_graph(out, lhs, rhs, start=True, stop=True):
                for b in range(PER):
                    last = pe.matmul(out[:, b, :], lhs(b), rhs(b), start=start and b == 0, stop=stop,
                                     skip_group_check=True)
                return last

            def turned(out, tile):
                for b in range(PER):
                    last = pe.transpose(out[:, b, :], tile[:, b, :], identity[:, :])
                return last

            def parts_product(out, a_hi, a_lo, hi, lo, start, stop):
                pe.matmul(out, a_hi, hi, start=start, stop=False, skip_group_check=True)
                pe.matmul(out, a_hi, lo, start=False, stop=False, skip_group_check=True)
                return pe.matmul(out, a_lo, hi, start=False, stop=stop, skip_group_check=True)

            def split_product(out, name, skip, hi, lo, start=True, stop=True, width=P):
                part = slice(SPLIT[name] + skip, SPLIT[name] + skip + width)
                return parts_product(out, weights_hi[:, part], weights_lo[:, part], hi, lo, start, stop)

            def two_products(out, hi, lo, pair_weights_hi, pair_weights_lo, first):
                for b in range(2):
                    last = parts_product(out[:, 2 * b:2 * b + 2, :], hi[:, first + b, :], lo[:, first + b, :],
                                         pair_weights_hi[:, :], pair_weights_lo[:, :], start=(b == 0), stop=(b == 1))
                return last

            def tap(k):
                return (k + TAPS // 2) * P

            def odd_conv_taps(out, steps):
                for k in steps:
                    a = k - REACH + 1
                    nodes = slice(BEFORE - 2 + a, BEFORE + HALF + a)
                    last = split_product(out, "conv2", tap(2 * a - 1), c1_hi[:, PER:2 * PER, nodes],
                                         c1_lo[:, PER:2 * PER, nodes], start=(k == 0), stop=(k == 2 * REACH - 1))
                return last

            def even_conv_taps(steps):
                for k in steps:
                    a = k - REACH
                    nodes = slice(BEFORE + a, BEFORE + HALF + a)
                    last = split_product(conv_bank[:, 0, :, :], "conv2", tap(2 * a), c1_hi[:, 0:PER, nodes],
                                         c1_lo[:, 0:PER, nodes], start=(k == 0), stop=(k == 2 * REACH))
                return last

            def pair_conv_taps(steps):
                for k in steps:
                    nodes = slice(k, k + HALF)
                    if k == 0:
                        last = split_product(conv_bank[:, 1, :, :], "conv2", tap(-2 * REACH), pair_hi[:, :, nodes],
                                             pair_lo[:, :, nodes], start=False, stop=False)
                    else:
                        last = parts_product(conv_bank[:, 1, :, :], pairs_hi[:, k - 1, :], pairs_lo[:, k - 1, :],
                                             pair_hi[:, :, nodes], pair_lo[:, :, nodes], start=False, stop=(k == 2 * REACH))
                return last

            def turn(t):
                g = t.A2
                if g.real:
                    if g.first: pe.wait_ge(pool_setup, CONV2_READY)
                    pe.wait_ge(c1_hi_ready, g.upto())
                    pe.wait_ge(c1_lo_ready, g.upto())
                    if t.B2.past(1): pe.wait_ge(conv_rel_ready, t.B2.upto(1))
                    if t.B1.past(1): pe.wait_ge(f_het_ready, t.B1.upto(1))
                    if g.past(1): pe.wait_ge(odd_conv_ready, g.upto(1))
                    odd_conv_taps(bank[6][:, :, 0:HALF + 2], range(0, 8)).then_inc(odd_conv_done, 1)
                    if g.past(1): pe.wait_ge(conv_sum_steps, g.steps(2, 1))
                    even_conv_taps(range(0, 1))
                g = t.A1
                if g.real:
                    pe.wait_ge(norm0.normed, g.upto())
                    if t.A2.past(1): pe.wait_ge(r_hidden_ready, t.A2.upto(1))
                    if g.past(1): pe.wait_ge(message_summed, g.upto(1))
                    turned(bank[3], h0n).then_inc(h0_turned, 1)
                g = t.A2
                if g.real:
                    pe.wait_ge(left_ready, g.upto())
                    pe.wait_ge(right_ready, g.upto())
                    if t.A1.past(1): pe.wait_ge(left_ready, t.A1.upto(1))
                    if t.A1.past(1): pe.wait_ge(right_ready, t.A1.upto(1))
                    per_graph(bank[7], lambda b: left[:, b, :], lambda b: right[:, b, :]).then_inc(dist_done, 1)
                    even_conv_taps(range(1, 6))
                g = t.B1
                if g.real:
                    pe.wait_ge(gru_ready, g.upto())
                    if t.C.past(1): pe.wait_ge(result_ready, t.C.upto(1))
                    if t.A2.past(1): pe.wait_ge(tanh_r_ready, t.A2.upto(1))
                    turned(bank[5], gru).then_inc(gru_turned, 1)
                g = t.A2
                if g.real:
                    even_conv_taps(range(6, 9)).then_inc(even_conv_done, 1)
                    pe.wait_ge(pair_hi_ready, g.upto())
                    pe.wait_ge(pair_lo_ready, g.upto())
                    pair_conv_taps(range(0, 2))
                g = t.C
                if g.real:
                    pe.wait_ge(h3_ready, g.upto())
                    pe.wait_ge(adj_eps_ready, g.upto())
                    if t.B2.past(1): pe.wait_ge(conv_rel_ready, t.B2.upto(1))
                    per_graph(bank[1], lambda b: h3[:, b, :], lambda b: adj_eps[:, b, :]).then_inc(agg_done, 1)
                g = t.A2
                if g.real:
                    pair_conv_taps(range(2, 3))
                    pe.wait_ge(masked_ready, g.upto())
                    pe.wait_ge(message_ready, g.upto())
                    if g.past(1): pe.wait_ge(n_summed, g.upto(1))
                    per_graph(bank[0], lambda b: message[g % 2][:, b, :], lambda b: masked[:, b, :]).then_inc(nmp_done, 1)
                g = t.A1
                if g.real:
                    pe.wait_ge(h0_ready, g.upto())
                    pe.wait_ge(h0_lo_ready, g.upto())
                    if t.B1.past(0): pe.wait_ge(x1_ready, t.B1.upto())
                    if g.past(1): pe.wait_ge(c1_ready, g.upto(1))
                    split_product(bank[5][:, :, :], "conv1", 0, h0_hi[g % 2][:, :, :], h0_lo[g % 2][:, :, :]).then_inc(conv1_done, 1)
                g = t.C
                if g.real:
                    pe.wait_ge(agg_hi_ready, g.upto())
                    pe.wait_ge(agg_lo_ready, g.upto())
                    if t.A2.past(0): pe.wait_ge(affinity_ready, t.A2.upto())
                    if g.past(1): pe.wait_ge(hidden_ready[1], g.upto(1))
                    split_product(bank[7][:, :, :], "W1", P, agg_hi[:, :, :], agg_lo[:, :, :]).then_inc(hidden_done[1], 1)
                    pe.wait_ge(agg_hi_ready, g.upto())
                    pe.wait_ge(agg_lo_ready, g.upto())
                    if t.A2.past(0): pe.wait_ge(odd_conv_ready, t.A2.upto())
                    if t.B2.past(1): pe.wait_ge(conv_rel_ready, t.B2.upto(1))
                    split_product(bank[6][:, :, :], "W1", 0, agg_hi[:, :, :], agg_lo[:, :, :]).then_inc(hidden_done[0], 1)
                g = t.A1
                if g.real:
                    pe.wait_ge(h0_ready, g.upto())
                    pe.wait_ge(h0_ready, g.upto())
                    per_graph(bank[3], lambda b: h0[g % 2][:, b, :], lambda b: weight("msg")).then_inc(message_done, 1)
                g = t.C
                if g.real:
                    pe.wait_ge(agg_hi_ready, g.upto())
                    pe.wait_ge(agg_lo_ready, g.upto())
                    if t.A2.past(1): pe.wait_ge(tanh_z_ready, t.A2.upto(1))
                    if g.past(1): pe.wait_ge(hidden_ready[2], g.upto(1))
                    split_product(bank[4][:, :, :], "W1", 2 * P, agg_hi[:, :, :], agg_lo[:, :, :]).then_inc(hidden_done[2], 1)
                    pe.wait_ge(agg_hi_ready, g.upto())
                    pe.wait_ge(agg_lo_ready, g.upto())
                    pe.wait_ge(agg_lo_ready, g.upto())
                    split_product(bank[1][:, :, :], "W1", 3 * P, agg_hi[:, :, :], agg_lo[:, :, :]).then_inc(hidden_done[3], 1)
                g = t.B1
                if g.real:
                    pe.wait_ge(norm1.normed, g.upto())
                    if t.A1.past(0): pe.wait_ge(c1_ready, t.A1.upto())
                    pe.wait_ge(x1_ready, g.upto())
                    turned(bank[5], h1n).then_inc(h1_turned, 1)
                g = t.A2
                if g.real:
                    pair_conv_taps(range(3, 8))
                g = t.B2
                if g.real:
                    pe.wait_ge(norm2b.normed, g.upto())
                    if t.B1.past(0): pe.wait_ge(h1_ready, t.B1.upto())
                    if t.C.past(1): pe.wait_ge(result_ready, t.C.upto(1))
                    turned(bank[5], h2nn).then_inc(h2_turned, 1)
                g = t.A2
                if g.real:
                    pair_conv_taps(range(8, 9)).then_inc(conv2_done, 1)
                g = t.B1
                if g.real:
                    pe.wait_ge(h1_ready, g.upto())
                    pe.wait_ge(h1_lo_ready, g.upto())
                    if t.A2.past(0): pe.wait_ge(nmp_lo_ready, t.A2.upto())
                    if t.A2.past(1): pe.wait_ge(n_summed, t.A2.upto(1))
                    two_products(bank[0], h1_hi, h1_lo, hom_het_hi, hom_het_lo, 0)
                    if t.C.past(0): pe.wait_ge(hidden_ready[0], t.C.upto())
                    if t.A2.past(0): pe.wait_ge(odd_conv_ready, t.A2.upto())
                    two_products(bank[6], h1_hi, h1_lo, hom_het_hi, hom_het_lo, 2).then_inc(hom_het_done, 1)
                g = t.C
                if g.real:
                    pe.wait_ge(square_summed[2], g.upto())
                    pe.wait_ge(hidden_ready[3], g.upto())
                    for b in range(PER):
                        last = pe.matmul(bank[1][:, 0, b:b + 1], square[0][:, b, :], ones[:, 0:1],
                                         start=True, stop=True, skip_group_check=True)
                    last.then_inc(rms_done, 1)
                g = t.A1
                if g.real:
                    pe.wait_ge(h0_ready, g.upto())
                    pe.wait_ge(h0_lo_ready, g.upto())
                    if t.C.past(0): pe.wait_ge(hidden_ready[1], t.C.upto())
                    if t.A2.past(0): pe.wait_ge(affinity_ready, t.A2.upto())
                    split_product(bank[7][0:96, :, :], "se", 0, h0_hi[g % 2][:, :, :], h0_lo[g % 2][:, :, :],
                                  width=96).then_inc(se_done, 1)
                g = t.B1
                if g.real:
                    pe.wait_ge(h1_ready, g.upto())
                    if t.A1.past(0): pe.wait_ge(message_summed, t.A1.upto())
                    if t.A2.past(1): pe.wait_ge(r_hidden_ready, t.A2.upto(1))
                    per_graph(bank[3], lambda b: h1[:, b, :], lambda b: weight("W_t")).then_inc(gate_done, 1)
                    pe.wait_ge(f_hom_ready, g.upto())
                    if t.C.past(0): pe.wait_ge(mean_square_ready, t.C.upto())
                    if g.past(1): pe.wait_ge(hom_ready, g.upto(1))
                    per_graph(bank[1], lambda b: adj[g % 4][:, b, :], lambda b: f_hom[:, b, :]).then_inc(hom_done, 1)
                g = t.A2
                if g.real:
                    if t.C.past(0): pe.wait_ge(hidden_ready[2], t.C.upto())
                    if g.past(1): pe.wait_ge(tanh_z_ready, g.upto(1))
                    split_product(bank[4][:, :, :], "hh", P, h0_hi[g % 2][:, :, :], h0_lo[g % 2][:, :, :], stop=False)
                    pe.wait_ge(nmp_hi_ready, g.upto())
                    pe.wait_ge(nmp_lo_ready, g.upto())
                    split_product(bank[4][:, :, :], "ih", 4 * P, nmp_hi[:, :, :], nmp_lo[:, :, :], start=False, stop=False)
                    if t.B1.past(0): pe.wait_ge(gate1_summed, t.B1.upto())
                    if t.A1.past(0): pe.wait_ge(message_summed, t.A1.upto())
                    split_product(bank[3][:, :, :], "hh", 2 * P, h0_hi[g % 2][:, :, :], h0_lo[g % 2][:, :, :])
                g = t.B2
                if g.real:
                    pe.wait_ge(h2_col_ready, g.upto())
                    pe.wait_ge(h2_col_lo_ready, g.upto())
                    if t.B1.past(0): pe.wait_ge(hom_ready, t.B1.upto())
                    if t.C.past(0): pe.wait_ge(mean_square_ready, t.C.upto())
                    two_products(bank[1], h2_col_hi, h2_col_lo, rel_root_hi, rel_root_lo, 0)
                g = t.C
                if g.real:
                    pe.wait_ge(rms_diag_ready, g.upto())
                    pe.wait_ge(rms_diag_lo_ready, g.upto())
                    if t.B1.past(0): pe.wait_ge(f_het_ready, t.B1.upto())
                    if g.past(1): pe.wait_ge(rms_wide_ready, g.upto(1))
                    pe.matmul(bank[0][:, :, :], ones[:, :].bitcast(F32R), rms_diag_hi[:, :, :], start=True, stop=False,
                              skip_group_check=True)
                    pe.matmul(bank[0][:, :, :], ones[:, :].bitcast(F32R), rms_diag_lo[:, :, :], start=False, stop=True,
                              skip_group_check=True).then_inc(rms_wide_done, 1)
                g = t.B2
                if g.real:
                    if t.B1.past(0): pe.wait_ge(f_het_ready, t.B1.upto())
                    if t.C.past(0): pe.wait_ge(hidden_ready[0], t.C.upto())
                    two_products(bank[6], h2_col_hi, h2_col_lo, rel_root_hi, rel_root_lo, 2).then_inc(rel_done, 1)
                g = t.A2
                if g.real:
                    if t.B2.past(0): pe.wait_ge(h2_col_ready, t.B2.upto())
                    if t.B1.past(0): pe.wait_ge(h1_ready, t.B1.upto())
                    if t.A1.past(0): pe.wait_ge(c1_ready, t.A1.upto())
                    split_product(bank[5][:, :, :], "hh", 0, h0_hi[g % 2][:, :, :], h0_lo[g % 2][:, :, :], stop=False)
                    pe.wait_ge(nmp_hi_ready, g.upto())
                    pe.wait_ge(nmp_lo_ready, g.upto())
                    split_product(bank[5][:, :, :], "ih", 3 * P, nmp_hi[:, :, :], nmp_lo[:, :, :], start=False, stop=False)
                    pe.wait_ge(x_conv_ready, g.upto())
                    pe.wait_ge(x_conv_lo_ready, g.upto())
                    split_product(bank[5][:, :, :], "ih", 0, x_conv_hi[:, :, :], x_conv_lo[:, :, :], start=False).then_inc(r_done, 1)
                g = t.B2
                if g.real:
                    pe.wait_ge(rel_ready, g.upto())
                    for b in range(PER):
                        last = pe.matmul((bank[1], bank[6])[b // 2][:, b % 2 * 2 + 1, :], adj[g % 4][:, b, :], rel[:, b, :],
                                         start=False, stop=True, skip_group_check=True)
                    last.then_inc(conv_rel_done, 1)
                g = t.A2
                if g.real:
                    pe.wait_ge(nmp_hi_ready, g.upto())
                    pe.wait_ge(nmp_lo_ready, g.upto())
                    if t.C.past(0): pe.wait_ge(rms_wide_ready, t.C.upto())
                    if t.B1.past(0): pe.wait_ge(f_het_ready, t.B1.upto())
                    pe.wait_ge(nmp_lo_ready, g.upto())
                    split_product(bank[0][:, :, :], "ih", 5 * P, nmp_hi[:, :, :], nmp_lo[:, :, :], stop=False)
                g = t.C
                if g.real:
                    pe.wait_ge(silu_ready[0], g.upto())
                    if t.A2.past(0): pe.wait_ge(tanh_r_ready, t.A2.upto())
                    if t.B2.past(0): pe.wait_ge(h2_col_ready, t.B2.upto())
                    if g.past(1): pe.wait_ge(result_ready, g.upto(1))
                    per_graph(bank[5], lambda b: silu[0][:, b, :], lambda b: weight("W2", P, 0), stop=False)
                g = t.A2
                if g.real:
                    pe.wait_ge(x_conv_ready, g.upto())
                    pe.wait_ge(x_conv_lo_ready, g.upto())
                    split_product(bank[0][:, :, :], "ih", 2 * P, x_conv_hi[:, :, :], x_conv_lo[:, :, :], start=False).then_inc(input_n_done, 1)
                    pe.wait_ge(x_conv_ready, g.upto())
                    pe.wait_ge(x_conv_lo_ready, g.upto())
                    split_product(bank[4][:, :, :], "ih", P, x_conv_hi[:, :, :], x_conv_lo[:, :, :], start=False).then_inc(z_done, 1)
                g = t.C
                if g.real:
                    pe.wait_ge(silu_ready[1], g.upto())
                    per_graph(bank[5], lambda b: silu[1][:, b, :], lambda b: weight("W2", P, P), start=False, stop=False)
                    pe.wait_ge(silu_ready[2], g.upto())
                    per_graph(bank[5], lambda b: silu[2][:, b, :], lambda b: weight("W2", P, 2 * P), start=False, stop=False)
                    pe.wait_ge(silu_ready[3], g.upto())
                    per_graph(bank[5], lambda b: silu[3][:, b, :], lambda b: weight("W2", P, 3 * P), start=False).then_inc(out_done, 1)

            turns(pe, turn)

        @block.scalar
        def _(act):
            act.wait_ge(conv2_loaded, 16)
            act.activation(weights_hi[:, CONV2], weights_raw[:, CONV2], ACT.Copy).then_inc(act_setup, 1)
            act.wait_ge(pool_setup, 6)
            for n in range(2):
                act.activation(pairs_hi[:, n * PER:(n + 1) * PER, :], pairs[n][:, :, :], ACT.Copy).then_inc(act_setup, 1)
            act.wait_ge(dve_setup, PREPARED)

            def turn(t):
                g = t.A2
                if g.real:
                    act.wait_ge(odd_conv_done, g.upto())
                    if g.past(1): act.wait_ge(odd_conv_added, g.upto(1))
                    act.activation(odd_conv[:, :, :], bank[6][:, :, 0:HALF + 2], ACT.Identity, scale=bn_scale[:, 1:2]).then_inc(odd_conv_ready, 1)
                g = t.B1
                if g.real:
                    act.wait_ge(rows_loaded, g.transfers(1))
                    if g.past(1): act.wait_ge(degree_ready, g.upto(1))
                    for b in range(PER):
                        last = act.activation(adj_rows[:, b, :], adj_rows[:, b, :], ACT.Copy, accum_out=row_sum[:, b:b + 1])
                    last.then_inc(rows_summed, 1)
                g = t.A2
                if g.real:
                    act.wait_ge(dist_done, g.upto())
                    if g.past(1): act.wait_ge(nmp_done, g.upto(1))
                    act.activation(masked[:, :, :], bank[7][:, :, :], ACT.Exp).then_inc(affinity_ready, 1)
                g = t.A1
                if g.real:
                    act.wait_ge(h0_turned, g.upto())
                    if g.past(2): act.wait_ge(z_done, g.upto(2))
                    if g.past(2): act.wait_ge(h_less_n_ready, g.upto(2))
                    act.activation(h0_hi[g % 2][:, :, :], bank[3][:, :, :], ACT.Relu)
                    act.activation(h0[g % 2][:, :, :], bank[3][:, :, :], ACT.Relu).then_inc(h0_ready, 1)
                g = t.C
                if g.real:
                    act.wait_ge(norm3.normed, g.upto())
                    if g.past(1): act.wait_ge(agg_done, g.upto(1))
                    for b in range(PER):
                        last = act.activation(h3[:, b, :], x3[:, b, :], ACT.Relu, bias=norm3_bias[:, b:b + 1],
                                              scale=norm3.scale[:, b:b + 1])
                    last.then_inc(h3_ready, 1)
                g = t.B2
                if g.real:
                    act.wait_ge(norm2.normed, g.upto())
                    if g.past(1): act.wait_ge(x2_h2_ready, g.upto(1))
                    if g.past(1): act.wait_ge(h2_turned, g.upto(1))
                    for b in range(PER):
                        last = act.activation(h2[:, b, :], x2[:, b, :], ACT.Relu, bias=norm2_bias[:, b:b + 1],
                                              scale=norm2.scale[:, b:b + 1])
                    last.then_inc(h2_ready, 1)
                g = t.C
                if g.real:
                    act.wait_ge(agg_done, g.upto())
                    if g.past(1): act.wait_ge(hidden_done[CHUNKS - 1], g.upto(1))
                    act.activation(agg_hi[:, :, :], bank[1][:, :, :], ACT.Copy).then_inc(agg_hi_ready, 1)
                g = t.A2
                if g.real:
                    act.wait_ge(nmp_done, g.upto())
                    if g.past(1): act.wait_ge(z_done, g.upto(1))
                    act.activation(nmp_hi[:, :, :], bank[0][:, :, :], ACT.Copy).then_inc(nmp_hi_ready, 1)
                g = t.A1
                if g.real:
                    act.wait_ge(conv1_done, g.upto())
                    if g.past(1): act.wait_ge(pair_ready, g.upto(1))
                    if g.past(1): act.wait_ge(c1_lo_ready, g.upto(1))
                    act.activation(c1[:, :, :].rearrange("p (s b) j -> p s b j", s=2),
                                   bank[5][:, :, :].rearrange("p b (j s) -> p s b j", s=2), ACT.Relu, bias=bn_bias[:, 0:1],
                                   scale=bn_scale[:, 0:1]).then_inc(c1_ready, 1)
                g = t.C
                if g.real:
                    act.wait_ge(hidden_done[1], g.upto())
                    if g.past(1): act.wait_ge(rms_done, g.upto(1))
                    act.activation(square[1][:, :, :], bank[7][:, :, :], ACT.Square,
                                   bias=column("h1")).then_inc(square_ready[1], 1)
                    act.wait_ge(hidden_done[0], g.upto())
                    if g.past(1): act.wait_ge(rms_done, g.upto(1))
                    act.activation(square[0][:, :, :], bank[6][:, :, :], ACT.Square,
                                   bias=column("h0")).then_inc(square_ready[0], 1)
                    act.wait_ge(hidden_done[2], g.upto())
                    if g.past(1): act.wait_ge(rms_done, g.upto(1))
                    act.activation(square[2][:, :, :], bank[4][:, :, :], ACT.Square,
                                   bias=column("h2")).then_inc(square_ready[2], 1)
                    act.wait_ge(hidden_done[3], g.upto())
                    if g.past(1): act.wait_ge(rms_done, g.upto(1))
                    act.activation(square[3][:, :, :], bank[1][:, :, :], ACT.Square,
                                   bias=column("h3")).then_inc(square_ready[3], 1)
                g = t.B1
                if g.real:
                    act.wait_ge(h1_turned, g.upto())
                    if g.past(1): act.wait_ge(gate_done, g.upto(1))
                    if g.past(1): act.wait_ge(hom_het_done, g.upto(1))
                    act.activation(h1_hi[:, :, :], bank[5][:, :, :], ACT.Relu)
                    act.activation(h1[:, :, :], bank[5][:, :, :], ACT.Relu).then_inc(h1_ready, 1)
                g = t.C
                if g.real:
                    act.wait_ge(hidden_done[3], g.upto())
                    if g.past(1): act.wait_ge(silu_ready[3], g.upto(1))
                    act.activation(hidden[3][:, :, :], bank[1][:, :, :], ACT.Identity,
                                   bias=column("h3")).then_inc(hidden_ready[3], 1)
                    act.wait_ge(hidden_done[0], g.upto())
                    if g.past(1): act.wait_ge(silu_ready[0], g.upto(1))
                    act.activation(hidden[0][:, :, :], bank[6][:, :, :], ACT.Identity,
                                   bias=column("h0")).then_inc(hidden_ready[0], 1)
                    act.wait_ge(hidden_done[2], g.upto())
                    if g.past(1): act.wait_ge(silu_ready[2], g.upto(1))
                    act.activation(hidden[2][:, :, :], bank[4][:, :, :], ACT.Identity,
                                   bias=column("h2")).then_inc(hidden_ready[2], 1)
                    act.wait_ge(hidden_done[1], g.upto())
                    if g.past(1): act.wait_ge(silu_ready[1], g.upto(1))
                    act.activation(hidden[1][:, :, :], bank[7][:, :, :], ACT.Identity,
                                   bias=column("h1")).then_inc(hidden_ready[1], 1)
                g = t.B2
                if g.real:
                    act.wait_ge(h2_turned, g.upto())
                    if g.past(1): act.wait_ge(conv_rel_done, g.upto(1))
                    act.activation(h2_col_hi[:, :, :], bank[5][:, :, :], ACT.Identity, bias=column("beta"), scale=column("gamma"))
                    act.activation(h2_col[:, :, :], bank[5][:, :, :], ACT.Identity, bias=column("beta"),
                                   scale=column("gamma")).then_inc(h2_col_ready, 1)
                g = t.A1
                if g.real:
                    act.wait_ge(pair_ready, g.upto())
                    if g.past(1): act.wait_ge(conv2_done, g.upto(1))
                    act.activation(pair_hi[:, :, REACH:REACH + HALF], pair[:, :, :], ACT.Copy).then_inc(pair_hi_ready, 1)
                g = t.B1
                if g.real:
                    act.wait_ge(hom_het_done, g.upto())
                    act.wait_ge(f_hom_ready, g.upto())
                    if g.past(1): act.wait_ge(mix_ready, g.upto(1))
                    act.activation(f_het[:, 0:2, :], bank[0][:, 1:PER:2, :], ACT.Copy)
                    act.activation(f_het[:, 2:4, :], bank[6][:, 1:PER:2, :], ACT.Copy).then_inc(f_het_ready, 1)
                g = t.A2
                if g.real:
                    act.wait_ge(conv_sum_steps, g.steps(2))
                    if g.past(1): act.wait_ge(z_done, g.upto(1))
                    act.activation(x_conv_hi[:, :, :], conv_sum[:, :, :], ACT.Relu, bias=bn_bias[:, 1:2])
                    act.activation(conv_sum[:, :, :], conv_sum[:, :, :], ACT.Relu, bias=bn_bias[:, 1:2]).then_inc(x_conv_ready, 1)
                g = t.B1
                if g.real:
                    act.wait_ge(gate1_summed, g.upto())
                    act.activation(gate_tanh[:, :, :], gate_tanh[:, :, :], ACT.Tanh, scale=0.5).then_inc(gate1_ready, 1)
                g = t.C
                if g.real:
                    act.wait_ge(rms_wide_done, g.upto())
                    if g.past(1): act.wait_ge(scaled_ready[CHUNKS - 1], g.upto(1))
                    act.activation(rms_wide[:, :, :], bank[0][:, :, :], ACT.Copy).then_inc(rms_wide_ready, 1)
                g = t.B2
                if g.real:
                    act.wait_ge(rel_done, g.upto())
                    act.wait_ge(h2_col_lo_ready, g.upto())
                    act.activation(rel[:, 0:2, :], bank[1][:, 0:PER:2, :], ACT.Copy)
                    act.activation(rel[:, 2:4, :], bank[6][:, 0:PER:2, :], ACT.Copy).then_inc(rel_ready, 1)
                g = t.A1
                if g.real:
                    act.wait_ge(message_summed, g.upto())
                    act.activation(message[g % 2][:, :, :], message[g % 2][:, :, :], ACT.Relu).then_inc(message_ready, 1)
                g = t.C
                if g.real:
                    for c in range(2):
                        act.wait_ge(scaled_ready[c], g.upto())
                        if g.past(1): act.wait_ge(out_done, g.upto(1))
                        act.activation(silu[c][:, :, :], hidden[c][:, :, :], ACT.Tanh,
                                       scale=half_rms[:, c:c + 1]).then_inc(silu_tanh_ready[c], 1)
                g = t.A2
                if g.real:
                    act.wait_ge(r_done, g.upto())
                    if g.past(1): act.wait_ge(gru_ready, g.upto(1))
                    act.activation(candidate[:, :, :], bank[5][:, :, :], ACT.Tanh, bias=gate_bias[:, 0:1],
                                   scale=0.5).then_inc(tanh_r_ready, 1)
                g = t.C
                if g.real:
                    act.wait_ge(scaled_ready[2], g.upto())
                    if g.past(1): act.wait_ge(out_done, g.upto(1))
                    act.activation(silu[2][:, :, :], hidden[2][:, :, :], ACT.Tanh,
                                   scale=half_rms[:, 2:2 + 1]).then_inc(silu_tanh_ready[2], 1)
                g = t.B1
                if g.real:
                    act.wait_ge(elu_neg_ready, g.upto())
                    act.activation(elu_neg[:, :, :], elu_neg[:, :, :], ACT.Exp).then_inc(elu_exp_ready, 1)
                g = t.C
                if g.real:
                    act.wait_ge(scaled_ready[3], g.upto())
                    if g.past(1): act.wait_ge(out_done, g.upto(1))
                    act.activation(silu[3][:, :, :], hidden[3][:, :, :], ACT.Tanh,
                                   scale=half_rms[:, 3:3 + 1]).then_inc(silu_tanh_ready[3], 1)
                g = t.A1
                if g.real:
                    act.wait_ge(se_done, g.upto())
                    act.wait_ge(left_ready, g.upto())
                    if g.past(1): act.wait_ge(dist_done, g.upto(1))
                    act.activation(right[0:32, :, :], bank[7][0:32, :, :], ACT.Identity, bias=column("se", 32))
                    act.activation(left[32:64, :, :], bank[7][32:64, :, :], ACT.Square, bias=column("se", 32, 32))
                    act.activation(right[64:96, :, :], bank[7][64:96, :, :], ACT.Square,
                                   bias=column("se", 32, 64)).then_inc(right_ready, 1)
                g = t.A2
                if g.real:
                    act.wait_ge(z_done, g.upto())
                    if g.past(1): act.wait_ge(z_part_ready, g.upto(1))
                    act.activation(gate_z[:, :, :], bank[4][:, :, :], ACT.Tanh, bias=gate_bias[:, 1:2],
                                   scale=0.5).then_inc(tanh_z_ready, 1)
                    act.wait_ge(n_summed, g.upto())
                    act.activation(candidate[:, :, :], candidate[:, :, :], ACT.Tanh, bias=column("ih_n")).then_inc(n_ready, 1)

            turns(act, turn)

        @block.vector
        def _(dve):
            for tile, before in ((c1_hi, BEFORE), (c1_lo, BEFORE), (pair_hi, REACH), (pair_lo, REACH)):
                dve.memset(tile[:, :, 0:before].bitcast(F32), 0.0)
                dve.memset(tile[:, :, before + HALF:before + HALF + REACH].bitcast(F32), 0.0)
            dve.memset(left[64:96, :, :], -1.0)
            dve.memset(right[32:64, :, :], -1.0)
            dve.wait_ge(weights_loaded, 64)
            dve.tensor_scalar(bn_var[:, :], column("v1", n=2), LN_EPS, None, ALU.add).then_inc(dve_setup, 1)
            dve.tensor_tensor(gate_sum[:, :], column("ih_r", n=2), column("hh_r", n=2), ALU.add).then_inc(dve_setup, 1)
            dve.tensor_scalar(half_rms[:, :], column("w0", n=CHUNKS), 0.5, None, ALU.mult).then_inc(dve_setup, 1)
            dve.tensor_copy(hom_het_hi[:, :], weight("theta", 2 * P))
            dve.tensor_copy(rel_root_hi[:, :], weight("rel", 2 * P))
            dve.tensor_copy(weights_hi[:, OTHERS], weights_raw[:, OTHERS]).then_inc(dve_setup, 1)
            dve.wait_ge(dve_setup, 4)
            dve.tensor_scalar(gate_bias[:, :], gate_sum[:, :], 0.5, None, ALU.mult)
            for c in range(CHUNKS):
                dve.tensor_scalar(weight("W2", P, c * P), weight("W2", P, c * P), half_rms[:, c:c + 1], None, ALU.mult)
            dve.tensor_tensor(hom_het_lo[:, :], weight("theta", 2 * P), hom_het_hi[:, :].bitcast(F32), ALU.subtract)
            dve.tensor_tensor(rel_root_lo[:, :], weight("rel", 2 * P), rel_root_hi[:, :].bitcast(F32), ALU.subtract)
            dve.tensor_tensor(weights_lo[:, OTHERS], weights_raw[:, OTHERS], weights_hi[:, OTHERS].bitcast(F32), ALU.subtract)
            dve.wait_ge(pool_setup, 3)
            dve.tensor_scalar(eps_identity[:, :], identity[:, :], column("eps"), None, ALU.mult)
            dve.wait_ge(pool_setup, 4)
            dve.tensor_tensor(bn_scale[:, :], bn_root[:, :], column("g1", n=2), ALU.mult).then_inc(dve_setup, 1)
            dve.wait_ge(dve_setup, 5)
            dve.tensor_scalar(minus_scale2[:, :], bn_scale[:, 1:2], -1.0, None, ALU.mult)
            dve.tensor_tensor(bn_mean[:, :], bn_scale[:, :], column("m1", n=2), ALU.mult).then_inc(dve_setup, 1)
            dve.wait_ge(dve_setup, 6)
            dve.tensor_tensor(bn_bias[:, :], column("b1", n=2), bn_mean[:, :], ALU.subtract).then_inc(dve_setup, 1)
            dve.wait_ge(dve_setup, PREPARED)

            def statistics(norm, tile, g):
                for b in range(PER):
                    last = dve.bn_stats(norm.stats[:, b, :], tile[:, b, :])
                last.then_inc(norm.stats_ready, 1)
                dve.wait_ge(norm.stats_ready, g.upto())
                if g.past(1): dve.wait_ge(norm.scale_steps, g.steps(2, 1))
                dve.sem_inc(dve_held, 1)
                for b in range(PER):
                    last = dve.bn_aggr(norm.moments[:, b, :], norm.stats[:, b, :])
                last.then_inc(norm.moments_ready, 1)

            def normalise(norm, out, tile, g):
                dve.wait_ge(norm.scale_steps, g.steps(2))
                for b in range(PER):
                    last = dve.tensor_scalar(out[:, b, :], tile[:, b, :], norm.moments[:, b, 0:1],
                                             norm.scale[:, b:b + 1], ALU.subtract, ALU.mult)
                last.then_inc(norm.normed, 1)

            def turn(t):
                g = t.C
                if g.real:
                    dve.wait_ge(norm3.scale_steps, g.steps(2))
                    if g.past(1): dve.wait_ge(h3_ready, g.upto(1))
                    dve.scalar_tensor_tensor(out=norm3_bias[:, :], in0=norm3.moments[:, :, 0], scalar=-1.0, in1=norm3.scale[:, :],
                                             op0=ALU.mult, op1=ALU.mult).then_inc(norm3.normed, 1)
                g = t.B1
                if g.real:
                    dve.wait_ge(rows_summed, g.upto())
                    if g.past(1): dve.wait_ge(deg_scale_ready, g.upto(1))
                    dve.tensor_scalar(degree[:, :], row_sum[:, :], DEG_EPS, None, ALU.add).then_inc(degree_ready, 1)
                g = t.N
                if g.real:
                    dve.wait_ge(x_loaded[g % 4], g.transfers(4))
                    statistics(norm0, x_in[g % 4], g)
                g = t.B2
                if g.real:
                    dve.wait_ge(norm2.scale_steps, g.steps(2))
                    if g.past(1): dve.wait_ge(h2_ready, g.upto(1))
                    dve.scalar_tensor_tensor(out=norm2_bias[:, :], in0=norm2.moments[:, :, 0], scalar=-1.0, in1=norm2.scale[:, :],
                                             op0=ALU.mult, op1=ALU.mult).then_inc(norm2.normed, 1)
                g = t.B1
                if g.real:
                    dve.wait_ge(gru_turned, g.upto())
                    if g.past(1): dve.wait_ge(elu_pos_ready, g.upto(1))
                    dve.tensor_tensor(x1[:, :, :], bank[5][:, :, :], x_in[g % 4][:, :, :], ALU.add).then_inc(x1_ready, 1)
                    dve.wait_ge(x1_ready, g.upto())
                    statistics(norm1, x1, g)
                g = t.A1
                if g.real:
                    dve.wait_ge(h0_ready, g.upto())
                    if g.past(2): dve.wait_ge(z_done, g.upto(2))
                    dve.tensor_tensor(h0_lo[g % 2][:, :, :], h0[g % 2][:, :, :], h0_hi[g % 2][:, :, :].bitcast(F32),
                                      ALU.subtract).then_inc(h0_lo_ready, 1)
                g = t.C
                if g.real:
                    dve.wait_ge(agg_hi_ready, g.upto())
                    if g.past(1): dve.wait_ge(hidden_done[CHUNKS - 1], g.upto(1))
                    dve.tensor_tensor(agg_lo[:, :, :], bank[1][:, :, :], agg_hi[:, :, :].bitcast(F32),
                                      ALU.subtract).then_inc(agg_lo_ready, 1)
                g = t.B2
                if g.real:
                    dve.wait_ge(h2_ready, g.upto())
                    statistics(norm2b, h2, g)
                g = t.B1
                if g.real:
                    if g.past(1): dve.wait_ge(h1_turned, g.upto(1))
                    normalise(norm1, h1n, x1, g)
                g = t.N
                if g.real:
                    if g.past(1): dve.wait_ge(h0_turned, g.upto(1))
                    normalise(norm0, h0n, x_in[g % 4], g)
                g = t.B2
                if g.real:
                    if g.past(1): dve.wait_ge(h2_turned, g.upto(1))
                    normalise(norm2b, h2nn, h2, g)
                g = t.A1
                if g.real:
                    dve.wait_ge(c1_ready, g.upto())
                    if g.past(1): dve.wait_ge(even_conv_done, g.upto(1))
                    dve.tensor_copy(c1_hi[:, :, BEFORE:BEFORE + HALF], c1[:, :, :]).then_inc(c1_hi_ready, 1)
                g = t.A2
                if g.real:
                    dve.wait_ge(nmp_hi_ready, g.upto())
                    if g.past(1): dve.wait_ge(z_done, g.upto(1))
                    dve.tensor_tensor(nmp_lo[:, :, :], bank[0][:, :, :], nmp_hi[:, :, :].bitcast(F32),
                                      ALU.subtract).then_inc(nmp_lo_ready, 1)
                g = t.B1
                if g.real:
                    dve.wait_ge(h1_ready, g.upto())
                    dve.tensor_tensor(h1_lo[:, :, :], h1[:, :, :], h1_hi[:, :, :].bitcast(F32),
                                      ALU.subtract).then_inc(h1_lo_ready, 1)
                g = t.A1
                if g.real:
                    dve.wait_ge(c1_hi_ready, g.upto())
                    dve.tensor_tensor(c1_lo[:, :, BEFORE:BEFORE + HALF], c1[:, :, :],
                                      c1_hi[:, :, BEFORE:BEFORE + HALF].bitcast(F32), ALU.subtract).then_inc(c1_lo_ready, 1)
                    dve.wait_ge(message_done, g.upto())
                    if g.past(2): dve.wait_ge(nmp_done, g.upto(2))
                    dve.tensor_tensor(message[g % 2][:, :, :], bank[3][:, :, :], row("msg"), ALU.add).then_inc(message_summed, 1)
                g = t.A2
                if g.real:
                    dve.wait_ge(odd_conv_added, g.upto())
                    dve.wait_ge(conv2_done, g.upto())
                    dve.scalar_tensor_tensor(out=conv_sum_parts, in0=conv_bank, scalar=bn_scale[:, 1:2],
                                             in1=conv_sum_parts, op0=ALU.mult, op1=ALU.add).then_inc(conv_sum_steps, 1)
                g = t.B1
                if g.real:
                    dve.wait_ge(hom_het_done, g.upto())
                    dve.wait_ge(deg_scale_ready, g.upto())
                    if g.past(1): dve.wait_ge(hom_done, g.upto(1))
                    scale = deg_scale[:, :].unsqueeze(2).to_broadcast([P, PER, P])
                    dve.tensor_tensor(f_hom[:, 0:2, :], bank[0][:, 0:PER:2, :], scale[:, 0:2, :], ALU.mult)
                    dve.tensor_tensor(f_hom[:, 2:4, :], bank[6][:, 0:PER:2, :], scale[:, 2:4, :], ALU.mult).then_inc(f_hom_ready, 1)
                g = t.C
                if g.real:
                    dve.wait_ge(rms_done, g.upto())
                    if g.past(1): dve.wait_ge(rms_scale_ready, g.upto(1))
                    dve.tensor_scalar(mean_square[:, :], bank[1][:, 0, 0:PER], 1.0 / HID, RMS_EPS,
                                      ALU.mult, ALU.add).then_inc(mean_square_ready, 1)
                g = t.A2
                if g.real:
                    dve.wait_ge(conv_sum_steps, g.steps(1))
                    dve.scalar_tensor_tensor(out=conv_sum_parts[:, 1], in0=conv_bank[:, 0], scalar=minus_scale2[:, :],
                                             in1=conv_sum_parts[:, 1], op0=ALU.mult, op1=ALU.add).then_inc(conv_sum_steps, 1)
                g = t.B2
                if g.real:
                    dve.wait_ge(h2_col_ready, g.upto())
                    dve.tensor_tensor(h2_col_lo[:, :, :], h2_col[:, :, :], h2_col_hi[:, :, :].bitcast(F32),
                                      ALU.subtract).then_inc(h2_col_lo_ready, 1)
                g = t.A1
                if g.real:
                    dve.wait_ge(se_done, g.upto())
                    if g.past(1): dve.wait_ge(dist_done, g.upto(1))
                    dve.tensor_scalar(left[0:32, :, :], bank[7][0:32, :, :], column("se", 32), 2.0,
                                      ALU.add, ALU.mult).then_inc(left_ready, 1)
                g = t.B1
                if g.real:
                    dve.wait_ge(gate_done, g.upto())
                    if g.past(1): dve.wait_ge(gated_ready, g.upto(1))
                    dve.tensor_tensor(gate_tanh[:, :, :], bank[3][:, :, :], row("b_t"), ALU.add).then_inc(gate1_summed, 1)
                g = t.C
                if g.real:
                    dve.wait_ge(rms_scale_ready, g.upto())
                    if g.past(1): dve.wait_ge(rms_diag_ready, g.upto(1))
                    dve.tensor_copy(rms_scale_hi[:, :], rms_scale[:, :]).then_inc(rms_scale_hi_ready, 1)
                g = t.B1
                if g.real:
                    dve.wait_ge(hom_done, g.upto())
                    if g.past(1): dve.wait_ge(gated_ready, g.upto(1))
                    dve.tensor_tensor(hom[:, :, :], bank[1][:, :, :], scale, ALU.mult).then_inc(hom_ready, 1)
                g = t.C
                if g.real:
                    dve.wait_ge(rms_scale_hi_ready, g.upto())
                    if g.past(1): dve.wait_ge(rms_diag_lo_ready, g.upto(1))
                    dve.tensor_tensor(rms_scale_lo[:, :], rms_scale[:, :], rms_scale_hi[:, :].bitcast(F32), ALU.subtract).then_inc(rms_scale_lo_ready, 1)
                g = t.B1
                if g.real:
                    dve.wait_ge(hom_ready, g.upto())
                    dve.wait_ge(f_het_ready, g.upto())
                    dve.tensor_tensor(hom[:, :, :], hom[:, :, :], f_het[:, :, :], ALU.subtract).then_inc(difference_ready, 1)
                g = t.C
                if g.real:
                    if g.past(1): dve.wait_ge(rms_wide_done, g.upto(1))
                    dve.tensor_tensor(rms_diag_hi[:, :, :], identity[:, :].unsqueeze(1).to_broadcast([P, PER, P]),
                                      rms_scale_hi[:, :].bitcast(F32).unsqueeze(2).to_broadcast([P, PER, P]), ALU.mult).then_inc(rms_diag_ready, 1)
                g = t.B1
                if g.real:
                    dve.wait_ge(gate1_ready, g.upto())
                    dve.wait_ge(difference_ready, g.upto())
                    dve.scalar_tensor_tensor(out=mix[:, :, :], in0=gate_tanh[:, :, :], scalar=1.0,
                                             in1=hom[:, :, :], op0=ALU.add, op1=ALU.mult).then_inc(gated_ready, 1)
                g = t.A2
                if g.real:
                    dve.wait_ge(x_conv_ready, g.upto())
                    if g.past(1): dve.wait_ge(z_done, g.upto(1))
                    dve.tensor_tensor(x_conv_lo[:, :, :], conv_sum[:, :, :], x_conv_hi[:, :, :].bitcast(F32),
                                      ALU.subtract).then_inc(x_conv_lo_ready, 1)
                g = t.B1
                if g.real:
                    dve.wait_ge(gated_ready, g.upto())
                    dve.scalar_tensor_tensor(out=mix[:, :, :], in0=mix[:, :, :], scalar=0.5,
                                             in1=f_het[:, :, :], op0=ALU.mult, op1=ALU.add).then_inc(mix_ready, 1)
                g = t.C
                if g.real:
                    for c in range(3):
                        dve.wait_ge(rms_wide_ready, g.upto())
                        dve.wait_ge(hidden_ready[c], g.upto())
                        dve.tensor_tensor(hidden[c][:, :, :], hidden[c][:, :, :], rms_wide[:, :, :], ALU.mult).then_inc(scaled_ready[c], 1)
                g = t.B1
                if g.real:
                    dve.wait_ge(mix_ready, g.upto())
                    if g.past(1): dve.wait_ge(x2_ready, g.upto(1))
                    dve.tensor_scalar(elu_neg[:, :, :], mix[:, :, :], 0.0, None, ALU.min).then_inc(elu_neg_ready, 1)
                g = t.C
                if g.real:
                    for c in range(2):
                        dve.wait_ge(silu_tanh_ready[c], g.upto())
                        dve.scalar_tensor_tensor(out=silu[c][:, :, :], in0=silu[c][:, :, :], scalar=1.0,
                                                 in1=hidden[c][:, :, :], op0=ALU.add, op1=ALU.mult).then_inc(silu_ready[c], 1)
                    dve.wait_ge(rms_wide_ready, g.upto())
                    dve.wait_ge(hidden_ready[3], g.upto())
                    dve.tensor_tensor(hidden[3][:, :, :], hidden[3][:, :, :], rms_wide[:, :, :], ALU.mult).then_inc(scaled_ready[3], 1)
                    dve.wait_ge(silu_tanh_ready[2], g.upto())
                    dve.scalar_tensor_tensor(out=silu[2][:, :, :], in0=silu[2][:, :, :], scalar=1.0,
                                             in1=hidden[2][:, :, :], op0=ALU.add, op1=ALU.mult).then_inc(silu_ready[2], 1)
                g = t.B1
                if g.real:
                    dve.wait_ge(mix_ready, g.upto())
                    dve.scalar_tensor_tensor(out=elu_pos[:, :, :], in0=mix[:, :, :], scalar=0.0,
                                             in1=x1[:, :, :], op0=ALU.max, op1=ALU.add).then_inc(elu_pos_ready, 1)
                g = t.B2
                if g.real:
                    dve.wait_ge(conv_rel_done, g.upto())
                    if g.past(1): dve.wait_ge(x3_b2_ready, g.upto(1))
                    if g.past(1): dve.wait_ge(h3_ready, g.upto(1))
                    dve.tensor_tensor(x3[:, 0:2, :], bank[1][:, 1:PER:2, :], row("rel")[:, 0:2, :], ALU.add)
                    dve.tensor_tensor(x3[:, 2:4, :], bank[6][:, 1:PER:2, :], row("rel")[:, 2:4, :], ALU.add).then_inc(conv_rel_ready, 1)
                g = t.C
                if g.real:
                    dve.wait_ge(silu_tanh_ready[3], g.upto())
                    dve.scalar_tensor_tensor(out=silu[3][:, :, :], in0=silu[3][:, :, :], scalar=1.0,
                                             in1=hidden[3][:, :, :], op0=ALU.add, op1=ALU.mult).then_inc(silu_ready[3], 1)
                g = t.A2
                if g.real:
                    dve.wait_ge(gate_r_ready, g.upto())
                    dve.scalar_tensor_tensor(out=candidate[:, :, :], in0=bank[3][:, :, :], scalar=column("hh_n"),
                                             in1=candidate[:, :, :], op0=ALU.add, op1=ALU.mult).then_inc(r_hidden_ready, 1)
                g = t.B2
                if g.real:
                    dve.wait_ge(conv_rel_ready, g.upto())
                    dve.wait_ge(x2_h2_ready, g.upto())
                    dve.scalar_tensor_tensor(out=x3[:, :, :], in0=x3[:, :, :], scalar=0.0,
                                             in1=x2_h2[:, :, :], op0=ALU.max, op1=ALU.add).then_inc(x3_ready, 1)
                g = t.A2
                if g.real:
                    dve.wait_ge(r_hidden_ready, g.upto())
                    dve.wait_ge(input_n_done, g.upto())
                    dve.tensor_tensor(candidate[:, :, :], candidate[:, :, :], bank[0][:, :, :], ALU.add).then_inc(n_summed, 1)
                g = t.B1
                if g.real:
                    dve.wait_ge(elu_exp_ready, g.upto())
                    dve.wait_ge(elu_pos_ready, g.upto())
                    if g.past(1): dve.wait_ge(x2_h2_ready, g.upto(1))
                    dve.scalar_tensor_tensor(out=x2[:, :, :], in0=elu_neg[:, :, :], scalar=-1.0,
                                             in1=elu_pos[:, :, :], op0=ALU.add, op1=ALU.add).then_inc(x2_ready, 1)
                g = t.B2
                if g.real:
                    dve.wait_ge(x3_ready, g.upto())
                    statistics(norm3, x3, g)
                g = t.B1
                if g.real:
                    dve.wait_ge(x2_ready, g.upto())
                    statistics(norm2, x2, g)
                g = t.A2
                if g.real:
                    dve.wait_ge(h_less_n_ready, g.upto())
                    dve.wait_ge(gate_z_ready, g.upto())
                    if g.past(1): dve.wait_ge(gru_turned, g.upto(1))
                    dve.tensor_tensor(gru[:, :, :], gate_z[:, :, :], h_less_n[:, :, :], ALU.mult).then_inc(z_part_ready, 1)
                g = t.C
                if g.real:
                    dve.wait_ge(out_done, g.upto())
                    dve.wait_ge(x3_b2_ready, g.upto())
                    if g.past(1): dve.wait_ge(stored, g.transfers(1, 1))
                    dve.tensor_tensor(result[:, :, :], bank[5][:, :, :], x3_b2[:, :, :], ALU.add).then_inc(result_ready, 1)
                g = t.A2
                if g.real:
                    dve.wait_ge(z_part_ready, g.upto())
                    dve.tensor_tensor(gru[:, :, :], gru[:, :, :], candidate[:, :, :], ALU.add).then_inc(gru_ready, 1)

            turns(dve, turn)

        @block.gpsimd
        def _(pool):
            pool.memset(identity[:, :], 0.0).then_inc(pool_setup, 1)
            pool.memset(ones[:, :], 1.0)
            pool.memset(minus_half[:, :], -0.5).then_inc(pool_setup, 1)
            pool.wait_ge(pool_setup, 1)
            pool.affine_select(out=identity[:, :], in_=identity[:, :], compare_op=ALU.not_equal, fill=1.0, base=0,
                               pattern=[[-1, P]], channel_multiplier=1).then_inc(pool_setup, 1)
            pool.wait_ge(pool_setup, 2)
            pool.wait_ge(dve_setup, 1)
            pool.tensor_tensor(bn_root[:, :], bn_var[:, :], minus_half[:, 0:2], ALU.pow).then_inc(pool_setup, 1)
            pool.wait_ge(dve_setup, PREPARED)

            def inverse_deviation(norm, g, used):
                pool.wait_ge(norm.moments_ready, g.upto())
                if g.past(1): pool.wait_ge(used, g.upto(1))
                pool.sem_inc(pool_held, 1)
                pool.tensor_scalar(norm.scale[:, :], norm.moments[:, :, 1], LN_EPS, None, ALU.add).then_inc(norm.scale_steps, 1)
                pool.wait_ge(norm.scale_steps, g.steps(1))
                pool.tensor_tensor(norm.scale[:, :], norm.scale[:, :], minus_half[:, :], ALU.pow).then_inc(norm.scale_steps, 1)

            def split_conv2():
                taps = weights_raw[:, CONV2][:, P:].rearrange("p (k s o) -> p s k o", s=2, o=P)
                halves = [slice(n * PER, (n + 1) * PER) for n in range(2)]
                pool.wait_ge(conv2_loaded, 16)
                for n, half in enumerate(halves):
                    pool.tensor_tensor(pairs[n][:, :, :], taps[:, 0, half, :], taps[:, 1, half, :], ALU.add).then_inc(pool_setup, 1)
                pool.wait_ge(act_setup, 1)
                pool.tensor_tensor(weights_lo[:, CONV2], weights_raw[:, CONV2], weights_hi[:, CONV2].bitcast(F32),
                                   ALU.subtract).then_inc(pool_setup, 1)
                pool.wait_ge(act_setup, 3)
                for n, half in enumerate(halves):
                    pool.tensor_tensor(pairs_lo[:, half, :], pairs[n][:, :, :], pairs_hi[:, half, :].bitcast(F32),
                                       ALU.subtract).then_inc(pool_setup, 1)

            def turn(t):
                if t.A1.first: split_conv2()
                g = t.A2
                if g.real:
                    pool.wait_ge(odd_conv_ready, g.upto())
                    pool.wait_ge(h0_ready, g.upto())
                    if g.past(1): pool.wait_ge(x_conv_lo_ready, g.upto(1))
                    pool.tensor_tensor(conv_sum[:, :, 0:P:2], odd_conv[:, :, 1:HALF + 1], h0[g % 2][:, :, 0:P:2], ALU.add)
                    pool.wait_ge(adj_loaded[g % 4], g.transfers(4))
                    pool.wait_ge(affinity_ready, g.upto())
                    pool.tensor_tensor(masked[:, :, :], masked[:, :, :], adj[g % 4][:, :, :], ALU.mult).then_inc(masked_ready, 1)
                g = t.B1
                if g.real:
                    pool.wait_ge(degree_ready, g.upto())
                    if g.past(1): pool.wait_ge(hom_ready, g.upto(1))
                    pool.tensor_tensor(deg_scale[:, :], degree[:, :], minus_half[:, :], ALU.pow).then_inc(deg_scale_ready, 1)
                g = t.N
                if g.real:
                    inverse_deviation(norm0, g, norm0.normed)
                g = t.B1
                if g.real:
                    inverse_deviation(norm1, g, norm1.normed)
                g = t.A2
                if g.real:
                    pool.tensor_tensor(conv_sum[:, :, 1:P:2], h0[g % 2][:, :, 1:P:2], odd_conv[:, :, 2:HALF + 2],
                                       ALU.subtract).then_inc(odd_conv_added, 1)
                g = t.B2
                if g.real:
                    inverse_deviation(norm2b, g, norm2b.normed)
                g = t.C
                if g.real:
                    pool.wait_ge(square_ready[0], g.upto())
                    pool.wait_ge(square_ready[1], g.upto())
                    pool.tensor_tensor(square[0][:, :, :], square[0][:, :, :], square[1][:, :, :],
                                       ALU.add).then_inc(square_summed[0], 1)
                g = t.A1
                if g.real:
                    pool.wait_ge(c1_ready, g.upto())
                    if g.past(1): pool.wait_ge(pair_lo_ready, g.upto(1))
                    pool.tensor_tensor(pair[:, :, :], c1[:, 0:PER, :], c1[:, PER:2 * PER, :], ALU.add).then_inc(pair_ready, 1)
                g = t.C
                if g.real:
                    pool.wait_ge(square_ready[2], g.upto())
                    pool.wait_ge(square_ready[3], g.upto())
                    pool.tensor_tensor(square[2][:, :, :], square[2][:, :, :], square[3][:, :, :],
                                       ALU.add).then_inc(square_summed[1], 1)
                    pool.wait_ge(square_summed[0], g.upto())
                    pool.wait_ge(square_summed[1], g.upto())
                    pool.tensor_tensor(square[0][:, :, :], square[0][:, :, :], square[2][:, :, :],
                                       ALU.add).then_inc(square_summed[2], 1)
                    pool.wait_ge(mean_square_ready, g.upto())
                    if g.past(1): pool.wait_ge(rms_scale_lo_ready, g.upto(1))
                    pool.tensor_tensor(rms_scale[:, :], mean_square[:, :], minus_half[:, :], ALU.pow).then_inc(rms_scale_ready, 1)
                    pool.wait_ge(rms_scale_lo_ready, g.upto())
                    if g.past(1): pool.wait_ge(rms_wide_done, g.upto(1))
                    pool.tensor_tensor(rms_diag_lo[:, :, :], identity[:, :].unsqueeze(1).to_broadcast([P, PER, P]),
                                       rms_scale_lo[:, :].unsqueeze(2).to_broadcast([P, PER, P]), ALU.mult).then_inc(rms_diag_lo_ready, 1)
                g = t.B2
                if g.real:
                    pool.wait_ge(h2_ready, g.upto())
                    if g.past(1): pool.wait_ge(x3_ready, g.upto(1))
                    pool.tensor_tensor(x2_h2[:, :, :], x2[:, :, :], h2[:, :, :], ALU.add).then_inc(x2_h2_ready, 1)
                    pool.wait_ge(adj_loaded[g % 4], g.transfers(4))
                    if g.past(1): pool.wait_ge(agg_done, g.upto(1))
                    pool.tensor_tensor(adj_eps[:, :, :], adj[g % 4][:, :, :],
                                       eps_identity[:, :].unsqueeze(1).to_broadcast([P, PER, P]), ALU.add).then_inc(adj_eps_ready, 1)
                g = t.C
                if g.real:
                    if g.past(1): pool.wait_ge(result_ready, g.upto(1))
                    pool.tensor_tensor(x3_b2[:, :, :], x3[:, :, :], row("out"), ALU.add).then_inc(x3_b2_ready, 1)
                g = t.A1
                if g.real:
                    pool.wait_ge(pair_hi_ready, g.upto())
                    if g.past(1): pool.wait_ge(conv2_done, g.upto(1))
                    pool.tensor_tensor(pair_lo[:, :, REACH:REACH + HALF], pair[:, :, :],
                                       pair_hi[:, :, REACH:REACH + HALF].bitcast(F32), ALU.subtract).then_inc(pair_lo_ready, 1)
                g = t.A2
                if g.real:
                    pool.wait_ge(tanh_r_ready, g.upto())
                    pool.sem_inc(pool_held, 1)
                    pool.tensor_scalar(candidate[:, :, :], candidate[:, :, :], 0.5, 0.5, ALU.mult, ALU.add).then_inc(gate_r_ready, 1)
                    pool.wait_ge(tanh_z_ready, g.upto())
                    pool.sem_inc(pool_held, 1)
                    pool.tensor_scalar(gate_z[:, :, :], gate_z[:, :, :], 0.5, 0.5, ALU.mult, ALU.add).then_inc(gate_z_ready, 1)
                    pool.wait_ge(n_ready, g.upto())
                    pool.tensor_tensor(h_less_n[:, :, :], h0[g % 2][:, :, :], candidate[:, :, :], ALU.subtract).then_inc(h_less_n_ready, 1)
                g = t.B2
                if g.real:
                    inverse_deviation(norm3, g, h3_ready)
                g = t.B1
                if g.real:
                    inverse_deviation(norm2, g, h2_ready)

            turns(pool, turn)


def kernel(**inputs):
    import numpy as np
    import concourse.bacc as bacc
    from concourse.bass_utils import run_bass_kernel_spmd

    a = {name: np.asarray(value) for name, value in inputs.items()}
    L0 = {name[7:]: value for name, value in a.items() if name.startswith("L0_gnn_")}

    x = a["x"].reshape(GROUPS, PER, P, P).transpose(2, 0, 1, 3)
    adj = a["adj"].reshape(GROUPS, PER, P, P).transpose(3, 0, 1, 2)
    adj_rows = a["adj"].reshape(GROUPS, PER, P, P).transpose(2, 0, 1, 3)
    se = np.zeros((P, 96), np.float32)
    b_se = np.zeros(P, np.float32)
    for n in range(3):
        se[:, 32 * n:32 * n + 3] = L0["w_se"].T
        b_se[32 * n:32 * n + 3] = L0["b_se"]
    w_ih = L0["w_ih"].T.reshape(2, P, 3 * P).transpose(1, 0, 2).reshape(P, -1)
    W2 = a["L3_gnn_W2"].reshape(CHUNKS, P, P).transpose(1, 0, 2).reshape(P, -1)
    weights = np.concatenate([L0["w_msg"].T, a["L1_gnn_theta"], a["L1_gnn_W_h"], a["L1_gnn_W_t"], a["L2_gnn_W_rel"],
                              a["L2_gnn_W_root"], W2], 1)
    split = np.concatenate([L0["conv1_w"][:, :, 0].T, se, w_ih, L0["w_hh"].T, a["L3_gnn_W1"],
                            L0["conv2_w"].transpose(1, 2, 0).reshape(P, -1)], 1)
    columns = np.stack([
        L0["bn1_g"], L0["bn2_g"], L0["bn1_b"], L0["bn2_b"], L0["bn1_m"], L0["bn2_m"], L0["bn1_v"], L0["bn2_v"],
        *L0["b_ih"].reshape(3, P), *L0["b_hh"].reshape(3, P), b_se, a["L2_gnn_ln_gamma"], a["L2_gnn_ln_beta"],
        np.broadcast_to(a["L3_gnn_epsilon"], (P,)), *a["L3_gnn_b1"].reshape(CHUNKS, P),
        *a["L3_gnn_rms_weight"].reshape(CHUNKS, P)], 1)
    rows = np.stack([L0["b_msg"], a["L1_gnn_b_t"], a["L2_gnn_b_rel"], a["L3_gnn_b2"]])

    nc = bacc.Bacc("TRN2", target_bir_lowering=False, num_devices=1)
    arrays, args = {}, []
    for name, value in (("x", x), ("adj", adj), ("adj_rows", adj_rows), ("weights", weights), ("split", split), ("columns", columns), ("rows", rows)):
        value = np.ascontiguousarray(value)
        arrays[f"in_{name}_dram"] = value
        args.append(nc.dram_tensor(f"in_{name}_dram", value.shape, mybir.dt.from_np(value.dtype), kind="ExternalInput").ap())
    args.append(nc.dram_tensor("out_dram", (P, GROUPS, PER, P), F32, kind="ExternalOutput").ap())
    graph_layers(nc, *args)
    r = run_bass_kernel_spmd(nc, [arrays], core_ids=[0])
    out = r.results[0]["out_dram"]
    return out.transpose(1, 2, 0, 3).reshape(GRAPHS, P, P)
```
